# Optimizing a Trainium2 kernel written in Bass

```python
import numpy as np
import jax
import jax.numpy as jnp

def _softmax(x, axis=-1):
    return jax.nn.softmax(x, axis=axis)

def _gelu(x):
    return jax.nn.gelu(x, approximate=True)

def _silu(x):
    return jax.nn.silu(x)

def _sigmoid(x):
    return jax.nn.sigmoid(x)

def _layernorm(x, axis=-1, eps=1e-05):
    m = jnp.mean(x, axis=axis, keepdims=True)
    v = jnp.var(x, axis=axis, keepdims=True)
    return (x - m) / jnp.sqrt(v + eps)

def _scatter_add(tgt, idx, src, axis=0):
    return tgt.at[idx].add(src)

def _segment_sum(src, seg, n):
    return jax.ops.segment_sum(src, seg, n)
kernel_name = 'mk_seq_preln_d1_jaxref_r8_267e6a'

def setup_inputs(seed: int=0):
    np.random.seed(seed)
    _w = jnp.asarray

    def _L0_attn_setup():
        import jax, jax.numpy as jnp
        import numpy as np

        def _parallel_scan_affine(log_a, b):
            T = log_a.shape[1]
            la, bv = (log_a, b)
            stride = 1
            while stride < T:
                la_prev = jnp.roll(la, stride, axis=1).at[:, :stride, :].set(0.0)
                bv_prev = jnp.roll(bv, stride, axis=1).at[:, :stride, :].set(0.0)
                bv = jnp.exp(la) * bv_prev + bv
                la = la + la_prev
                stride *= 2
            return bv
        key = jax.random.key(seed)
        kx, kwz, kwh = jax.random.split(key, 3)
        B, T, D = (4, 512, 128)
        x = jax.random.normal(kx, (B, T, D), dtype=jnp.float32)
        Wz = jax.random.normal(kwz, (D, D), dtype=jnp.float32) * 0.02
        bz = jnp.zeros((D,), dtype=jnp.float32)
        Wh = jax.random.normal(kwh, (D, D), dtype=jnp.float32) * 0.02
        bh = jnp.zeros((D,), dtype=jnp.float32)
        return {'x': x, 'Wz': Wz, 'bz': bz, 'Wh': Wh, 'bh': bh}
    _L0_attn_in = _L0_attn_setup()

    def _L0_ffn_setup():
        import jax, jax.numpy as jnp
        import numpy as np
        from jax.scipy.linalg import expm
        B, S, D, E, K, NROT = (2, 256, 128, 8, 2, 3)
        DF = 4 * D
        EPS = 1e-05
        key = jax.random.key(seed)
        ks = jax.random.split(key, 8)
        s = lambda d: 1.0 / np.sqrt(d)
        return {'x': jax.random.normal(ks[0], (B, S, D), jnp.float32), 'ln_g': jnp.ones((D,), jnp.float32), 'ln_b': jnp.zeros((D,), jnp.float32), 'abel_w': jax.random.normal(ks[1], (D, D), jnp.float32) * s(D), 'abel_b': jnp.zeros((D,), jnp.float32), 'gate_w_moe': jax.random.normal(ks[2], (D, E), jnp.float32) * s(D), 'gate_b_moe': jnp.zeros((E,), jnp.float32), 'w1': jax.random.normal(ks[3], (E, D, DF), jnp.float32) * s(D), 'b1': jnp.zeros((E, DF), jnp.float32), 'w2': jax.random.normal(ks[4], (E, DF, D), jnp.float32) * s(DF), 'b2': jnp.zeros((E, D), jnp.float32), 'gens': jax.random.normal(ks[5], (NROT, D, D), jnp.float32) * 0.02, 'mix_w': jax.random.normal(ks[6], (2 * D, 1), jnp.float32) * s(2 * D), 'mix_b': jnp.zeros((1,), jnp.float32)}
    _L0_ffn_in = _L0_ffn_setup()
    _d = {'L0_attn_x': _L0_attn_in['x'], 'L0_attn_Wz': _L0_attn_in['Wz'], 'L0_attn_bz': _L0_attn_in['bz'], 'L0_attn_Wh': _L0_attn_in['Wh'], 'L0_attn_bh': _L0_attn_in['bh'], 'L0_ffn_ln_g': _L0_ffn_in['ln_g'], 'L0_ffn_ln_b': _L0_ffn_in['ln_b'], 'L0_ffn_abel_w': _L0_ffn_in['abel_w'], 'L0_ffn_abel_b': _L0_ffn_in['abel_b'], 'L0_ffn_gate_w_moe': _L0_ffn_in['gate_w_moe'], 'L0_ffn_gate_b_moe': _L0_ffn_in['gate_b_moe'], 'L0_ffn_w1': _L0_ffn_in['w1'], 'L0_ffn_b1': _L0_ffn_in['b1'], 'L0_ffn_w2': _L0_ffn_in['w2'], 'L0_ffn_b2': _L0_ffn_in['b2'], 'L0_ffn_gens': _L0_ffn_in['gens'], 'L0_ffn_mix_w': _L0_ffn_in['mix_w'], 'L0_ffn_mix_b': _L0_ffn_in['mix_b']}
    _x0 = _d['L0_attn_x']
    _d['L0_attn_x'] = jax.random.normal(jax.random.fold_in(jax.random.key(seed), 1), (32, 256, 128), dtype=_x0.dtype)
    del _x0
    return _d

def reference(L0_attn_x, L0_attn_Wz, L0_attn_bz, L0_attn_Wh, L0_attn_bh, L0_ffn_ln_g, L0_ffn_ln_b, L0_ffn_abel_w, L0_ffn_abel_b, L0_ffn_gate_w_moe, L0_ffn_gate_b_moe, L0_ffn_w1, L0_ffn_b1, L0_ffn_w2, L0_ffn_b2, L0_ffn_gens, L0_ffn_mix_w, L0_ffn_mix_b):

    def _L0_attn_ref(x, Wz, bz, Wh, bh):
        import jax, jax.numpy as jnp
        import numpy as np

        def _parallel_scan_affine(log_a, b):
            T = log_a.shape[1]
            la, bv = (log_a, b)
            stride = 1
            while stride < T:
                la_prev = jnp.roll(la, stride, axis=1).at[:, :stride, :].set(0.0)
                bv_prev = jnp.roll(bv, stride, axis=1).at[:, :stride, :].set(0.0)
                bv = jnp.exp(la) * bv_prev + bv
                la = la + la_prev
                stride *= 2
            return bv
        z = jax.nn.sigmoid(jnp.einsum('btd,ed->bte', x, Wz) + bz)
        h_tilde = jnp.einsum('btd,ed->bte', x, Wh) + bh
        log_a = jnp.log(1.0 - z + 1e-08)
        b = z * h_tilde
        h_out = _parallel_scan_affine(log_a, b)
        return h_out

    def _L0_ffn_ref(x, ln_g, ln_b, abel_w, abel_b, gate_w_moe, gate_b_moe, w1, b1, w2, b2, gens, mix_w, mix_b):
        import jax, jax.numpy as jnp
        import numpy as np
        from jax.scipy.linalg import expm
        B, S, D, E, K, NROT = (2, 256, 128, 8, 2, 3)
        DF = 4 * D
        EPS = 1e-05
        residual = x
        mu = jnp.mean(x, axis=-1, keepdims=True)
        var = jnp.mean((x - mu) ** 2, axis=-1, keepdims=True)
        xn = (x - mu) * jax.lax.rsqrt(var + EPS) * ln_g + ln_b
        abel = jax.nn.gelu(xn @ abel_w + abel_b, approximate=False)
        logits = xn @ gate_w_moe + gate_b_moe
        tw, ti = jax.lax.top_k(logits, K)
        tw = jax.nn.softmax(tw, axis=-1)
        onehot = (ti[..., None] == jnp.arange(E)).astype(tw.dtype)
        wdense = jnp.sum(tw[..., None] * onehot, axis=2)
        h = jax.nn.gelu(jnp.einsum('bsd,edf->besf', xn, w1) + b1[None, :, None, :], approximate=False)
        eo = jnp.einsum('besf,efd->besd', h, w2) + b2[None, :, None, :]
        moe = jnp.einsum('besd,bse->bsd', eo, wdense)
        rot = expm(gens[0])
        for i in range(1, NROT):
            rot = rot @ expm(gens[i])
        nonabel = moe @ rot
        combined = jnp.concatenate([abel, nonabel], axis=-1)
        g = jax.nn.sigmoid(combined @ mix_w + mix_b)
        return residual + abel * (1.0 - g) + nonabel * g
    x = L0_attn_x
    x = x + _L0_attn_ref(_layernorm(x, axis=-1), L0_attn_Wz, L0_attn_bz, L0_attn_Wh, L0_attn_bh)
    x = x + _L0_ffn_ref(_layernorm(x, axis=-1), L0_ffn_ln_g, L0_ffn_ln_b, L0_ffn_abel_w, L0_ffn_abel_b, L0_ffn_gate_w_moe, L0_ffn_gate_b_moe, L0_ffn_w1, L0_ffn_b1, L0_ffn_w2, L0_ffn_b2, L0_ffn_gens, L0_ffn_mix_w, L0_ffn_mix_b)
    return x

_drawn_inputs = setup_inputs


def setup_inputs(seed=0):
    import zlib

    import numpy as np

    out = dict(_drawn_inputs(seed))
    spreads = {'L0_attn_bz': (0.0, 0.656),
     'L0_attn_bh': (0.0, 0.1),
     'L0_ffn_ln_g': (1.0, 0.2),
     'L0_ffn_ln_b': (0.0, 0.1),
     'L0_ffn_abel_b': (0.0, 0.532),
     'L0_ffn_gate_b_moe': (0.0, 0.1),
     'L0_ffn_b1': (0.0, 0.499),
     'L0_ffn_b2': (0.0, 0.368)}
    factors = {'L0_attn_Wz': 2.692}
    for name, (base, spread) in spreads.items():
        noise = np.random.default_rng([zlib.crc32(name.encode()), seed]).standard_normal(out[name].shape)
        drawn = base * np.exp(spread * noise) if base else spread * noise
        out[name] = jnp.asarray(drawn.astype(out[name].dtype))
    for name, factor in factors.items():
        out[name] = (out[name] * factor).astype(out[name].dtype)
    return out
```

```python
from contextlib import ExitStack

import concourse.bass as bass
from concourse import mybir

F32 = mybir.dt.float32
F16 = mybir.dt.float16
BF16 = mybir.dt.bfloat16
I32 = mybir.dt.int32
U32 = mybir.dt.uint32
ALU = mybir.AluOpType
ACT = mybir.ActivationFunctionType
AX = mybir.AxisListType

P = 128
EPS = 1e-5
A_GUARD = 1e-8
WSCALE = 256.0
MAGIC = float(0x5F3759DF)
SQUARINGS = 8


def gru_moe_block(nc, x, wz, bz, wh, bh, ln_g, ln_b, abel_w, abel_b, gate_w, gate_b,
                  w1, b1, w2, b2, gens, mix_w, mix_b, out):
    B, T, D = x.shape
    E, _, DF = w1.shape
    NROT = gens.shape[0]
    assert D == P and T % P == 0 and DF % P == 0
    TOK = B * T
    NT = TOK // P
    CT = 4
    NCH = NT // CT
    CW = CT * P
    BPC = CW // T
    FB = DF // P
    NP = E * (E - 1) // 2
    REGION = TOK + P
    SPARE = NP * REGION
    NS = NT + NP
    ROW = P + 5
    W_LO, W_HI, SCALE_R, MEAN_R, TOKEN = P, P + 1, P + 2, P + 3, P + 4
    NX = 4
    RB = 4
    XT = NT // NX
    assert NS <= P and NCH % 2 == 0 and NS % RB == 0
    PAIRS = [(a, b) for a in range(E) for b in range(a + 1, E)]

    x_tiles = x.rearrange("b t d -> (b t) d").rearrange("(n p) d -> p n d", p=P)
    out_rows = out.rearrange("b t d -> (b t) d")
    slots = nc.dram_tensor("slots", [SPARE + P, ROW], F32).ap()

    ctx = ExitStack()
    with ctx:
        def sb(name, shape, dt=F32):
            return ctx.enter_context(nc.sbuf_tensor(name, shape, dt))

        def sem(name):
            return ctx.enter_context(nc.semaphore(name))

        bank = [ctx.enter_context(nc.psum_tensor(f"bank{i}", [P, 512], F32)) for i in range(8)]

        ident = sb("ident", [P, P])
        ident2 = sb("ident2", [P, P])
        tri = sb("tri", [P, P], BF16)
        ones_b = sb("ones_b", [P, P], BF16)
        ones_f = sb("ones_f", [1, P])
        ones_h = sb("ones_h", [2, P], F16)
        pair_no = sb("pair_no", [P, NP])
        pad_base = sb("pad_base", [P, NP])
        lo_tab = sb("lo_tab", [P, NP])
        hi_tab = sb("hi_tab", [P, NP])
        part_no = sb("part_no", [P, 1])
        tok_no = sb("tok_no", [P, NT])
        row_sel = sb("row_sel", [2, 2])
        zero_row = sb("zero_row", [P, ROW])
        x_all = sb("x_all", [P, NT, P])
        wz_n = sb("wz_n", [P, P])
        wh_n = sb("wh_n", [P, P])
        bz_c = sb("bz_c", [P, 1])
        bh_c = sb("bh_c", [P, 1])
        g_c = sb("g_c", [P, 1])
        beta_c = sb("beta_c", [P, 2])
        aw_n = sb("aw_n", [P, P])
        ab_r = sb("ab_r", [1, P])
        gw_n = sb("gw_n", [P, E])
        gb_r = sb("gb_r", [1, E])
        w1_n = sb("w1_n", [P, E, DF])
        b1_n = sb("b1_n", [E * FB, P])
        w2_n = sb("w2_n", [P, E * FB, P])
        b2_n = sb("b2_n", [E, P])
        mix_r = sb("mix_r", [1, 2 * P + 1])
        wzh_t = sb("wzh_t", [P, 2, P])
        nbz = sb("nbz", [P, 1])
        g256 = sb("g256", [P, 1])
        gw = sb("gw", [P, E])
        gb = sb("gb", [1, E])
        aw_hi = sb("aw_hi", [P, P], F16)
        aw_lo = sb("aw_lo", [P, P], F16)
        ab_hl = sb("ab_hl", [2, P], F16)
        ab_s = sb("ab_s", [2, P])
        ab_h = sb("ab_h", [2, P], F16)
        ab_l = sb("ab_l", [2, P])
        w1_hi = sb("w1_hi", [P, E, DF], F16)
        w1_lo = sb("w1_lo", [P, E, DF], F16)
        b1_t = sb("b1_t", [P, E * FB])
        b1_s = sb("b1_s", [P, E * FB])
        w2_t = sb("w2_t", [P, DF])
        w2_hi = sb("w2_hi", [P, E * FB, P], F16)
        w2_lo = sb("w2_lo", [P, E * FB, P], F16)
        b2_t = sb("b2_t", [P, E, 2])
        b2_s = sb("b2_s", [2, E * P])
        b2_h = sb("b2_h", [2, E * P], F16)
        b2_l = sb("b2_l", [2, E * P])
        b2_hl = sb("b2_hl", [2, E * P], F16)
        mix_b_all = sb("mix_b_all", [P, 2 * P + 1])
        mixb_h = sb("mixb_h", [P, 1])
        RG = NROT * P
        a_1 = sb("a_1", [P, RG])
        a_1t = sb("a_1t", [P, RG])
        a_2 = sb("a_2", [P, RG])
        a_2t = sb("a_2t", [P, RG])
        a_3 = sb("a_3", [P, RG])
        a_4t = sb("a_4t", [P, RG])
        q_s = sb("q_s", [P, RG])
        p_s = sb("p_s", [P, RG])
        em = [sb(f"em{i}", [P, RG]) for i in range(2)]
        emt = [sb(f"emt{i}", [P, RG]) for i in range(2)]
        f_s = sb("f_s", [P, 2, P])
        rot = sb("rot", [P, P])
        st0 = sb("st0", [P, NT, 6])
        mv0 = sb("mv0", [P, NT, 2])
        nw0 = sb("nw0", [P, 4, NT])
        xn = [sb(f"xn{i}", [P, CT, P]) for i in range(2)]
        x_t = sb("x_t", [P, CW])
        tneg = sb("tneg", [P, CW])
        hcand = sb("hcand", [P, CW])
        omz = sb("omz", [P, CW])
        acoef = sb("acoef", [P, CW])
        bneg = sb("bneg", [P, CW])
        hseq = [sb(f"hseq{i}", [P, CW]) for i in range(2)]
        x1 = sb("x1", [P, CT, P])
        st1 = sb("st1", [P, CT, 6])
        mv1 = sb("mv1", [P, CT, 2])
        nw1 = sb("nw1", [P, 4, 2 * CT])
        sy = sb("sy", [P, CT])
        rows = [sb(f"rows{i}", [P, CT, ROW]) for i in range(2)]
        y2_t = sb("y2_t", [P, CW])
        lg = sb("lg", [P, CT, E])
        mx = sb("mx", [P, CT, 8])
        mi = sb("mi", [P, CT, 8], U32)
        idx = sb("idx", [P, CT, 2])
        gap = sb("gap", [P, CT])
        elo = sb("elo", [P, CT])
        ehi = sb("ehi", [P, CT])
        sgn = sb("sgn", [P, CT])
        gaps = sb("gaps", [P, CT])
        th = sb("th", [P, CT])
        pr1 = sb("pr1", [P, CT])
        pair = sb("pair", [P, CT])
        hot = sb("hot", [P, CT, NP], BF16)
        hsum = sb("hsum", [P, NP])
        carry = sb("carry", [P, NP], BF16)
        rsel = sb("rsel", [P, CT, NP])
        rank = sb("rank", [P, CT])
        pos = [sb(f"pos{i}", [P, CT], I32) for i in range(2)]
        pad_at = sb("pad_at", [P, NP], I32)
        cnt_i = sb("cnt_i", [P, 2, NP], I32)
        pl = sb("pl", [P, 6, NP])
        pc = sb("pc", [P, 8])
        plan_f = sb("plan_f", [P, 3])
        plan = sb("plan", [3, P], I32)
        srow = [sb(f"srow{i}", [P, ROW]) for i in range(RB)]
        x_hi = [sb(f"x_hi{i}", [P, P], F16) for i in range(2)]
        x_lo = [sb(f"x_lo{i}", [P, P], F16) for i in range(2)]
        h_f = [sb(f"h_f{k}", [P, DF]) for k in range(2)]
        h_hi = [[sb(f"h_hi{i}{k}", [P, DF], F16) for k in range(2)] for i in range(2)]
        h_lo = [[sb(f"h_lo{i}{k}", [P, DF], F16) for k in range(2)] for i in range(2)]
        cat = [sb(f"cat{i}", [P, 2 * P]) for i in range(2)]
        y_lo = sb("y_lo", [P, P])
        prod = sb("prod", [P, 2 * P])
        dot = sb("dot", [P, 1])
        tg = sb("tg", [P, 1])
        gate = sb("gate", [P, 1])
        diff = sb("diff", [P, P])
        base = [sb(f"base{i}", [P, P]) for i in range(2)]
        part = sb("part", [P, P])
        fin = [sb(f"fin{i}", [P, P]) for i in range(2)]
        tok_i = [sb(f"tok_i{i}", [P, 1], I32) for i in range(2)]

        attn_in = sem("attn_in")
        small_in = sem("small_in")
        gens_in = sem("gens_in")
        w1_in = sem("w1_in")
        w2_in = sem("w2_in")
        x_in = [sem(f"x_in{i}") for i in range(NX)]
        spare_in = sem("spare_in")
        consts = sem("consts")
        prep_pe = sem("prep_pe")
        prep_act = sem("prep_act")
        prep_dve = sem("prep_dve")
        xn_ready = sem("xn_ready")
        xt_psum = sem("xt_psum")
        xt_ready = sem("xt_ready")
        u_psum = sem("u_psum")
        v_psum = sem("v_psum")
        tneg_ready = sem("tneg_ready")
        hcand_ready = sem("hcand_ready")
        omz_done = sem("omz_done")
        ab_done = sem("ab_done")
        scan_done = sem("scan_done")
        ht_psum = sem("ht_psum")
        x1_done = sem("x1_done")
        st1_done = sem("st1_done")
        mv1_done = sem("mv1_done")
        newton = sem("newton")
        y2_ready = sem("y2_ready")
        y2t_psum = sem("y2t_psum")
        y2t_ready = sem("y2t_ready")
        lg_psum = sem("lg_psum")
        lg_copied = sem("lg_copied")
        route = sem("route")
        gap_ready = sem("gap_ready")
        th_ready = sem("th_ready")
        hot_ready = sem("hot_ready")
        carry_ready = sem("carry_ready")
        rank_psum = sem("rank_psum")
        rank_done = sem("rank_done")
        rank_sum = sem("rank_sum")
        stat0 = sem("stat0")
        w2_split = sem("w2_split")
        pos_ready = sem("pos_ready")
        scattered = [sem(f"scattered{i}") for i in range(2)]
        pads_in = sem("pads_in")
        counts_psum = sem("counts_psum")
        pads_ready = sem("pads_ready")
        plan_step = sem("plan_step")
        plan_psum = sem("plan_psum")
        plan_ready = sem("plan_ready")
        row_in = [sem(f"row_in{i}") for i in range(RB)]
        x_psum = sem("x_psum")
        xhi_ready = sem("xhi_ready")
        xlo_ready = sem("xlo_ready")
        up_psum = [sem(f"up_psum{k}") for k in range(2)]
        h_ready = [sem(f"h_ready{k}") for k in range(2)]
        hhi_ready = [sem(f"hhi_ready{k}") for k in range(2)]
        hlo_ready = [sem(f"hlo_ready{k}") for k in range(2)]
        down_psum = [sem(f"down_psum{k}") for k in range(2)]
        abel_psum = sem("abel_psum")
        abel_ready = sem("abel_ready")
        ylo_done = sem("ylo_done")
        nonabel_ready = sem("nonabel_ready")
        dot_ready = sem("dot_ready")
        tg_ready = sem("tg_ready")
        diff_ready = sem("diff_ready")
        base_ready = sem("base_ready")
        part_done = sem("part_done")
        gate_done = sem("gate_done")
        fin_ready = sem("fin_ready")
        stored = [sem(f"stored{i}") for i in range(2)]

        block = ctx.enter_context(nc.Block())

        def after(eng, s, n):
            if not isinstance(n, int) or n > 0:
                eng.wait_ge(s, n)

        def wait_apart(eng, *waits):
            waits = [(s, n if isinstance(n, int) else eng.to_reg(n)) for s, n in waits]
            eng.wait_ge(consts, CONSTS)
            for s, n in waits:
                after(eng, s, n)

        def walk(eng, step, n, width=2):
            for j in range(width):
                step(j, j // 2, j % 2, 0, j)
            with eng.Fori(1, n // width - 1) as i:
                for k in range(width):
                    step(width * i + k, width // 2 * i + k // 2, k % 2, i, k)
            for j in range(n - width, n + 2):
                step(j, j // 2, j % 2, j // width, j % width)

        def known(j, n):
            return j if isinstance(j, int) else None

        NEWTON = 11

        def rsqrt(dve, tab, s, base_count, first_src_done):
            v, y, t, u = (tab[:, k, :] for k in range(4))
            n = [0]

            def link(ins):
                n[0] += 1
                ins.then_inc(s, 1)
                return n[0]

            def wait():
                dve.wait_ge(s, base_count + n[0])

            first_src_done()
            link(nc.vector.tensor_scalar(t.bitcast(I32), v.bitcast(I32), 1, None, ALU.logical_shift_right))
            wait()
            link(nc.vector.tensor_scalar(y.bitcast(I32), t.bitcast(I32), -1.0, MAGIC, ALU.mult, ALU.add))
            for _ in range(3):
                wait()
                link(nc.vector.tensor_tensor(t, y, y, ALU.mult))
                wait()
                link(nc.vector.scalar_tensor_tensor(u, t, -0.5, v, ALU.mult, ALU.mult))
                wait()
                link(nc.vector.scalar_tensor_tensor(y, u, 1.5, y, ALU.add, ALU.mult))
            assert n[0] == NEWTON

        NEWTON1 = NEWTON + 2
        ROUTE = 12
        CONSTS = 19 + 2 * NP
        ACT_PREP1 = 12 + 2 * SQUARINGS + 2 * E + 3
        ACT_PREP = ACT_PREP1 + 6
        DVE_PREP = 21
        PLAN = 15

        @block.sync
        def _(sp):
            for dst, src in ((wz_n[:], wz), (wh_n[:], wh), (bz_c[:], bz.rearrange("(p a) -> p a", a=1)),
                             (bh_c[:], bh.rearrange("(p a) -> p a", a=1))):
                sp.dma_start(dst, src).then_inc(attn_in, 16)
            sp.dma_start(a_1[:].rearrange("p (g d) -> p g d", g=NROT), gens.rearrange("g p d -> p g d")).then_inc(gens_in, 16)
            for c in range(NX):
                sp.dma_start(x_all[:, c * XT:(c + 1) * XT, :], x_tiles[:, c * XT:(c + 1) * XT, :]).then_inc(x_in[c], 16)
            for dst, src in (
                (g_c[:], ln_g.rearrange("(p a) -> p a", a=1)),
                (beta_c[:, 0:1], ln_b.rearrange("(p a) -> p a", a=1)),
                (beta_c[:, 1:2], ln_b.rearrange("(p a) -> p a", a=1)),
                (aw_n[:], abel_w), (ab_r[:], abel_b.rearrange("(a n) -> a n", a=1)),
                (gw_n[:], gate_w), (gb_r[:], gate_b.rearrange("(a n) -> a n", a=1)),
                (b1_n[:], b1.rearrange("e (f p) -> (e f) p", p=P)), (b2_n[:], b2),
                (mix_r[:, 0:2 * P], mix_w.rearrange("n a -> a n")),
                (mix_r[:, 2 * P:2 * P + 1], mix_b.rearrange("(a n) -> a n", a=1)),
            ):
                sp.dma_start(dst, src).then_inc(small_in, 16)
            sp.dma_start(w1_n[:], w1.rearrange("e d f -> d e f")).then_inc(w1_in, 16)
            sp.dma_start(w2_n[:].rearrange("p (e f) d -> p e f d", e=E),
                         w2.rearrange("e (f p) d -> p e f d", p=P)).then_inc(w2_in, 16)
            sp.wait_ge(consts, CONSTS)
            sp.dma_start(slots[SPARE:SPARE + P, :], zero_row[:]).then_inc(spare_in, 16)
            sp.wait_ge(spare_in, 16)
            sp.wait_ge(plan_ready, 1)
            for s in scattered:
                sp.wait_ge(s, 16 * CT * NCH // 2)
            sp.wait_ge(pads_in, 16 * NP)

            def step(j, half, par, quarter, slot):
                if known(j, 0) is not None and j >= NS:
                    return
                at = sp.value_load(plan[2:3, bass.ds(j, 1)], min_val=0, max_val=SPARE)
                after(sp, fin_ready, j - RB + 1)
                sp.dma_start(srow[slot][:], slots[bass.ds(at, P), :]).then_inc(row_in[slot], 16)

            walk(sp, step, NS, RB)

        @block.gpsimd
        def _(pool):
            n = [0]

            def done(ins):
                n[0] += 1
                ins.then_inc(consts, 1)

            done(pool.memset(ident[:], 0.0))
            done(pool.memset(ident2[:], 0.0))
            done(pool.memset(tri[:], 1.0))
            done(pool.memset(ones_b[:], 1.0))
            done(pool.memset(ones_f[:], 1.0))
            done(pool.memset(ones_h[:], 1.0))
            done(pool.memset(row_sel[:], 0.0))
            done(pool.memset(zero_row[:], 0.0))
            done(pool.memset(pl[:, 5, :], 1.0))
            done(pool.memset(carry[:], 0.0))
            pool.wait_ge(consts, n[0])
            done(pool.memset(zero_row[:, TOKEN:TOKEN + 1], float(TOK)))
            done(pool.affine_select(out=ident[:], in_=ident[:], compare_op=ALU.not_equal, fill=1.0,
                                    base=0, pattern=[[-1, P]], channel_multiplier=1))
            done(pool.affine_select(out=ident2[:], in_=ident2[:], compare_op=ALU.not_equal, fill=2.0,
                                    base=0, pattern=[[-1, P]], channel_multiplier=1))
            done(pool.affine_select(out=tri[:], in_=tri[:], compare_op=ALU.is_gt, fill=0.0,
                                    base=0, pattern=[[1, P]], channel_multiplier=-1))
            done(pool.affine_select(out=row_sel[:], in_=row_sel[:], compare_op=ALU.not_equal, fill=1.0,
                                    base=0, pattern=[[-1, 2]], channel_multiplier=1))
            exact = dict(allow_small_or_imprecise_dtypes=True)
            done(pool.iota(pair_no[:], pattern=[[1, NP]], base=0, channel_multiplier=0, **exact))
            done(pool.iota(pad_base[:], pattern=[[REGION, NP]], base=0, channel_multiplier=1, **exact))
            done(pool.iota(part_no[:], pattern=[[0, 1]], base=0, channel_multiplier=1, **exact))
            done(pool.iota(tok_no[:], pattern=[[P, NT]], base=0, channel_multiplier=1, **exact))
            for k, (a, b) in enumerate(PAIRS):
                done(pool.memset(lo_tab[:, k:k + 1], float(a)))
                done(pool.memset(hi_tab[:, k:k + 1], float(b)))
            assert n[0] == CONSTS

            def step(j, half, par, quarter, slot):
                if known(j, 0) is not None and j >= NCH:
                    return
                wait_apart(pool, (pos_ready, j + 1))
                for t in range(CT):
                    pool.indirect_dma_start(
                        out=slots, out_offset=bass.IndirectOffsetOnAxis(ap=pos[par][:, t:t + 1], axis=0),
                        in_=rows[par][:, t, :], in_offset=None).then_inc(scattered[par], 16)

            walk(pool, step, NCH)
            pool.wait_ge(pads_ready, 1)
            for k in range(NP):
                pool.indirect_dma_start(
                    out=slots, out_offset=bass.IndirectOffsetOnAxis(ap=pad_at[:, k:k + 1], axis=0),
                    in_=zero_row[:], in_offset=None).then_inc(pads_in, 16)

            def tile(j, half, par, quarter, slot):
                jj = known(j, 0)
                if jj is None or jj < NS:
                    wait_apart(pool, (h_ready[0], j + 1), (down_psum[0], j - 1))
                    pool.tensor_copy(h_hi[par][0][:], h_f[0][:]).then_inc(hhi_ready[0], 1)
                if jj is None or jj >= 2:
                    wait_apart(pool, (fin_ready, j - 1))
                    pool.indirect_dma_start(
                        out=out_rows, out_offset=bass.IndirectOffsetOnAxis(ap=tok_i[par][:, 0:1], axis=0),
                        in_=fin[par][:], in_offset=None, bounds_check=TOK - 1, oob_is_err=False,
                    ).then_inc(stored[par], 16)
                if jj is None or jj < NS:
                    wait_apart(pool, (h_ready[1], j + 1), (down_psum[1], j - 1))
                    pool.tensor_copy(h_hi[par][1][:], h_f[1][:]).then_inc(hhi_ready[1], 1)
                if jj is None or 1 <= jj <= NS:
                    pool.wait_ge(dot_ready, j)
                    after(pool, fin_ready, j - 1)
                    pool.tensor_tensor(diff[:], cat[1 - par][:, P:2 * P], cat[1 - par][:, 0:P],
                                       ALU.subtract).then_inc(diff_ready, 1)

            walk(pool, tile, NS, RB)
            for s in stored:
                pool.wait_ge(s, 16 * NS // 2)

        @block.scalar
        def _(act):
            n = [0]

            def done(ins):
                n[0] += 1
                ins.then_inc(prep_act, 1)

            act.wait_ge(attn_in, 64)
            done(act.activation(nbz[:], bz_c[:], ACT.Gelu))
            act.wait_ge(prep_act, 1)
            done(act.mul(nbz[:], bz_c[:], -0.5))
            act.wait_ge(prep_pe, 1)
            done(act.copy(wzh_t[:].rearrange("p a b -> p (a b)"), bank[0][:, 0:2 * P]))
            act.wait_ge(prep_pe, 2)
            done(act.copy(a_1t[:], bank[1][:, 0:RG]))
            act.wait_ge(prep_pe, 3)
            done(act.copy(a_2[:], bank[1][:, 0:RG]))
            done(act.copy(a_2t[:], bank[2][:, 0:RG]))
            act.wait_ge(prep_pe, 4)
            done(act.copy(a_3[:], bank[3][:, 0:RG]))
            done(act.mul(a_4t[:], bank[4][:, 0:RG], 1.0 / 24.0))
            act.wait_ge(prep_pe, 5)
            done(act.copy(em[0][:], bank[1][:, 0:RG]))
            act.wait_ge(prep_pe, 6)
            done(act.copy(emt[0][:], bank[2][:, 0:RG]))
            for k in range(SQUARINGS):
                act.wait_ge(prep_pe, 7 + k)
                done(act.copy(em[(k + 1) % 2][:], bank[1][:, 0:RG]))
                done(act.copy(emt[(k + 1) % 2][:], bank[2][:, 0:RG]))
            act.wait_ge(prep_pe, 7 + SQUARINGS)
            done(act.copy(f_s[:].rearrange("p a b -> p (a b)"), bank[1][:, 0:2 * P]))
            act.wait_ge(prep_pe, 8 + SQUARINGS)
            done(act.copy(rot[:], bank[2][:, 0:P]))
            assert n[0] == 12 + 2 * SQUARINGS
            for e in range(E):
                act.wait_ge(prep_pe, 9 + SQUARINGS + 2 * e)
                done(act.copy(w2_t[:], bank[3][:]))
                act.wait_ge(prep_pe, 10 + SQUARINGS + 2 * e)
                done(act.mul(w2_hi[:, e * FB:(e + 1) * FB, :].rearrange("p a b -> p (a b)"), bank[4][:], WSCALE))
            PE0 = 8 + SQUARINGS + 2 * E
            act.wait_ge(prep_pe, PE0 + 1)
            done(act.copy(b1_t[:], bank[5][:, 0:E * FB]))
            for k in range(2):
                done(act.copy(b2_t[:, :, k], bank[5][:, 64:64 + E]))
            assert n[0] == ACT_PREP1
            act.wait_ge(prep_pe, PE0 + 2)
            done(act.copy(gb[:], bank[7][0:1, 256:256 + E]))
            done(act.mul(ab_s[:], bank[7][0:2, 0:P], WSCALE))
            done(act.copy(mix_b_all[:], bank[5][:, 0:2 * P + 1]))
            for k in range(2):
                done(act.mul(b2_s[:, k * 512:(k + 1) * 512], bank[k][0:2, :], WSCALE))
            act.wait_ge(prep_act, n[0])
            done(act.mul(mixb_h[:], mix_b_all[:, 2 * P:2 * P + 1], 0.5))
            assert n[0] == ACT_PREP

            def step(i, half, par, quarter, slot):
                ii = known(i, 0)
                if ii is None or ii < NCH:
                    act.wait_ge(xt_psum, i + 1)
                    after(act, v_psum, i)
                    act.copy(x_t[:], bank[0][:]).then_inc(xt_ready, 1)
                    act.wait_ge(u_psum, i + 1)
                    after(act, ab_done, 2 * i)
                    act.activation(tneg[:], bank[1][:], ACT.Tanh, bias=nbz[:], scale=-0.5).then_inc(tneg_ready, 1)
                    act.wait_ge(v_psum, i + 1)
                    act.activation(hcand[:], bank[2][:], ACT.Identity, bias=bh_c[:]).then_inc(hcand_ready, 1)
                if ii is None or 1 <= ii <= NCH:
                    act.wait_ge(y2t_psum, i)
                    after(act, lg_psum, i - 1)
                    act.copy(y2_t[:], bank[4][:]).then_inc(y2t_ready, 1)
                    act.wait_ge(gap_ready, i)
                    after(act, pos_ready, i - 1)
                    act.activation(th[:], gaps[:], ACT.Tanh).then_inc(th_ready, 1)

            walk(act, step, NCH)
            act.wait_ge(plan_ready, 1)

            def tile(j, half, par, quarter, slot):
                jj = known(j, 0)

                def up(k):
                    e = act.value_load(plan[k:k + 1, bass.ds(j, 1)], min_val=0, max_val=E - 1)
                    act.wait_ge(up_psum[k], j + 1)
                    after(act, hlo_ready[k], j)
                    for f in range(FB):
                        ins = act.activation(h_f[k][:, f * P:(f + 1) * P], bank[1 + k][:, f * P:(f + 1) * P],
                                             ACT.Gelu, bias=b1_s[:, bass.ds(e * FB + f, 1)], scale=1.0 / WSCALE)
                    ins.then_inc(h_ready[k], 1)

                if jj == 0:
                    act.wait_ge(x_psum, 1)
                    act.copy(x_hi[0][:], bank[0][:, 0:P]).then_inc(xhi_ready, 1)
                if jj is None or jj < NS:
                    up(0)
                    act.wait_ge(abel_psum, j + 1)
                    after(act, fin_ready, j - 1)
                    act.activation(cat[par][:, 0:P], bank[5][:, 0:P], ACT.Gelu, scale=1.0 / WSCALE)\
                       .then_inc(abel_ready, 1)
                    act.activation(base[par][:], srow[slot][:, 0:P], ACT.Identity,
                                   bias=srow[slot][:, MEAN_R:MEAN_R + 1],
                                   scale=srow[slot][:, SCALE_R:SCALE_R + 1]).then_inc(base_ready, 1)
                if jj is None or jj < NS - 1:
                    act.wait_ge(x_psum, j + 2)
                    after(act, up_psum[1], j)
                    act.copy(x_hi[1 - par][:], bank[0][:, 0:P]).then_inc(xhi_ready, 1)
                if jj is None or jj < NS:
                    up(1)
                if jj is None or 1 <= jj <= NS:
                    act.wait_ge(dot_ready, j)
                    act.activation(tg[:], dot[:], ACT.Tanh, bias=mixb_h[:], scale=0.5).then_inc(tg_ready, 1)

            walk(act, tile, NS, RB)

        @block.tensor
        def _(pe):
            n = [0]

            def done(ins):
                n[0] += 1
                ins.then_inc(prep_pe, 1)

            def mm(o, lhs, rhs, start=True, stop=True):
                return pe.matmul(o, lhs, rhs, start=start, stop=stop)

            def g(t, k):
                return t[:, k * P:(k + 1) * P]

            pe.wait_ge(consts, CONSTS)
            pe.wait_ge(attn_in, 64)
            pe.transpose(bank[0][:, 0:P], wz_n[:], ident[:])
            done(pe.transpose(bank[0][:, P:2 * P], wh_n[:], ident[:]))
            pe.wait_ge(prep_dve, 1)
            for k in range(NROT):
                ins = pe.transpose(g(bank[1], k), g(a_1, k), ident[:])
            done(ins)
            pe.wait_ge(prep_act, 4)
            for k in range(NROT):
                mm(g(bank[1], k), g(a_1t, k), g(a_1, k))
                ins = mm(g(bank[2], k), g(a_1, k), g(a_1t, k))
            done(ins)
            pe.wait_ge(prep_act, 6)
            for k in range(NROT):
                mm(g(bank[3], k), g(a_1t, k), g(a_2, k))
                ins = mm(g(bank[4], k), g(a_2, k), g(a_2t, k))
            done(ins)
            pe.wait_ge(prep_act, 8)
            pe.wait_ge(prep_dve, 6)
            for k in range(NROT):
                mm(g(bank[1], k), g(a_4t, k), g(q_s, k), stop=False)
                ins = mm(g(bank[1], k), ident[:], g(p_s, k), start=False)
            done(ins)
            pe.wait_ge(prep_act, 9)
            for k in range(NROT):
                ins = pe.transpose(g(bank[2], k), g(em[0], k), ident[:])
            done(ins)
            for s in range(SQUARINGS):
                pe.wait_ge(prep_act, 10 + 2 * s)
                e, et = em[s % 2], emt[s % 2]
                for k in range(NROT):
                    mm(g(bank[1], k), g(et, k), g(e, k), stop=False)
                    mm(g(bank[1], k), ident2[:], g(e, k), start=False)
                    mm(g(bank[2], k), g(e, k), g(et, k), stop=False)
                    ins = mm(g(bank[2], k), ident2[:], g(et, k), start=False)
                done(ins)
            e, et = em[SQUARINGS % 2], emt[SQUARINGS % 2]
            pe.wait_ge(prep_act, 10 + 2 * SQUARINGS)
            mm(g(bank[1], 0), g(et, 0), g(e, 1), stop=False)
            mm(g(bank[1], 0), ident[:], g(e, 0), start=False, stop=False)
            mm(g(bank[1], 0), ident[:], g(e, 1), start=False)
            mm(g(bank[1], 1), g(e, 1), g(et, 0), stop=False)
            mm(g(bank[1], 1), ident[:], g(et, 0), start=False, stop=False)
            done(mm(g(bank[1], 1), ident[:], g(et, 1), start=False))
            pe.wait_ge(prep_act, 11 + 2 * SQUARINGS)
            mm(g(bank[2], 0), f_s[:, 1, :], g(e, 2), stop=False)
            mm(g(bank[2], 0), ident[:], f_s[:, 0, :], start=False, stop=False)
            mm(g(bank[2], 0), ident[:], g(e, 2), start=False, stop=False)
            done(mm(g(bank[2], 0), ident[:], ident[:], start=False))
            pe.wait_ge(w2_in, 16)
            pe.wait_ge(prep_act, 12 + 2 * SQUARINGS)
            A0 = 12 + 2 * SQUARINGS
            for ex in range(E):
                pe.wait_ge(prep_act, A0 + 2 * ex)
                for f in range(FB):
                    ins = pe.transpose(g(bank[3], f), w2_n[:, ex * FB + f, :], ident[:])
                done(ins)
                pe.wait_ge(prep_act, A0 + 2 * ex + 1)
                if ex:
                    pe.wait_ge(w2_split, ex)
                for f in range(FB):
                    ins = mm(g(bank[4], f), g(w2_t, f), rot[:])
                done(ins)
            pe.wait_ge(small_in, 16 * 11)
            pe.transpose(bank[5][:, 0:E * FB], b1_n[:], ident[0:E * FB, 0:E * FB])
            done(pe.transpose(bank[5][:, 64:64 + E], b2_n[:], ident[0:E, 0:E]))
            pe.wait_ge(prep_act, ACT_PREP1)
            pe.wait_ge(w1_in, 16)
            for ex in range(E):
                mm(bank[ex // 4][0:2, (ex % 4) * P:(ex % 4 + 1) * P], b2_t[:, ex, :], rot[:])
            for ex in range(E):
                for f in range(FB):
                    mm(bank[6][:, ex * FB + f:ex * FB + f + 1], w1_n[:, ex, f * P:(f + 1) * P], beta_c[:, 0:1])
            mm(bank[5][:, 0:2 * P + 1], ones_f[:], mix_r[:])
            mm(bank[7][0:1, 256:256 + E], beta_c[:, 0:1], gw_n[:], stop=False)
            mm(bank[7][0:1, 256:256 + E], ones_f[:, 0:1], gb_r[:], start=False)
            mm(bank[7][0:2, 0:P], beta_c[:], aw_n[:], stop=False)
            done(mm(bank[7][0:2, 0:P], ones_f[:, 0:2], ab_r[:], start=False))
            pe.wait_ge(prep_act, ACT_PREP)
            pe.wait_ge(prep_dve, DVE_PREP)
            pe.wait_ge(w2_split, E)

            def step(i, half, par, quarter, slot):
                ii = known(i, 0)
                a = ii is None or ii < NCH
                b = ii is None or 1 <= ii <= NCH
                if b:
                    pe.wait_ge(scan_done, i)
                    after(pe, x1_done, i - 1)
                    for t in range(CT):
                        ins = pe.transpose(g(bank[3], t), g(hseq[1 - par], t), ident[:])
                    ins.then_inc(ht_psum, 1)
                if a:
                    pe.wait_ge(xn_ready, i + 1)
                    after(pe, xt_ready, i)
                    for t in range(CT):
                        ins = pe.transpose(g(bank[0], t), xn[par][:, t, :], ident[:])
                    ins.then_inc(xt_psum, 1)
                    pe.wait_ge(xt_ready, i + 1)
                    after(pe, tneg_ready, i)
                    mm(bank[1][:], wzh_t[:, 0, :], x_t[:]).then_inc(u_psum, 1)
                    after(pe, hcand_ready, i)
                    mm(bank[2][:], wzh_t[:, 1, :], x_t[:]).then_inc(v_psum, 1)
                if b:
                    pe.wait_ge(y2_ready, i)
                    after(pe, y2t_ready, i - 1)
                    for t in range(CT):
                        ins = pe.transpose(g(bank[4], t), rows[1 - par][:, t, 0:P], ident[:])
                    ins.then_inc(y2t_psum, 1)
                    pe.wait_ge(y2t_ready, i)
                    after(pe, lg_copied, i - 1)
                    for t in range(CT):
                        mm(bank[6][:, t * E:(t + 1) * E], g(y2_t, t), gw[:], stop=False)
                        ins = mm(bank[6][:, t * E:(t + 1) * E], ones_f[:], gb[:], start=False)
                    ins.then_inc(lg_psum, 1)
                    pe.wait_ge(hot_ready, i)
                    after(pe, carry_ready, i - 1)
                    after(pe, rank_done, i - 1)
                    r = bank[7][:, 0:CT * NP]
                    mm(r, tri[:], hot[:].rearrange("p t n -> p (t n)"), stop=False)
                    r3 = r.rearrange("p (t n) -> p t n", t=CT)
                    for t in range(CT - 1):
                        mm(r3[:, t + 1:CT, :], ones_b[:],
                           hot[:, t:t + 1, :].broadcast_to([P, CT - 1 - t, NP]), start=False, stop=False)
                    mm(r3, ones_b[:], carry[:].rearrange("p (a n) -> p a n", a=1).broadcast_to([P, CT, NP]),
                       start=False).then_inc(rank_psum, 1)

            walk(pe, step, NCH)
            pe.wait_ge(carry_ready, NCH)
            pe.wait_ge(rank_done, NCH)
            mm(bank[7][:, 0:NP], ones_b[:], carry[:]).then_inc(counts_psum, 1)
            pe.wait_ge(plan_step, PLAN)
            pe.transpose(bank[6][0:3, 0:P], plan_f[:], ident[:]).then_inc(plan_psum, 1)
            pe.wait_ge(plan_ready, 1)

            def tile(j, half, par, quarter, slot):
                jj = known(j, 0)

                def turn(j, slot, n):
                    pe.wait_ge(row_in[slot], 16 * n)
                    after(pe, xlo_ready, j)
                    pe.transpose(bank[0][:, 0:P], srow[slot][:, 0:P], ident[:]).then_inc(x_psum, 1)

                def up(k):
                    e = pe.value_load(plan[k:k + 1, bass.ds(j, 1)], min_val=0, max_val=E - 1)
                    pe.wait_ge(xlo_ready, j + 1)
                    after(pe, h_ready[k], j)
                    for f in range(FB):
                        o = g(bank[1 + k], f)
                        hi = w1_hi[:, bass.ds(e, 1), f * P:(f + 1) * P].rearrange("p a n -> p (a n)")
                        lo = w1_lo[:, bass.ds(e, 1), f * P:(f + 1) * P].rearrange("p a n -> p (a n)")
                        mm(o, hi, x_hi[par][:], stop=False)
                        mm(o, hi, x_lo[par][:], start=False, stop=False)
                        ins = mm(o, lo, x_hi[par][:], start=False)
                    ins.then_inc(up_psum[k], 1)

                def down(k):
                    e = pe.value_load(plan[k:k + 1, bass.ds(j - 1, 1)], min_val=0, max_val=E - 1)
                    pe.wait_ge(hlo_ready[k], j)
                    after(pe, ylo_done if k == 0 else nonabel_ready, j - 1)
                    o = bank[3 + k][:, 0:P]
                    mm(o, ones_h[:], b2_hl[:, bass.ds(e * P, P)], stop=False)
                    hh, hl = h_hi[1 - par][k], h_lo[1 - par][k]
                    for f in range(FB):
                        hi = w2_hi[:, bass.ds(e * FB + f, 1), :].rearrange("p a n -> p (a n)")
                        lo = w2_lo[:, bass.ds(e * FB + f, 1), :].rearrange("p a n -> p (a n)")
                        mm(o, g(hh, f), hi, start=False, stop=False)
                        mm(o, g(hh, f), lo, start=False, stop=False)
                        ins = mm(o, g(hl, f), hi, start=False, stop=(f == FB - 1))
                    ins.then_inc(down_psum[k], 1)

                here = jj is None or jj < NS
                prev = jj is None or 1 <= jj <= NS
                if jj == 0:
                    turn(0, 0, 1)
                if here:
                    up(0)
                    after(pe, abel_ready, j)
                    o = bank[5][:, 0:P]
                    mm(o, ones_h[:], ab_hl[:], stop=False)
                    mm(o, x_hi[par][:], aw_hi[:], start=False, stop=False)
                    mm(o, x_hi[par][:], aw_lo[:], start=False, stop=False)
                    mm(o, x_lo[par][:], aw_hi[:], start=False).then_inc(abel_psum, 1)
                if prev:
                    down(0)
                if jj is None or jj < NS - 1:
                    turn(j + 1, (slot + 1) % RB, quarter + (slot + 1) // RB + 1)
                if here:
                    up(1)
                if prev:
                    down(1)

            walk(pe, tile, NS, RB)

        @block.vector
        def _(dve):
            n = [0]

            def done(ins):
                n[0] += 1
                ins.then_inc(prep_dve, 1)

            def split(hi, lo, src, scale, first):
                done(nc.vector.tensor_scalar(hi, src, scale, None, ALU.mult))
                dve.wait_ge(prep_dve, n[0])
                done(nc.vector.scalar_tensor_tensor(lo, src, scale, hi, ALU.mult, ALU.subtract))

            def rows_split(dst, hi, lo, src):
                done(nc.vector.tensor_copy(hi, src))
                dve.wait_ge(prep_dve, n[0])
                done(nc.vector.scalar_tensor_tensor(lo, src, 1.0, hi, ALU.mult, ALU.subtract))
                dve.wait_ge(prep_dve, n[0])
                done(nc.vector.tensor_scalar(lo, lo, row_sel[:, 1:2], None, ALU.mult))
                dve.wait_ge(prep_dve, n[0])
                done(nc.vector.scalar_tensor_tensor(dst, hi, row_sel[:, 0:1], lo, ALU.mult, ALU.add))

            dve.wait_ge(gens_in, 16)
            done(nc.vector.tensor_scalar(a_1[:], a_1[:], 2.0 ** -SQUARINGS, None, ALU.mult))

            def stats(c):
                dve.wait_ge(x_in[c], 16)
                for t in range(c * XT, (c + 1) * XT):
                    ins = nc.vector.bn_stats(st0[:, t, :], x_all[:, t, :])
                ins.then_inc(stat0, 1)
                dve.wait_ge(stat0, 2 * c + 1)
                for t in range(c * XT, (c + 1) * XT):
                    ins = nc.vector.bn_aggr(mv0[:, t, :], st0[:, t, :])
                ins.then_inc(stat0, 1)

            stats(0)
            dve.wait_ge(prep_act, 8)
            dve.wait_ge(consts, CONSTS)
            def g3(t):
                return t[:].rearrange("p (g d) -> p g d", g=NROT)
            id3 = ident[:].rearrange("p (a d) -> p a d", a=1).broadcast_to([P, NROT, P])
            done(nc.vector.scalar_tensor_tensor(p_s[:], a_2[:], 0.5, a_1[:], ALU.mult, ALU.add))
            done(nc.vector.scalar_tensor_tensor(g3(q_s), g3(a_1), 1.0 / 5, id3, ALU.mult, ALU.add))
            dve.wait_ge(prep_dve, 3)
            done(nc.vector.scalar_tensor_tensor(p_s[:], a_3[:], 1.0 / 6, p_s[:], ALU.mult, ALU.add))
            done(nc.vector.scalar_tensor_tensor(q_s[:], a_2[:], 1.0 / 30, q_s[:], ALU.mult, ALU.add))
            dve.wait_ge(prep_dve, 5)
            done(nc.vector.scalar_tensor_tensor(q_s[:], a_3[:], 1.0 / 210, q_s[:], ALU.mult, ALU.add))
            for c in range(1, NX):
                stats(c)
            dve.wait_ge(stat0, 2 * NX)
            nc.vector.tensor_scalar(nw0[:, 0, :], mv0[:, :, 1], EPS, None, ALU.add).then_inc(stat0, 1)
            rsqrt(dve, nw0, stat0, 2 * NX + 1, lambda: dve.wait_ge(stat0, 2 * NX + 1))
            dve.wait_ge(small_in, 16 * 11)
            done(nc.vector.tensor_scalar(g256[:], g_c[:], WSCALE, None, ALU.mult))
            done(nc.vector.tensor_scalar(gw[:], gw_n[:], g_c[:, 0:1], None, ALU.mult))
            dve.wait_ge(prep_dve, 8)
            split(aw_hi[:], aw_lo[:], aw_n[:], g256[:, 0:1], 0)
            dve.wait_ge(w1_in, 16)
            split(w1_hi[:], w1_lo[:], w1_n[:], g256[:, 0:1], 0)
            for ex in range(E):
                dve.wait_ge(prep_act, 12 + 2 * SQUARINGS + 2 * ex + 2)
                lo = w2_lo[:, ex * FB:(ex + 1) * FB, :].rearrange("p a b -> p (a b)")
                hi = w2_hi[:, ex * FB:(ex + 1) * FB, :].rearrange("p a b -> p (a b)")
                nc.vector.scalar_tensor_tensor(lo, bank[4][:], WSCALE, hi, ALU.mult, ALU.subtract).then_inc(w2_split, 1)
            dve.wait_ge(prep_act, ACT_PREP)
            dve.wait_ge(prep_pe, 10 + SQUARINGS + 2 * E)
            done(nc.vector.tensor_tensor(b1_s[:], bank[6][:, 0:E * FB], b1_t[:], ALU.add))
            rows_split(ab_hl[:], ab_h[:], ab_l[:], ab_s[:])
            rows_split(b2_hl[:], b2_h[:], b2_l[:], b2_s[:])
            assert n[0] == DVE_PREP
            dve.wait_ge(stat0, 2 * NX + 1 + NEWTON)

            def normalize(i, par):
                after(dve, xt_psum, i - 1)
                for t in range(CT):
                    c = i * CT + t
                    ins = nc.vector.tensor_scalar(
                        xn[par][:, t, :], x_all[:, bass.ds(c, 1), :].rearrange("p a d -> p (a d)"),
                        mv0[:, bass.ds(c, 1), 0:1].rearrange("p a d -> p (a d)"),
                        nw0[:, 1, bass.ds(c, 1)], ALU.subtract, ALU.mult)
                ins.then_inc(xn_ready, 1)

            def step(i, half, par, quarter, slot):
                ii = known(i, 0)
                a = ii is None or ii < NCH
                b = ii is None or 1 <= ii <= NCH
                if ii == 0:
                    normalize(0, 0)
                if b:
                    row = rows[1 - par]
                    dve.wait_ge(ht_psum, i)
                    nc.vector.tensor_tensor(x1[:], x_all[:, bass.ds((i - 1) * CT, CT), :],
                                            bank[3][:].rearrange("p (t d) -> p t d", t=CT), ALU.add).then_inc(x1_done, 1)
                    dve.wait_ge(x1_done, i)
                    for t in range(CT):
                        ins = nc.vector.bn_stats(st1[:, t, :], x1[:, t, :])
                    ins.then_inc(st1_done, 1)
                    wait_apart(dve, (st1_done, i))
                    for t in range(CT):
                        ins = nc.vector.bn_aggr(mv1[:, t, :], st1[:, t, :])
                    ins.then_inc(mv1_done, 1)
                    dve.wait_ge(mv1_done, i)
                    n1 = (i - 1) * NEWTON1
                    nc.vector.tensor_scalar(nw1[:, 0, 0:CT], mv1[:, :, 1], EPS, None, ALU.add).then_inc(newton, 1)
                    nc.vector.tensor_scalar(nw1[:, 0, CT:2 * CT], mv1[:, :, 1], 1.0 + EPS, EPS * EPS,
                                            ALU.mult, ALU.add).then_inc(newton, 1)
                    rsqrt(dve, nw1, newton, n1 + 2, lambda: dve.wait_ge(newton, n1 + 2))
                    dve.wait_ge(newton, n1 + NEWTON1)
                    after(dve, scattered[1 - par], 16 * CT * (half - 1 + par))
                    for t in range(CT):
                        ins = nc.vector.tensor_scalar(row[:, t, 0:P], x1[:, t, :], mv1[:, t, 0:1],
                                                      nw1[:, 1, CT + t:CT + t + 1], ALU.subtract, ALU.mult)
                    ins.then_inc(y2_ready, 1)
                    r1 = (i - 1) * ROUTE
                    nc.vector.tensor_tensor(sy[:], nw1[:, 0, CT:2 * CT], nw1[:, 1, CT:2 * CT], ALU.mult).then_inc(route, 1)
                    dve.wait_ge(route, r1 + 1)
                    nc.vector.scalar_tensor_tensor(row[:, :, SCALE_R], nw1[:, 1, 0:CT], 1.0, sy[:], ALU.add, ALU.mult)
                    nc.vector.tensor_copy(row[:, :, MEAN_R], mv1[:, :, 0])
                    nc.vector.tensor_copy(row[:, :, TOKEN], tok_no[:, bass.ds((i - 1) * CT, CT)])
                if a:
                    dve.wait_ge(tneg_ready, i + 1)
                    nc.vector.tensor_scalar(omz[:], tneg[:], 1.0, 0.5, ALU.add, ALU.mult).then_inc(omz_done, 1)
                    dve.wait_ge(omz_done, i + 1)
                    nc.vector.tensor_scalar(acoef[:], omz[:], A_GUARD, None, ALU.add).then_inc(ab_done, 1)
                    dve.wait_ge(hcand_ready, i + 1)
                    nc.vector.scalar_tensor_tensor(bneg[:], omz[:], 1.0, hcand[:], ALU.subtract, ALU.mult).then_inc(ab_done, 1)
                    dve.wait_ge(ab_done, 2 * (i + 1))
                    after(dve, ht_psum, i - 1)
                    for s in range(BPC):
                        c = slice(s * T, (s + 1) * T)
                        ins = nc.vector.tensor_tensor_scan(hseq[par][:, c], acoef[:, c], bneg[:, c], 0.0,
                                                           ALU.mult, ALU.subtract)
                    ins.then_inc(scan_done, 1)
                if b:
                    dve.wait_ge(lg_psum, i)
                    nc.vector.tensor_copy(lg[:].rearrange("p t e -> p (t e)"), bank[6][:, 0:CT * E]).then_inc(lg_copied, 1)
                    wait_apart(dve, (lg_copied, i))
                    for t in range(CT):
                        ins = nc.vector.max(mx[:, t, :], lg[:, t, :])
                    ins.then_inc(route, 1)
                    wait_apart(dve, (route, r1 + 2))
                    for t in range(CT):
                        ins = nc.vector.max_index(mi[:, t, :], mx[:, t, :], lg[:, t, :])
                    ins.then_inc(route, 1)
                    nc.vector.tensor_tensor(gap[:], mx[:, :, 0], mx[:, :, 1], ALU.subtract).then_inc(route, 1)
                    dve.wait_ge(route, r1 + 3)
                    nc.vector.tensor_copy(idx[:], mi[:, :, 0:2]).then_inc(route, 1)
                    dve.wait_ge(route, r1 + 5)
                    nc.vector.tensor_tensor(elo[:], idx[:, :, 0], idx[:, :, 1], ALU.min).then_inc(route, 1)
                    nc.vector.tensor_tensor(sgn[:], idx[:, :, 0], idx[:, :, 1], ALU.is_lt).then_inc(route, 1)
                    nc.vector.tensor_tensor(ehi[:], idx[:, :, 0], idx[:, :, 1], ALU.max).then_inc(route, 1)
                    dve.wait_ge(route, r1 + 7)
                    nc.vector.scalar_tensor_tensor(gaps[:], sgn[:], -0.5, gap[:], ALU.add, ALU.mult).then_inc(gap_ready, 1)
                    nc.vector.tensor_scalar(pr1[:], elo[:], -0.5, (2 * E - 3) / 2, ALU.mult, ALU.add).then_inc(route, 1)
                    dve.wait_ge(route, r1 + 9)
                    nc.vector.tensor_tensor(pr1[:], pr1[:], elo[:], ALU.mult).then_inc(route, 1)
                    dve.wait_ge(route, r1 + 10)
                    nc.vector.scalar_tensor_tensor(pair[:], pr1[:], -1.0, ehi[:], ALU.add, ALU.add).then_inc(route, 1)
                    dve.wait_ge(route, r1 + 11)
                    nc.vector.tensor_tensor(
                        hot[:], pair_no[:].rearrange("p (a n) -> p a n", a=1).broadcast_to([P, CT, NP]),
                        pair[:].rearrange("p (t a) -> p t a", a=1).broadcast_to([P, CT, NP]), ALU.is_equal).then_inc(hot_ready, 1)
                if ii is None or ii < NCH - 1:
                    normalize(i + 1, 1 - par)
                if b:
                    dve.wait_ge(hot_ready, i)
                    nc.vector.tensor_reduce(hsum[:], hot[:].rearrange("p t n -> p n t"), AX.X, ALU.add).then_inc(route, 1)
                    dve.wait_ge(th_ready, i)
                    nc.vector.tensor_scalar(row[:, :, W_LO], th[:], 0.5 / WSCALE, 0.5 / WSCALE, ALU.mult, ALU.add)
                    nc.vector.tensor_scalar(row[:, :, W_HI], th[:], -0.5 / WSCALE, 0.5 / WSCALE, ALU.mult, ALU.add)
                    dve.wait_ge(rank_psum, i)
                    nc.vector.tensor_tensor(rsel[:].rearrange("p t n -> p (t n)"), hot[:].rearrange("p t n -> p (t n)"),
                                            bank[7][:, 0:CT * NP], ALU.mult).then_inc(rank_done, 1)
                    dve.wait_ge(route, r1 + 12)
                    nc.vector.tensor_tensor(carry[:], carry[:], hsum[:], ALU.add).then_inc(carry_ready, 1)
                    dve.wait_ge(rank_done, i)
                    nc.vector.tensor_reduce(rank[:], rsel[:], AX.X, ALU.add).then_inc(rank_sum, 1)
                    dve.wait_ge(rank_sum, i)
                    nc.vector.scalar_tensor_tensor(pos[1 - par][:], pair[:], float(REGION), rank[:],
                                                   ALU.mult, ALU.add).then_inc(pos_ready, 1)

            walk(dve, step, NCH)

            k = [0]

            def link(ins):
                k[0] += 1
                ins.then_inc(plan_step, 1)
                dve.wait_ge(plan_step, k[0])

            counts = bank[7][:, 0:NP]
            dve.wait_ge(counts_psum, 1)
            nc.vector.tensor_tensor(pad_at[:], pad_base[:], counts, ALU.add).then_inc(pads_ready, 1)
            tiles, upto, first, at_or_after, tmp, ones_np = (pl[:, q, :] for q in range(6))
            p_no, p_first, used, within = pc[:, 0:1], pc[:, 1:2], pc[:, 2:3], pc[:, 3:4]
            link(nc.vector.tensor_scalar(cnt_i[:, 0, :], counts, float(P - 1), None, ALU.add))
            link(nc.vector.tensor_scalar(cnt_i[:, 1, :], cnt_i[:, 0, :], P.bit_length() - 1, None, ALU.logical_shift_right))
            link(nc.vector.tensor_scalar(tiles, cnt_i[:, 1, :], 1.0, None, ALU.max))
            link(nc.vector.tensor_tensor_scan(upto, ones_np, tiles, 0.0, ALU.mult, ALU.add))
            link(nc.vector.tensor_tensor(first, upto, tiles, ALU.subtract))
            link(nc.vector.tensor_scalar(at_or_after, first, part_no[:, 0:1], None, ALU.is_le))
            nc.vector.tensor_reduce(p_no, at_or_after, AX.X, ALU.add)
            link(nc.vector.tensor_tensor(tmp, at_or_after, first, ALU.mult))
            link(nc.vector.tensor_reduce(p_first, tmp, AX.X, ALU.max))
            link(nc.vector.tensor_scalar(p_no, p_no, -1.0, None, ALU.add))
            link(nc.vector.tensor_scalar(at_or_after, pair_no[:], p_no, None, ALU.is_equal))
            nc.vector.tensor_tensor(tiles, at_or_after, lo_tab[:], ALU.mult)
            nc.vector.tensor_tensor(used, part_no[:], upto[:, NP - 1:NP], ALU.is_lt)
            nc.vector.tensor_tensor(within, part_no[:], p_first, ALU.subtract)
            link(nc.vector.tensor_tensor(tmp, at_or_after, hi_tab[:], ALU.mult))
            nc.vector.tensor_reduce(plan_f[:, 0:1], tiles, AX.X, ALU.add)
            nc.vector.tensor_reduce(plan_f[:, 1:2], tmp, AX.X, ALU.add)
            link(nc.vector.tensor_scalar(within, within, float(P), float(-SPARE), ALU.mult, ALU.add))
            link(nc.vector.scalar_tensor_tensor(within, p_no, float(REGION), within, ALU.mult, ALU.add))
            link(nc.vector.tensor_tensor(within, within, used, ALU.mult))
            link(nc.vector.tensor_scalar(plan_f[:, 2:3], within, float(SPARE), None, ALU.add))
            assert k[0] == PLAN
            dve.wait_ge(plan_psum, 1)
            nc.vector.tensor_copy(plan[:], bank[6][0:3, 0:P]).then_inc(plan_ready, 1)

            def tile(j, half, par, quarter, slot):
                jj = known(j, 0)
                here = jj is None or jj < NS
                prev = jj is None or 1 <= jj <= NS

                def low_x(j, par):
                    dve.wait_ge(xhi_ready, j + 1)
                    nc.vector.tensor_tensor(x_lo[par][:], bank[0][:, 0:P], x_hi[par][:], ALU.subtract).then_inc(xlo_ready, 1)

                def low_h(k):
                    dve.wait_ge(hhi_ready[k], j + 1)
                    after(dve, down_psum[k], j - 1)
                    nc.vector.tensor_tensor(h_lo[par][k][:], h_f[k][:], h_hi[par][k][:], ALU.subtract).then_inc(hlo_ready[k], 1)

                if jj == 0:
                    low_x(0, 0)
                if jj is None or jj < NS - 1:
                    after(dve, up_psum[1], j)
                    low_x(j + 1, 1 - par)
                if here:
                    low_h(0)
                row, both = srow[(slot - 1) % RB], cat[1 - par]
                if prev:
                    dve.wait_ge(down_psum[0], j)
                    nc.vector.tensor_scalar(y_lo[:], bank[3][:, 0:P], row[:, W_LO:W_LO + 1], None, ALU.mult).then_inc(ylo_done, 1)
                    dve.wait_ge(ylo_done, j)
                    dve.wait_ge(down_psum[1], j)
                    nc.vector.scalar_tensor_tensor(both[:, P:2 * P], bank[4][:, 0:P], row[:, W_HI:W_HI + 1], y_lo[:],
                                                   ALU.mult, ALU.add).then_inc(nonabel_ready, 1)
                    dve.wait_ge(nonabel_ready, j)
                    dve.wait_ge(abel_ready, j)
                    nc.vector.tensor_tensor_reduce(prod[:], both[:], mix_b_all[:, 0:2 * P], 1.0, 0.0,
                                                   ALU.mult, ALU.add, dot[:]).then_inc(dot_ready, 1)
                if here:
                    low_h(1)
                if prev:
                    dve.wait_ge(tg_ready, j)
                    nc.vector.tensor_scalar(gate[:], tg[:], 0.5, 0.5, ALU.mult, ALU.add).then_inc(gate_done, 1)
                    after(dve, stored[1 - par], 16 * (half - 1 + par))
                    nc.vector.tensor_copy(tok_i[1 - par][:], row[:, TOKEN:TOKEN + 1])
                    dve.wait_ge(gate_done, j)
                    dve.wait_ge(diff_ready, j)
                    nc.vector.scalar_tensor_tensor(part[:], diff[:], gate[:, 0:1], both[:, 0:P],
                                                   ALU.mult, ALU.add).then_inc(part_done, 1)
                    dve.wait_ge(part_done, j)
                    dve.wait_ge(base_ready, j)
                    nc.vector.tensor_tensor(fin[1 - par][:], part[:], base[1 - par][:], ALU.add).then_inc(fin_ready, 1)

            walk(dve, tile, NS, RB)


NAMES = ["L0_attn_x", "L0_attn_Wz", "L0_attn_bz", "L0_attn_Wh", "L0_attn_bh", "L0_ffn_ln_g", "L0_ffn_ln_b",
         "L0_ffn_abel_w", "L0_ffn_abel_b", "L0_ffn_gate_w_moe", "L0_ffn_gate_b_moe", "L0_ffn_w1", "L0_ffn_b1",
         "L0_ffn_w2", "L0_ffn_b2", "L0_ffn_gens", "L0_ffn_mix_w", "L0_ffn_mix_b"]


def kernel(**inputs):
    import numpy as np
    import concourse.bacc as bacc
    from concourse.bass_utils import run_bass_kernel_spmd

    nc = bacc.Bacc("TRN2", target_bir_lowering=False, num_devices=1)
    arrays, args = {}, []
    for name in NAMES:
        a = np.ascontiguousarray(inputs[name])
        arrays[f"in_{name}"] = a
        args.append(nc.dram_tensor(f"in_{name}", a.shape, mybir.dt.from_np(a.dtype), kind="ExternalInput").ap())
    shape = inputs["L0_attn_x"].shape
    args.append(nc.dram_tensor("result", shape, F32, kind="ExternalOutput").ap())
    gru_moe_block(nc, *args)
    r = run_bass_kernel_spmd(nc, [arrays], core_ids=[0])
    return r.results[0]["result"]
```

```python
from contextlib import ExitStack

import concourse.bass as bass
from concourse import mybir

F32 = mybir.dt.float32
F16 = mybir.dt.float16
BF16 = mybir.dt.bfloat16
I32 = mybir.dt.int32
U32 = mybir.dt.uint32
ALU = mybir.AluOpType
ACT = mybir.ActivationFunctionType
AX = mybir.AxisListType

P = 128
EPS = 1e-5
A_GUARD = 1e-8
WSCALE = 256.0
MAGIC = float(0x5F3759DF)
SQUARINGS = 6


def gru_moe_block(nc, x, wz, bz, wh, bh, ln_g, ln_b, abel_w, abel_b, gate_w, gate_b,
                  w1, b1, w2, b2, gens, mix_w, mix_b, out):
    B, T, D = x.shape
    E, _, DF = w1.shape
    NROT = gens.shape[0]
    assert D == P and T % P == 0 and DF % P == 0
    TOK = B * T
    NT = TOK // P
    CT = 4
    NCH = NT // CT
    CW = CT * P
    BPC = CW // T
    FB = DF // P
    NP = E * (E - 1) // 2
    REGION = TOK + P
    SPARE = NP * REGION
    NS = NT + NP
    ROW = P + 5
    W_LO, W_HI, SCALE_R, MEAN_R, TOKEN = P, P + 1, P + 2, P + 3, P + 4
    NX = 4
    RB = 4
    NG = NS // RB
    XT = NT // NX
    assert NS <= P and NCH % RB == 0 and NS % RB == 0
    PAIRS = [(a, b) for a in range(E) for b in range(a + 1, E)]

    x_tiles = x.rearrange("b t d -> (b t) d").rearrange("(n p) d -> p n d", p=P)
    out_rows = out.rearrange("b t d -> (b t) d")
    slots = nc.dram_tensor("slots", [SPARE + P, ROW], F32).ap()

    ctx = ExitStack()
    with ctx:
        def sb(name, shape, dt=F32):
            return ctx.enter_context(nc.sbuf_tensor(name, shape, dt))

        def sem(name):
            return ctx.enter_context(nc.semaphore(name))

        bank = [ctx.enter_context(nc.psum_tensor(f"bank{i}", [P, 512], F32)) for i in range(8)]

        ident = sb("ident", [P, P])
        ident2 = sb("ident2", [P, P])
        tri = sb("tri", [P, P], BF16)
        ones_b = sb("ones_b", [P, P], BF16)
        ones_f = sb("ones_f", [1, P])
        ones_h = sb("ones_h", [2, P], F16)
        pair_no = sb("pair_no", [P, NP])
        pad_base = sb("pad_base", [P, NP])
        lo_tab = sb("lo_tab", [P, NP])
        hi_tab = sb("hi_tab", [P, NP])
        part_no = sb("part_no", [P, 1])
        tok_no = sb("tok_no", [P, NT])
        row_sel = sb("row_sel", [2, 2])
        zero_row = sb("zero_row", [P, ROW])
        x_all = sb("x_all", [P, NT, P])
        wz_n = sb("wz_n", [P, P])
        wh_n = sb("wh_n", [P, P])
        bz_c = sb("bz_c", [P, 1])
        bh_c = sb("bh_c", [P, 1])
        g_c = sb("g_c", [P, 1])
        beta_c = sb("beta_c", [P, 2])
        aw_n = sb("aw_n", [P, P])
        ab_r = sb("ab_r", [1, P])
        gw_n = sb("gw_n", [P, E])
        gb_r = sb("gb_r", [1, E])
        w1_n = sb("w1_n", [P, E, DF])
        b1_n = sb("b1_n", [E * FB, P])
        w2_n = sb("w2_n", [P, E * FB, P])
        b2_n = sb("b2_n", [E, P])
        mix_r = sb("mix_r", [1, 2 * P + 1])
        wzh_t = sb("wzh_t", [P, 2, P])
        nbz = sb("nbz", [P, 1])
        g256 = sb("g256", [P, 1])
        gw = sb("gw", [P, E])
        gb_all = sb("gb_all", [P, E])
        beta_all = sb("beta_all", [P, P])
        aw_hi = sb("aw_hi", [P, P], F16)
        aw_lo = sb("aw_lo", [P, P], F16)
        ab_hl = sb("ab_hl", [2, P], F16)
        ab_s = sb("ab_s", [2, P])
        ab_h = sb("ab_h", [2, P], F16)
        ab_l = sb("ab_l", [2, P])
        w1_hi = sb("w1_hi", [P, E, DF], F16)
        w1_lo = sb("w1_lo", [P, E, DF], F16)
        b1_t = sb("b1_t", [P, E * FB])
        b1_s = sb("b1_s", [P, E * FB])
        w2_t = [sb(f"w2_t{i}", [P, DF]) for i in range(2)]
        w2_f = [sb(f"w2_f{i}", [P, FB, P]) for i in range(2)]
        w2_hi = sb("w2_hi", [P, E * FB, P], F16)
        w2_lo = sb("w2_lo", [P, E * FB, P], F16)
        b2_t = sb("b2_t", [P, E, 2])
        b2_s = sb("b2_s", [2, E * P])
        b2_h = sb("b2_h", [2, E * P], F16)
        b2_l = sb("b2_l", [2, E * P])
        b2_hl = sb("b2_hl", [2, E * P], F16)
        mix_b_all = sb("mix_b_all", [P, 2 * P + 1])
        mixb_h = sb("mixb_h", [P, 1])
        RG = NROT * P
        a_1 = sb("a_1", [P, RG])
        a_1t = sb("a_1t", [P, RG])
        a_2 = sb("a_2", [P, RG])
        a_2t = sb("a_2t", [P, RG])
        a_3 = sb("a_3", [P, RG])
        a_4t = sb("a_4t", [P, RG])
        q_s = sb("q_s", [P, RG])
        p_s = sb("p_s", [P, RG])
        em = [sb(f"em{i}", [P, RG]) for i in range(2)]
        emt = [sb(f"emt{i}", [P, RG]) for i in range(2)]
        f_s = sb("f_s", [P, 2, P])
        rot = sb("rot", [P, P])
        st0 = sb("st0", [P, NT, 6])
        mv0 = sb("mv0", [P, NT, 2])
        nw0 = sb("nw0", [P, 4, NT])
        shift0 = sb("shift0", [P, NT])
        xn = [sb(f"xn{i}", [P, CT, P]) for i in range(2)]
        x_t = sb("x_t", [P, CW])
        tneg = sb("tneg", [P, CW])
        hcand = sb("hcand", [P, CW])
        omz = sb("omz", [P, CW])
        acoef = sb("acoef", [P, CW])
        bneg = sb("bneg", [P, CW])
        hseq = [sb(f"hseq{i}", [P, CW]) for i in range(2)]
        st1 = sb("st1", [P, CT, 6])
        mv1 = sb("mv1", [P, CT, 2])
        nw1 = sb("nw1", [P, 4, 2 * CT])
        sy = sb("sy", [P, CT])
        h_row = sb("h_row", [P, CW])
        x1 = sb("x1", [P, CT, P])
        rows = [sb(f"rows{i}", [P, CT, ROW]) for i in range(RB)]
        y2_t = sb("y2_t", [P, CW])
        lg = sb("lg", [P, CT, E])
        mx = sb("mx", [P, CT, 8])
        mi = sb("mi", [P, CT, 8], U32)
        idx = sb("idx", [P, CT, 2])
        gap = sb("gap", [P, CT])
        elo = sb("elo", [P, CT])
        ehi = sb("ehi", [P, CT])
        sgn = sb("sgn", [P, CT])
        gaps = sb("gaps", [P, CT])
        th = sb("th", [P, CT])
        pr1 = sb("pr1", [P, CT])
        pair = sb("pair", [P, CT])
        hot = sb("hot", [P, CT, NP], BF16)
        hsum = sb("hsum", [P, NP])
        carry = sb("carry", [P, NP], BF16)
        rsel = sb("rsel", [P, CT, NP])
        rank = sb("rank", [P, CT])
        pos = [sb(f"pos{i}", [P, CT], I32) for i in range(RB)]
        pad_at = sb("pad_at", [P, NP], I32)
        cnt_i = sb("cnt_i", [P, 2, NP], I32)
        pl = sb("pl", [P, 6, NP])
        pc = sb("pc", [P, 8])
        plan_f = sb("plan_f", [P, 3])
        plan_e = sb("plan_e", [1, NG + 1, 2 * (RB + 1) + 2], I32)
        plan_row = sb("plan_row", [1, P], I32)
        srow = [sb(f"srow{i}", [P, ROW]) for i in range(RB)]
        x_hi = [sb(f"x_hi{i}", [P, P], F16) for i in range(2)]
        x_lo = [sb(f"x_lo{i}", [P, P], F16) for i in range(2)]
        h_f = [sb(f"h_f{k}", [P, DF]) for k in range(2)]
        h_hi = [[sb(f"h_hi{k}{i}", [P, DF], F16) for i in range(2)] for k in range(2)]
        h_lo = [[sb(f"h_lo{k}{i}", [P, DF], F16) for i in range(2)] for k in range(2)]
        cat = [x_all[:, 2 * i:2 * i + 2, :].rearrange("p a d -> p (a d)") for i in range(2)]
        prod = x_all[:, 4:6, :].rearrange("p a d -> p (a d)")
        y_lo, diff, part = (x_all[:, i, :] for i in range(6, 9))
        base = [x_all[:, i, :] for i in range(9, 11)]
        fin = [x_all[:, i, :] for i in range(11, 13)]
        dot = [sb(f"dot{i}", [P, 1]) for i in range(2)]
        tg = sb("tg", [P, 1])
        gate = sb("gate", [P, 1])
        tok_i = [sb(f"tok_i{i}", [P, 1], I32) for i in range(2)]

        attn_in = sem("attn_in")
        small_in = sem("small_in")
        gens_in = sem("gens_in")
        w1_in = sem("w1_in")
        w2_in = sem("w2_in")
        x_in = [sem(f"x_in{i}") for i in range(NX)]
        spare_in = sem("spare_in")
        consts = sem("consts")
        prep_pe = sem("prep_pe")
        prep_act = sem("prep_act")
        prep_dve = sem("prep_dve")
        w1_hi_done = sem("w1_hi_done")
        w1_ready = sem("w1_ready")
        w2t_psum = sem("w2t_psum")
        w2t_copied = sem("w2t_copied")
        w2r_psum = sem("w2r_psum")
        w2r_copied = sem("w2r_copied")
        w2_hi_done = sem("w2_hi_done")
        w2_ready = sem("w2_ready")
        bt_psum = sem("bt_psum")
        bt_copied = sem("bt_copied")
        bias_psum = sem("bias_psum")
        bias_copied = sem("bias_copied")
        bias_step = sem("bias_step")
        xn_ready = sem("xn_ready")
        xt_psum = sem("xt_psum")
        xt_ready = sem("xt_ready")
        u_psum = sem("u_psum")
        v_psum = sem("v_psum")
        tneg_ready = sem("tneg_ready")
        hcand_ready = sem("hcand_ready")
        omz_done = sem("omz_done")
        ab_done = sem("ab_done")
        scan_done = sem("scan_done")
        h_psum = sem("h_psum")
        h_copied = sem("h_copied")
        x1_ready = sem("x1_ready")
        st1_done = sem("st1_done")
        mv1_done = sem("mv1_done")
        newton = sem("newton")
        y2_ready = sem("y2_ready")
        y2t_psum = sem("y2t_psum")
        y2t_ready = sem("y2t_ready")
        lg_psum = sem("lg_psum")
        lg_copied = sem("lg_copied")
        sy_done = sem("sy_done")
        route = sem("route")
        gap_ready = sem("gap_ready")
        th_ready = sem("th_ready")
        hot_ready = sem("hot_ready")
        carry_ready = sem("carry_ready")
        rank_psum = sem("rank_psum")
        rank_done = sem("rank_done")
        rank_sum = sem("rank_sum")
        stat0 = sem("stat0")
        pos_ready = sem("pos_ready")
        scattered = [sem(f"scattered{i}") for i in range(RB)]
        pads_in = sem("pads_in")
        counts_psum = sem("counts_psum")
        pads_ready = sem("pads_ready")
        plan_step = sem("plan_step")
        plan_psum = sem("plan_psum")
        plan_ready = sem("plan_ready")
        row_in = [sem(f"row_in{i}") for i in range(RB)]
        x_psum = sem("x_psum")
        xhi_ready = sem("xhi_ready")
        xlo_ready = sem("xlo_ready")
        up_psum = [sem(f"up_psum{k}") for k in range(2)]
        h_ready = [sem(f"h_ready{k}") for k in range(2)]
        hhi_done = [sem(f"hhi_done{k}") for k in range(2)]
        hlo_ready = [sem(f"hlo_ready{k}") for k in range(2)]
        down_psum = [sem(f"down_psum{k}") for k in range(2)]
        abel_psum = sem("abel_psum")
        abel_ready = sem("abel_ready")
        ylo_done = sem("ylo_done")
        nonabel_ready = sem("nonabel_ready")
        dot_ready = sem("dot_ready")
        tg_ready = sem("tg_ready")
        diff_ready = sem("diff_ready")
        base_ready = sem("base_ready")
        part_done = sem("part_done")
        gate_done = sem("gate_done")
        fin_ready = sem("fin_ready")
        tok_ready = sem("tok_ready")
        stored = [sem(f"stored{i}") for i in range(2)]

        block = ctx.enter_context(nc.Block())

        def after(eng, s, n):
            if not isinstance(n, int) or n > 0:
                eng.wait_ge(s, n)

        def wait_apart(eng, *waits):
            waits = [(s, n if isinstance(n, int) else eng.to_reg(n)) for s, n in waits]
            eng.wait_ge(consts, CONSTS)
            for s, n in waits:
                after(eng, s, n)

        def walk(eng, step, n, width=2):
            for j in range(width):
                step(j, j // 2, j % 2, 0, j)
            with eng.Fori(1, n // width - 1) as i:
                for k in range(width):
                    step(width * i + k, width // 2 * i + k // 2, k % 2, i, k)
            for j in range(n - width, n + 2):
                step(j, j // 2, j % 2, j // width, j % width)

        def load_experts(eng, table, group):
            table.clear()
            _, v = nc.values_load_multi_w_load_instructions(
                plan_e[:, bass.ds(group, 1), :].rearrange("p a n -> p (a n)"), engines=[eng], min_val=0, max_val=E - 1,
                skip_runtime_bounds_check_because="the plan's experts come from lo_tab and hi_tab")
            for k in range(-1, RB):
                table[k] = (v[k + 1], v[k + 2 + RB])

        def known(j, n):
            return j if isinstance(j, int) else None

        NEWTON = 11

        def rsqrt(dve, tab, s, base_count, first_src_done):
            v, y, t, u = (tab[:, k, :] for k in range(4))
            n = [0]

            def link(ins):
                n[0] += 1
                ins.then_inc(s, 1)
                return n[0]

            def wait():
                dve.wait_ge(s, base_count + n[0])

            first_src_done()
            link(nc.vector.tensor_scalar(t.bitcast(I32), v.bitcast(I32), 1, None, ALU.logical_shift_right))
            wait()
            link(nc.vector.tensor_scalar(y.bitcast(I32), t.bitcast(I32), -1.0, MAGIC, ALU.mult, ALU.add))
            for _ in range(3):
                wait()
                link(nc.vector.tensor_tensor(t, y, y, ALU.mult))
                wait()
                link(nc.vector.scalar_tensor_tensor(u, t, -0.5, v, ALU.mult, ALU.mult))
                wait()
                link(nc.vector.scalar_tensor_tensor(y, u, 1.5, y, ALU.add, ALU.mult))
            assert n[0] == NEWTON

        STAT0 = 2 * NX + 1 + NEWTON + 1
        BIAS = 9
        NEWTON1 = NEWTON + 2
        ROUTE = 11
        CONSTS = 19 + 2 * NP
        ACT_PREP = 13 + 2 * SQUARINGS
        PE_PREP = 9 + SQUARINGS
        DVE_PREP = 8
        PLAN = 15

        @block.sync
        def _(sp):
            for dst, src in ((wz_n[:], wz), (wh_n[:], wh), (bz_c[:], bz.rearrange("(p a) -> p a", a=1)),
                             (bh_c[:], bh.rearrange("(p a) -> p a", a=1))):
                sp.dma_start(dst, src).then_inc(attn_in, 16)
            sp.dma_start(a_1[:].rearrange("p (g d) -> p g d", g=NROT), gens.rearrange("g p d -> p g d")).then_inc(gens_in, 16)
            for c in range(NX):
                sp.dma_start(x_all[:, c * XT:(c + 1) * XT, :], x_tiles[:, c * XT:(c + 1) * XT, :]).then_inc(x_in[c], 16)
            for dst, src in (
                (g_c[:], ln_g.rearrange("(p a) -> p a", a=1)),
                (beta_c[:, 0:1], ln_b.rearrange("(p a) -> p a", a=1)),
                (beta_c[:, 1:2], ln_b.rearrange("(p a) -> p a", a=1)),
                (aw_n[:], abel_w), (ab_r[:], abel_b.rearrange("(a n) -> a n", a=1)),
                (gw_n[:], gate_w), (gb_r[:], gate_b.rearrange("(a n) -> a n", a=1)),
                (b1_n[:], b1.rearrange("e (f p) -> (e f) p", p=P)), (b2_n[:], b2),
                (mix_r[:, 0:2 * P], mix_w.rearrange("n a -> a n")),
                (mix_r[:, 2 * P:2 * P + 1], mix_b.rearrange("(a n) -> a n", a=1)),
            ):
                sp.dma_start(dst, src).then_inc(small_in, 16)
            sp.dma_start(w1_n[:], w1.rearrange("e d f -> d e f")).then_inc(w1_in, 16)
            sp.dma_start(w2_n[:].rearrange("p (e f) d -> p e f d", e=E),
                         w2.rearrange("e (f p) d -> p e f d", p=P)).then_inc(w2_in, 16)
            sp.wait_ge(consts, CONSTS)
            sp.dma_start(slots[SPARE:SPARE + P, :], zero_row[:]).then_inc(spare_in, 16)
            sp.wait_ge(spare_in, 16)
            sp.wait_ge(plan_ready, 1)
            for s in scattered:
                sp.wait_ge(s, 16 * CT * NCH // RB)
            sp.wait_ge(pads_in, 16 * NP)

            def step(j, half, par, quarter, slot):
                if known(j, 0) is not None and j >= NS:
                    return
                at = sp.value_load(plan_row[:, bass.ds(j, 1)], min_val=0, max_val=SPARE)
                after(sp, tok_ready, j - RB + 1)
                sp.dma_start(srow[slot][:], slots[bass.ds(at, P), :]).then_inc(row_in[slot], 16)

            walk(sp, step, NS, RB)

        @block.gpsimd
        def _(pool):
            n = [0]

            def done(ins):
                n[0] += 1
                ins.then_inc(consts, 1)

            done(pool.memset(ident[:], 0.0))
            done(pool.memset(ident2[:], 0.0))
            done(pool.memset(tri[:], 1.0))
            done(pool.memset(ones_b[:], 1.0))
            done(pool.memset(ones_f[:], 1.0))
            done(pool.memset(ones_h[:], 1.0))
            done(pool.memset(row_sel[:], 0.0))
            done(pool.memset(zero_row[:], 0.0))
            done(pool.memset(pl[:, 5, :], 1.0))
            done(pool.memset(carry[:], 0.0))
            pool.wait_ge(consts, n[0])
            done(pool.memset(zero_row[:, TOKEN:TOKEN + 1], float(TOK)))
            done(pool.affine_select(out=ident[:], in_=ident[:], compare_op=ALU.not_equal, fill=1.0,
                                    base=0, pattern=[[-1, P]], channel_multiplier=1))
            done(pool.affine_select(out=ident2[:], in_=ident2[:], compare_op=ALU.not_equal, fill=2.0,
                                    base=0, pattern=[[-1, P]], channel_multiplier=1))
            done(pool.affine_select(out=tri[:], in_=tri[:], compare_op=ALU.is_gt, fill=0.0,
                                    base=0, pattern=[[1, P]], channel_multiplier=-1))
            done(pool.affine_select(out=row_sel[:], in_=row_sel[:], compare_op=ALU.not_equal, fill=1.0,
                                    base=0, pattern=[[-1, 2]], channel_multiplier=1))
            exact = dict(allow_small_or_imprecise_dtypes=True)
            done(pool.iota(pair_no[:], pattern=[[1, NP]], base=0, channel_multiplier=0, **exact))
            done(pool.iota(pad_base[:], pattern=[[REGION, NP]], base=0, channel_multiplier=1, **exact))
            done(pool.iota(part_no[:], pattern=[[0, 1]], base=0, channel_multiplier=1, **exact))
            done(pool.iota(tok_no[:], pattern=[[P, NT]], base=0, channel_multiplier=1, **exact))
            for k, (a, b) in enumerate(PAIRS):
                done(pool.memset(lo_tab[:, k:k + 1], float(a)))
                done(pool.memset(hi_tab[:, k:k + 1], float(b)))
            assert n[0] == CONSTS

            def step(i, half, par, quarter, slot):
                ii = known(i, 0)
                if ii is None or ii < NCH:
                    pool.wait_ge(h_copied, i + 1)
                    after(pool, y2_ready, i)
                    pool.tensor_tensor(x1[:].rearrange("p t d -> p (t d)"), h_row[:],
                                       x_all[:, bass.ds(i * CT, CT), :].rearrange("p t d -> p (t d)"),
                                       ALU.add).then_inc(x1_ready, 1)
                if ii is None or ii >= 2:
                    wait_apart(pool, (pos_ready, i - 1))
                    s = (slot - 2) % RB
                    for t in range(CT):
                        pool.indirect_dma_start(
                            out=slots, out_offset=bass.IndirectOffsetOnAxis(ap=pos[s][:, t:t + 1], axis=0),
                            in_=rows[s][:, t, :], in_offset=None).then_inc(scattered[s], 16)

            walk(pool, step, NCH, RB)
            pool.wait_ge(pads_ready, 1)
            for k in range(NP):
                pool.indirect_dma_start(
                    out=slots, out_offset=bass.IndirectOffsetOnAxis(ap=pad_at[:, k:k + 1], axis=0),
                    in_=zero_row[:], in_offset=None).then_inc(pads_in, 16)

            def tile(j, half, par, quarter, slot):
                jj = known(j, 0)
                if jj is None or jj >= 2:
                    after(pool, stored[par], 16 * (half - 1))
                    pool.wait_ge(part_done, j - 1)
                    pool.wait_ge(base_ready, j - 1)
                    pool.tensor_tensor(fin[par][:], part, base[par][:], ALU.add).then_inc(fin_ready, 1)
                    wait_apart(pool, (fin_ready, j - 1))
                    pool.tensor_copy(tok_i[par][:], srow[(slot - 2) % RB][:, TOKEN:TOKEN + 1]).then_inc(tok_ready, 1)
                    wait_apart(pool, (tok_ready, j - 1))
                    pool.indirect_dma_start(
                        out=out_rows, out_offset=bass.IndirectOffsetOnAxis(ap=tok_i[par][:, 0:1], axis=0),
                        in_=fin[par][:], in_offset=None, bounds_check=TOK - 1, oob_is_err=False,
                    ).then_inc(stored[par], 16)
                if jj is None or 1 <= jj <= NS:
                    pool.wait_ge(dot_ready, j)
                    after(pool, part_done, j - 1)
                    pool.tensor_tensor(diff, cat[1 - par][:, P:2 * P], cat[1 - par][:, 0:P],
                                       ALU.subtract).then_inc(diff_ready, 1)

            walk(pool, tile, NS, RB)
            for s in stored:
                pool.wait_ge(s, 16 * NS // 2)

        @block.scalar
        def _(act):
            n = [0]

            def done(ins):
                n[0] += 1
                ins.then_inc(prep_act, 1)

            act.wait_ge(attn_in, 64)
            done(act.activation(nbz[:], bz_c[:], ACT.Gelu))
            act.wait_ge(prep_act, 1)
            done(act.mul(nbz[:], bz_c[:], -0.5))
            act.wait_ge(prep_pe, 1)
            done(act.copy(wzh_t[:].rearrange("p a b -> p (a b)"), bank[0][:, 0:2 * P]))
            act.wait_ge(prep_pe, 2)
            done(act.copy(a_1t[:], bank[1][:, 0:RG]))
            act.wait_ge(prep_pe, 3)
            done(act.copy(a_2[:], bank[1][:, 0:RG]))
            done(act.copy(a_2t[:], bank[2][:, 0:RG]))
            act.wait_ge(prep_pe, 4)
            done(act.copy(a_3[:], bank[3][:, 0:RG]))
            done(act.mul(a_4t[:], bank[4][:, 0:RG], 1.0 / 24.0))
            act.wait_ge(prep_pe, 5)
            done(act.copy(em[0][:], bank[1][:, 0:RG]))
            act.wait_ge(prep_pe, 6)
            done(act.copy(emt[0][:], bank[2][:, 0:RG]))
            for k in range(SQUARINGS):
                act.wait_ge(prep_pe, 7 + k)
                done(act.copy(em[(k + 1) % 2][:], bank[1][:, 0:RG]))
                done(act.copy(emt[(k + 1) % 2][:], bank[2][:, 0:RG]))
            act.wait_ge(prep_pe, 7 + SQUARINGS)
            done(act.copy(f_s[:].rearrange("p a b -> p (a b)"), bank[1][:, 0:2 * P]))
            act.wait_ge(prep_pe, 8 + SQUARINGS)
            done(act.copy(rot[:], bank[2][:, 0:P]))
            assert n[0] == 12 + 2 * SQUARINGS
            act.wait_ge(prep_pe, PE_PREP)
            done(act.copy(gb_all[:], bank[7][:, 0:E]))
            assert n[0] == ACT_PREP
            act.wait_ge(stat0, STAT0)

            def normalize(i, par):
                after(act, xt_psum, i - 1)
                for t in range(CT):
                    c = i * CT + t
                    ins = act.activation(xn[par][:, t, :], x_all[:, bass.ds(c, 1), :].rearrange("p a d -> p (a d)"),
                                         ACT.Identity, bias=shift0[:, bass.ds(c, 1)], scale=nw0[:, 1, bass.ds(c, 1)])
                ins.then_inc(xn_ready, 1)

            normalize(0, 0)

            def step(i, half, par, quarter, slot):
                ii = known(i, 0)
                if ii is None or ii < NCH:
                    act.wait_ge(xt_psum, i + 1)
                    after(act, v_psum, i)
                    act.copy(x_t[:], bank[0][:]).then_inc(xt_ready, 1)
                    act.wait_ge(u_psum, i + 1)
                    after(act, ab_done, 2 * i)
                    act.activation(tneg[:], bank[1][:], ACT.Tanh, bias=nbz[:], scale=-0.5).then_inc(tneg_ready, 1)
                    act.wait_ge(v_psum, i + 1)
                    act.activation(hcand[:], bank[2][:], ACT.Identity, bias=bh_c[:]).then_inc(hcand_ready, 1)
                if ii is None or ii < NCH - 1:
                    normalize(i + 1, 1 - par)
                if ii is None or ii >= 2:
                    act.wait_ge(gap_ready, i - 1)
                    after(act, pos_ready, i - 2)
                    act.activation(th[:], gaps[:], ACT.Tanh).then_inc(th_ready, 1)
                if ii is None or 1 <= ii <= NCH:
                    act.wait_ge(y2t_psum, i)
                    after(act, lg_psum, i - 1)
                    act.copy(y2_t[:], bank[4][:]).then_inc(y2t_ready, 1)
                if ii is None or ii < NCH:
                    act.wait_ge(h_psum, i + 1)
                    after(act, x1_ready, i)
                    act.copy(h_row[:], bank[3][:]).then_inc(h_copied, 1)

            walk(act, step, NCH, RB)

            act.wait_ge(bt_psum, 1)
            act.copy(b1_t[:], bank[5][:, 0:E * FB])
            for k in range(2):
                ins = act.copy(b2_t[:, :, k], bank[5][:, 64:64 + E])
            ins.then_inc(bt_copied, 1)
            act.wait_ge(bias_psum, 1)
            act.mul(ab_s[:], bank[5][0:2, 0:P], WSCALE)
            for k in range(2):
                act.mul(b2_s[:, k * 512:(k + 1) * 512], bank[6 + k][0:2, :], WSCALE)
            act.copy(mix_b_all[:], bank[2][:, 0:2 * P + 1]).then_inc(bias_copied, 1)
            act.wait_ge(bias_copied, 1)
            act.mul(mixb_h[:], mix_b_all[:, 2 * P:2 * P + 1], 0.5).then_inc(bias_copied, 1)
            act.wait_ge(bias_copied, 2)
            for e in range(E):
                act.wait_ge(w2t_psum, e + 1)
                if e >= 2:
                    act.wait_ge(w2r_psum, e - 1)
                act.copy(w2_t[e % 2][:], bank[(3, 0)[e % 2]][:]).then_inc(w2t_copied, 1)
                act.wait_ge(w2r_psum, e + 1)
                if e >= 2:
                    act.wait_ge(w2_ready, e - 1)
                act.mul(w2_f[e % 2][:].rearrange("p a b -> p (a b)"), bank[(4, 1)[e % 2]][:],
                        WSCALE).then_inc(w2r_copied, 1)
            act.wait_ge(bias_step, BIAS)
            act.wait_ge(plan_ready, 1)

            experts = {}

            def tile(j, half, par, quarter, slot):
                jj = known(j, 0)
                if slot == 0 and (jj is None or jj < NS):
                    load_experts(mybir.EngineType.Activation, experts, quarter)

                def up(k):
                    e = experts[slot][k]
                    act.wait_ge(up_psum[k], j + 1)
                    after(act, hlo_ready[k], j)
                    h = h_f[k]
                    for f in range(FB):
                        ins = act.activation(h[:, f * P:(f + 1) * P], bank[1 + k][:, f * P:(f + 1) * P],
                                             ACT.Gelu, bias=b1_s[:, bass.ds(e * FB + f, 1)], scale=1.0 / WSCALE)
                    ins.then_inc(h_ready[k], 1)

                if jj == 0:
                    act.wait_ge(x_psum, 1)
                    act.copy(x_hi[0][:], bank[0][:, 0:P]).then_inc(xhi_ready, 1)
                if jj is None or jj < NS:
                    up(0)
                if jj is None or jj >= 2:
                    act.wait_ge(dot_ready, j - 1)
                    act.activation(tg[:], dot[par][:], ACT.Tanh, bias=mixb_h[:], scale=0.5).then_inc(tg_ready, 1)
                if jj is None or jj < NS - 1:
                    act.wait_ge(x_psum, j + 2)
                    after(act, up_psum[1], j)
                    act.copy(x_hi[1 - par][:], bank[0][:, 0:P]).then_inc(xhi_ready, 1)
                if jj is None or jj < NS:
                    up(1)
                    act.wait_ge(abel_psum, j + 1)
                    after(act, part_done, j - 1)
                    act.activation(cat[par][:, 0:P], bank[5][:, 0:P], ACT.Gelu, scale=1.0 / WSCALE)\
                       .then_inc(abel_ready, 1)
                    after(act, fin_ready, j - 1)
                    act.activation(base[par][:], srow[slot][:, 0:P], ACT.Identity,
                                   bias=srow[slot][:, MEAN_R:MEAN_R + 1],
                                   scale=srow[slot][:, SCALE_R:SCALE_R + 1]).then_inc(base_ready, 1)

            walk(act, tile, NS, RB)

        @block.tensor
        def _(pe):
            n = [0]

            def done(ins):
                n[0] += 1
                ins.then_inc(prep_pe, 1)

            def mm(o, lhs, rhs, start=True, stop=True):
                return pe.matmul(o, lhs, rhs, start=start, stop=stop)

            def g(t, k):
                return t[:, k * P:(k + 1) * P]

            pe.wait_ge(consts, CONSTS)
            pe.wait_ge(attn_in, 64)
            pe.transpose(bank[0][:, 0:P], wz_n[:], ident[:])
            done(pe.transpose(bank[0][:, P:2 * P], wh_n[:], ident[:]))
            pe.wait_ge(prep_dve, 1)
            for k in range(NROT):
                ins = pe.transpose(g(bank[1], k), g(a_1, k), ident[:])
            done(ins)
            pe.wait_ge(prep_act, 4)
            for k in range(NROT):
                mm(g(bank[1], k), g(a_1t, k), g(a_1, k))
                ins = mm(g(bank[2], k), g(a_1, k), g(a_1t, k))
            done(ins)
            pe.wait_ge(prep_act, 6)
            for k in range(NROT):
                mm(g(bank[3], k), g(a_1t, k), g(a_2, k))
                ins = mm(g(bank[4], k), g(a_2, k), g(a_2t, k))
            done(ins)
            pe.wait_ge(prep_act, 8)
            pe.wait_ge(prep_dve, 6)
            for k in range(NROT):
                mm(g(bank[1], k), g(a_4t, k), g(q_s, k), stop=False)
                ins = mm(g(bank[1], k), ident[:], g(p_s, k), start=False)
            done(ins)
            pe.wait_ge(prep_act, 9)
            for k in range(NROT):
                ins = pe.transpose(g(bank[2], k), g(em[0], k), ident[:])
            done(ins)
            for s in range(SQUARINGS):
                pe.wait_ge(prep_act, 10 + 2 * s)
                e, et = em[s % 2], emt[s % 2]
                for k in range(NROT):
                    mm(g(bank[1], k), g(et, k), g(e, k), stop=False)
                    mm(g(bank[1], k), ident2[:], g(e, k), start=False)
                    mm(g(bank[2], k), g(e, k), g(et, k), stop=False)
                    ins = mm(g(bank[2], k), ident2[:], g(et, k), start=False)
                done(ins)
            e, et = em[SQUARINGS % 2], emt[SQUARINGS % 2]
            pe.wait_ge(prep_act, 10 + 2 * SQUARINGS)
            mm(g(bank[1], 0), g(et, 0), g(e, 1), stop=False)
            mm(g(bank[1], 0), ident[:], g(e, 0), start=False, stop=False)
            mm(g(bank[1], 0), ident[:], g(e, 1), start=False)
            mm(g(bank[1], 1), g(e, 1), g(et, 0), stop=False)
            mm(g(bank[1], 1), ident[:], g(et, 0), start=False, stop=False)
            done(mm(g(bank[1], 1), ident[:], g(et, 1), start=False))
            pe.wait_ge(prep_act, 11 + 2 * SQUARINGS)
            mm(g(bank[2], 0), f_s[:, 1, :], g(e, 2), stop=False)
            mm(g(bank[2], 0), ident[:], f_s[:, 0, :], start=False, stop=False)
            mm(g(bank[2], 0), ident[:], g(e, 2), start=False, stop=False)
            done(mm(g(bank[2], 0), ident[:], ident[:], start=False))
            pe.wait_ge(small_in, 16 * 11)
            pe.wait_ge(prep_dve, DVE_PREP)
            mm(bank[7][:, 0:E], beta_all[:], gw_n[:], stop=False)
            done(mm(bank[7][:, 0:E], ones_f[:], gb_r[:], start=False))
            assert n[0] == PE_PREP
            pe.wait_ge(prep_act, ACT_PREP)

            def step(i, half, par, quarter, slot):
                ii = known(i, 0)
                a = ii is None or ii < NCH
                b = ii is None or 1 <= ii <= NCH
                c = ii is None or ii >= 2
                if a:
                    pe.wait_ge(xn_ready, i + 1)
                    after(pe, xt_ready, i)
                    for t in range(CT):
                        ins = pe.transpose(g(bank[0], t), xn[par][:, t, :], ident[:])
                    ins.then_inc(xt_psum, 1)
                    pe.wait_ge(xt_ready, i + 1)
                    after(pe, tneg_ready, i)
                    mm(bank[1][:], wzh_t[:, 0, :], x_t[:]).then_inc(u_psum, 1)
                    after(pe, hcand_ready, i)
                    mm(bank[2][:], wzh_t[:, 1, :], x_t[:]).then_inc(v_psum, 1)
                if c:
                    pe.wait_ge(hot_ready, i - 1)
                    after(pe, carry_ready, i - 2)
                    after(pe, rank_done, i - 2)
                    r = bank[7][:, 0:CT * NP]
                    mm(r, tri[:], hot[:].rearrange("p t n -> p (t n)"), stop=False)
                    r3 = r.rearrange("p (t n) -> p t n", t=CT)
                    for t in range(CT - 1):
                        mm(r3[:, t + 1:CT, :], ones_b[:],
                           hot[:, t:t + 1, :].broadcast_to([P, CT - 1 - t, NP]), start=False, stop=False)
                    mm(r3, ones_b[:], carry[:].rearrange("p (a n) -> p a n", a=1).broadcast_to([P, CT, NP]),
                       start=False).then_inc(rank_psum, 1)
                if b:
                    pe.wait_ge(y2_ready, i)
                    after(pe, y2t_ready, i - 1)
                    for t in range(CT):
                        ins = pe.transpose(g(bank[4], t), rows[(slot - 1) % RB][:, t, 0:P], ident[:])
                    ins.then_inc(y2t_psum, 1)
                if a:
                    pe.wait_ge(scan_done, i + 1)
                    after(pe, h_copied, i)
                    for t in range(CT):
                        ins = pe.transpose(g(bank[3], t), g(hseq[par], t), ident[:])
                    ins.then_inc(h_psum, 1)
                if b:
                    pe.wait_ge(y2t_ready, i)
                    after(pe, lg_copied, i - 1)
                    for t in range(CT):
                        ins = mm(bank[6][:, t * E:(t + 1) * E], g(y2_t, t), gw[:])
                    ins.then_inc(lg_psum, 1)

            walk(pe, step, NCH, RB)
            pe.wait_ge(carry_ready, NCH)
            pe.wait_ge(rank_done, NCH)
            mm(bank[7][:, 0:NP], ones_b[:], carry[:]).then_inc(counts_psum, 1)
            pe.transpose(bank[5][:, 0:E * FB], b1_n[:], ident[0:E * FB, 0:E * FB])
            pe.transpose(bank[5][:, 64:64 + E], b2_n[:], ident[0:E, 0:E]).then_inc(bt_psum, 1)
            pe.wait_ge(plan_step, PLAN)
            for q in range(3):
                ins = pe.transpose(bank[6][0:1, q * P:(q + 1) * P], plan_f[:, q:q + 1], ident[:])
            ins.then_inc(plan_psum, 1)
            pe.wait_ge(plan_ready, 1)
            pe.wait_ge(bt_copied, 1)
            pe.wait_ge(w1_in, 16)
            for ex in range(E):
                mm(bank[6 + ex // 4][0:2, (ex % 4) * P:(ex % 4 + 1) * P], b2_t[:, ex, :], rot[:])
            for ex in range(E):
                for f in range(FB):
                    mm(bank[1][:, ex * FB + f:ex * FB + f + 1], w1_n[:, ex, f * P:(f + 1) * P], beta_c[:, 0:1])
            mm(bank[2][:, 0:2 * P + 1], ones_f[:], mix_r[:])
            mm(bank[5][0:2, 0:P], beta_c[:], aw_n[:], stop=False)
            mm(bank[5][0:2, 0:P], ones_f[:, 0:2], ab_r[:], start=False).then_inc(bias_psum, 1)
            pe.wait_ge(w2_in, 16)

            def w2_turn(ex):
                if ex >= 2:
                    pe.wait_ge(w2t_copied, ex - 1)
                for f in range(FB):
                    ins = pe.transpose(g(bank[(3, 0)[ex % 2]], f), w2_n[:, ex * FB + f, :], ident[:])
                ins.then_inc(w2t_psum, 1)

            w2_turn(0)
            pe.wait_ge(bias_step, 1)
            for ex in range(E):
                if ex + 1 < E:
                    w2_turn(ex + 1)
                pe.wait_ge(w2t_copied, ex + 1)
                if ex >= 2:
                    pe.wait_ge(w2r_copied, ex - 1)
                for f in range(FB):
                    ins = mm(g(bank[(4, 1)[ex % 2]], f), g(w2_t[ex % 2], f), rot[:])
                ins.then_inc(w2r_psum, 1)
            pe.wait_ge(w2_ready, E)
            pe.wait_ge(w1_ready, 1)
            pe.wait_ge(bias_step, BIAS)

            experts = {}

            def tile(j, half, par, quarter, slot):
                jj = known(j, 0)
                if slot == 0:
                    load_experts(mybir.EngineType.PE, experts, quarter)

                def turn(j, slot, n):
                    pe.wait_ge(row_in[slot], 16 * n)
                    after(pe, xlo_ready, j)
                    pe.transpose(bank[0][:, 0:P], srow[slot][:, 0:P], ident[:]).then_inc(x_psum, 1)

                def up(k):
                    e = experts[slot][k]
                    pe.wait_ge(xlo_ready, j + 1)
                    after(pe, h_ready[k], j)
                    for f in range(FB):
                        o = g(bank[1 + k], f)
                        hi = w1_hi[:, bass.ds(e, 1), f * P:(f + 1) * P].rearrange("p a n -> p (a n)")
                        lo = w1_lo[:, bass.ds(e, 1), f * P:(f + 1) * P].rearrange("p a n -> p (a n)")
                        mm(o, hi, x_hi[par][:], stop=False)
                        mm(o, hi, x_lo[par][:], start=False, stop=False)
                        ins = mm(o, lo, x_hi[par][:], start=False)
                    ins.then_inc(up_psum[k], 1)

                def down(k):
                    e = experts[slot - 1][k]
                    pe.wait_ge(hlo_ready[k], j)
                    after(pe, ylo_done if k == 0 else nonabel_ready, j - 1)
                    o = bank[3 + k][:, 0:P]
                    for f in range(FB):
                        at = bass.ds(e * FB + f, 1)
                        hi, lo = (w[:, at, :].rearrange("p a n -> p (a n)") for w in (w2_hi, w2_lo))
                        mm(o, g(h_hi[k][1 - par], f), hi, start=(f == 0), stop=False)
                        mm(o, g(h_hi[k][1 - par], f), lo, start=False, stop=False)
                        mm(o, g(h_lo[k][1 - par], f), hi, start=False, stop=False)
                    ins = mm(o, ones_h[:], b2_hl[:, bass.ds(e * P, P)], start=False)
                    ins.then_inc(down_psum[k], 1)

                here = jj is None or jj < NS
                prev = jj is None or 1 <= jj <= NS
                if jj == 0:
                    turn(0, 0, 1)
                if here:
                    up(0)
                    after(pe, abel_ready, j)
                    o = bank[5][:, 0:P]
                    mm(o, ones_h[:], ab_hl[:], stop=False)
                    mm(o, x_hi[par][:], aw_hi[:], start=False, stop=False)
                    mm(o, x_hi[par][:], aw_lo[:], start=False, stop=False)
                    mm(o, x_lo[par][:], aw_hi[:], start=False).then_inc(abel_psum, 1)
                if prev:
                    down(0)
                if jj is None or jj < NS - 1:
                    turn(j + 1, (slot + 1) % RB, quarter + (slot + 1) // RB + 1)
                if here:
                    up(1)
                if prev:
                    down(1)

            walk(pe, tile, NS, RB)

        @block.vector
        def _(dve):
            n = [0]

            def done(ins):
                n[0] += 1
                ins.then_inc(prep_dve, 1)

            def rows_split(dst, hi, lo, src, k):
                nc.vector.tensor_copy(hi, src).then_inc(bias_step, 1)
                dve.wait_ge(bias_step, k + 1)
                nc.vector.scalar_tensor_tensor(lo, src, 1.0, hi, ALU.mult, ALU.subtract).then_inc(bias_step, 1)
                dve.wait_ge(bias_step, k + 2)
                nc.vector.tensor_scalar(lo, lo, row_sel[:, 1:2], None, ALU.mult).then_inc(bias_step, 1)
                dve.wait_ge(bias_step, k + 3)
                nc.vector.scalar_tensor_tensor(dst, hi, row_sel[:, 0:1], lo, ALU.mult, ALU.add).then_inc(bias_step, 1)

            dve.wait_ge(gens_in, 16)
            done(nc.vector.tensor_scalar(a_1[:], a_1[:], 2.0 ** -SQUARINGS, None, ALU.mult))

            def stats(c):
                dve.wait_ge(x_in[c], 16)
                for t in range(c * XT, (c + 1) * XT):
                    ins = nc.vector.bn_stats(st0[:, t, :], x_all[:, t, :])
                ins.then_inc(stat0, 1)
                dve.wait_ge(stat0, 2 * c + 1)
                for t in range(c * XT, (c + 1) * XT):
                    ins = nc.vector.bn_aggr(mv0[:, t, :], st0[:, t, :])
                ins.then_inc(stat0, 1)

            stats(0)
            dve.wait_ge(prep_act, 8)
            dve.wait_ge(consts, CONSTS)
            def g3(t):
                return t[:].rearrange("p (g d) -> p g d", g=NROT)
            id3 = ident[:].rearrange("p (a d) -> p a d", a=1).broadcast_to([P, NROT, P])
            done(nc.vector.scalar_tensor_tensor(p_s[:], a_2[:], 0.5, a_1[:], ALU.mult, ALU.add))
            done(nc.vector.scalar_tensor_tensor(g3(q_s), g3(a_1), 1.0 / 5, id3, ALU.mult, ALU.add))
            dve.wait_ge(prep_dve, 3)
            done(nc.vector.scalar_tensor_tensor(p_s[:], a_3[:], 1.0 / 6, p_s[:], ALU.mult, ALU.add))
            done(nc.vector.scalar_tensor_tensor(q_s[:], a_2[:], 1.0 / 30, q_s[:], ALU.mult, ALU.add))
            dve.wait_ge(prep_dve, 5)
            done(nc.vector.scalar_tensor_tensor(q_s[:], a_3[:], 1.0 / 210, q_s[:], ALU.mult, ALU.add))
            for c in range(1, NX):
                stats(c)
            dve.wait_ge(stat0, 2 * NX)
            nc.vector.tensor_scalar(nw0[:, 0, :], mv0[:, :, 1], EPS, None, ALU.add).then_inc(stat0, 1)
            rsqrt(dve, nw0, stat0, 2 * NX + 1, lambda: dve.wait_ge(stat0, 2 * NX + 1))
            dve.wait_ge(stat0, STAT0 - 1)
            nc.vector.scalar_tensor_tensor(shift0[:], mv0[:, :, 0], -1.0, nw0[:, 1, :], ALU.mult, ALU.mult).then_inc(stat0, 1)
            dve.wait_ge(small_in, 16 * 11)
            done(nc.vector.tensor_scalar(gw[:], gw_n[:], g_c[:, 0:1], None, ALU.mult))
            done(nc.vector.tensor_copy(beta_all[:], beta_c[:, 0:1].broadcast_to([P, P])))
            assert n[0] == DVE_PREP
            dve.wait_ge(prep_act, ACT_PREP)

            def step(i, half, par, quarter, slot):
                ii = known(i, 0)
                a = ii is None or ii < NCH
                b = ii is None or 1 <= ii <= NCH
                c = ii is None or ii >= 2
                rb, rc = rows[(slot - 1) % RB], rows[(slot - 2) % RB]
                n1, r1 = (i - 1) * NEWTON1, (i - 2) * ROUTE
                v, y, t, u = (nw1[:, k, :] for k in range(4))

                if c:
                    dve.wait_ge(lg_psum, i - 1)
                    nc.vector.tensor_tensor(lg[:], bank[6][:, 0:CT * E].rearrange("p (t e) -> p t e", t=CT),
                                            gb_all[:].rearrange("p (a e) -> p a e", a=1).broadcast_to([P, CT, E]),
                                            ALU.add).then_inc(lg_copied, 1)
                    wait_apart(dve, (lg_copied, i - 1))
                    for k in range(CT):
                        ins = nc.vector.max(mx[:, k, :], lg[:, k, :])
                    ins.then_inc(route, 1)
                    wait_apart(dve, (route, r1 + 1))
                    for k in range(CT):
                        ins = nc.vector.max_index(mi[:, k, :], mx[:, k, :], lg[:, k, :])
                    ins.then_inc(route, 1)
                    nc.vector.tensor_tensor(gap[:], mx[:, :, 0], mx[:, :, 1], ALU.subtract).then_inc(route, 1)
                if b:
                    dve.wait_ge(x1_ready, i)
                    for k in range(CT):
                        ins = nc.vector.bn_stats(st1[:, k, :], x1[:, k, :])
                    ins.then_inc(st1_done, 1)
                if c:
                    dve.wait_ge(route, r1 + 3)
                    nc.vector.tensor_copy(idx[:], mi[:, :, 0:2]).then_inc(route, 1)
                if b:
                    wait_apart(dve, (st1_done, i))
                    for k in range(CT):
                        ins = nc.vector.bn_aggr(mv1[:, k, :], st1[:, k, :])
                    ins.then_inc(mv1_done, 1)
                if c:
                    dve.wait_ge(route, r1 + 4)
                    nc.vector.tensor_tensor(elo[:], idx[:, :, 0], idx[:, :, 1], ALU.min).then_inc(route, 1)
                    nc.vector.tensor_tensor(sgn[:], idx[:, :, 0], idx[:, :, 1], ALU.is_lt).then_inc(route, 1)
                    nc.vector.tensor_tensor(ehi[:], idx[:, :, 0], idx[:, :, 1], ALU.max).then_inc(route, 1)
                if b:
                    dve.wait_ge(mv1_done, i)
                    nc.vector.tensor_scalar(nw1[:, 0, 0:CT], mv1[:, :, 1], EPS, None, ALU.add).then_inc(newton, 1)
                    nc.vector.tensor_scalar(nw1[:, 0, CT:2 * CT], mv1[:, :, 1], 1.0 + EPS, EPS * EPS,
                                            ALU.mult, ALU.add).then_inc(newton, 1)
                if c:
                    dve.wait_ge(route, r1 + 7)
                    nc.vector.scalar_tensor_tensor(gaps[:], sgn[:], -0.5, gap[:], ALU.add, ALU.mult).then_inc(gap_ready, 1)
                    nc.vector.tensor_scalar(pr1[:], elo[:], -0.5, (2 * E - 3) / 2, ALU.mult, ALU.add).then_inc(route, 1)
                if b:
                    dve.wait_ge(newton, n1 + 2)
                    nc.vector.tensor_scalar(t.bitcast(I32), v.bitcast(I32), 1, None, ALU.logical_shift_right)\
                      .then_inc(newton, 1)
                if c:
                    dve.wait_ge(route, r1 + 8)
                    nc.vector.tensor_tensor(pr1[:], pr1[:], elo[:], ALU.mult).then_inc(route, 1)
                if b:
                    dve.wait_ge(newton, n1 + 3)
                    nc.vector.tensor_scalar(y.bitcast(I32), t.bitcast(I32), -1.0, MAGIC, ALU.mult, ALU.add)\
                      .then_inc(newton, 1)
                if c:
                    dve.wait_ge(route, r1 + 9)
                    nc.vector.scalar_tensor_tensor(pair[:], pr1[:], -1.0, ehi[:], ALU.add, ALU.add).then_inc(route, 1)

                def newton_step(k, between=None):
                    dve.wait_ge(newton, n1 + 4 + 3 * k)
                    nc.vector.tensor_tensor(t, y, y, ALU.mult).then_inc(newton, 1)
                    if between:
                        between()
                    dve.wait_ge(newton, n1 + 5 + 3 * k)
                    nc.vector.scalar_tensor_tensor(u, t, -0.5, v, ALU.mult, ALU.mult).then_inc(newton, 1)

                def newton_end(k):
                    dve.wait_ge(newton, n1 + 6 + 3 * k)
                    nc.vector.scalar_tensor_tensor(y, u, 1.5, y, ALU.add, ALU.mult).then_inc(newton, 1)

                def one_hot():
                    dve.wait_ge(route, r1 + 10)
                    nc.vector.tensor_tensor(
                        hot[:], pair_no[:].rearrange("p (a n) -> p a n", a=1).broadcast_to([P, CT, NP]),
                        pair[:].rearrange("p (t a) -> p t a", a=1).broadcast_to([P, CT, NP]), ALU.is_equal).then_inc(hot_ready, 1)

                def hot_sum():
                    dve.wait_ge(hot_ready, i - 1)
                    nc.vector.tensor_reduce(hsum[:], hot[:].rearrange("p t n -> p n t"), AX.X, ALU.add).then_inc(route, 1)

                def keep_rate():
                    dve.wait_ge(tneg_ready, i + 1)
                    nc.vector.tensor_scalar(omz[:], tneg[:], 1.0, 0.5, ALU.add, ALU.mult).then_inc(omz_done, 1)

                def decay():
                    dve.wait_ge(omz_done, i + 1)
                    nc.vector.tensor_scalar(acoef[:], omz[:], A_GUARD, None, ALU.add).then_inc(ab_done, 1)

                if b:
                    newton_step(0, one_hot if c else None)
                elif c:
                    one_hot()
                if c:
                    hot_sum()
                if b:
                    newton_end(0)
                    newton_step(1)
                if a:
                    keep_rate()
                if b:
                    newton_end(1)
                if b:
                    newton_step(2, decay if a else None)
                    after(dve, scattered[(slot - 1) % RB], 16 * CT * (quarter if slot else quarter - 1))
                    nc.vector.tensor_copy(rb[:, :, MEAN_R], mv1[:, :, 0])
                    nc.vector.tensor_copy(rb[:, :, TOKEN], tok_no[:, bass.ds((i - 1) * CT, CT)])
                    newton_end(2)
                elif a:
                    decay()
                if a:
                    dve.wait_ge(hcand_ready, i + 1)
                    nc.vector.scalar_tensor_tensor(bneg[:], omz[:], 1.0, hcand[:], ALU.subtract, ALU.mult).then_inc(ab_done, 1)
                if b:
                    dve.wait_ge(newton, n1 + NEWTON1)
                    for k in range(CT):
                        ins = nc.vector.tensor_scalar(rb[:, k, 0:P], x1[:, k, :], mv1[:, k, 0:1],
                                                      nw1[:, 1, CT + k:CT + k + 1], ALU.subtract, ALU.mult)
                    ins.then_inc(y2_ready, 1)
                    nc.vector.tensor_tensor(sy[:], nw1[:, 0, CT:2 * CT], nw1[:, 1, CT:2 * CT], ALU.mult).then_inc(sy_done, 1)
                if a:
                    dve.wait_ge(ab_done, 2 * (i + 1))
                    after(dve, h_psum, i - 1)
                    for k in range(BPC):
                        at = slice(k * T, (k + 1) * T)
                        ins = nc.vector.tensor_tensor_scan(hseq[par][:, at], acoef[:, at], bneg[:, at], 0.0,
                                                           ALU.mult, ALU.subtract)
                    ins.then_inc(scan_done, 1)
                if b:
                    dve.wait_ge(sy_done, i)
                    nc.vector.scalar_tensor_tensor(rb[:, :, SCALE_R], nw1[:, 1, 0:CT], 1.0, sy[:], ALU.add, ALU.mult)
                if c:
                    dve.wait_ge(rank_psum, i - 1)
                    nc.vector.tensor_tensor(rsel[:].rearrange("p t n -> p (t n)"), hot[:].rearrange("p t n -> p (t n)"),
                                            bank[7][:, 0:CT * NP], ALU.mult).then_inc(rank_done, 1)
                    dve.wait_ge(route, r1 + 11)
                    nc.vector.tensor_tensor(carry[:], carry[:], hsum[:], ALU.add).then_inc(carry_ready, 1)
                    dve.wait_ge(th_ready, i - 1)
                    nc.vector.tensor_scalar(rc[:, :, W_LO], th[:], 0.5 / WSCALE, 0.5 / WSCALE, ALU.mult, ALU.add)
                    nc.vector.tensor_scalar(rc[:, :, W_HI], th[:], -0.5 / WSCALE, 0.5 / WSCALE, ALU.mult, ALU.add)
                    dve.wait_ge(rank_done, i - 1)
                    nc.vector.tensor_reduce(rank[:], rsel[:], AX.X, ALU.add).then_inc(rank_sum, 1)
                    dve.wait_ge(rank_sum, i - 1)
                    nc.vector.scalar_tensor_tensor(pos[(slot - 2) % RB][:], pair[:], float(REGION), rank[:],
                                                   ALU.mult, ALU.add).then_inc(pos_ready, 1)

            walk(dve, step, NCH, RB)

            k = [0]

            def link(ins):
                k[0] += 1
                ins.then_inc(plan_step, 1)
                dve.wait_ge(plan_step, k[0])

            counts = bank[7][:, 0:NP]
            dve.wait_ge(counts_psum, 1)
            nc.vector.tensor_tensor(pad_at[:], pad_base[:], counts, ALU.add).then_inc(pads_ready, 1)
            tiles, upto, first, at_or_after, tmp, ones_np = (pl[:, q, :] for q in range(6))
            p_no, p_first, used, within = pc[:, 0:1], pc[:, 1:2], pc[:, 2:3], pc[:, 3:4]
            link(nc.vector.tensor_scalar(cnt_i[:, 0, :], counts, float(P - 1), None, ALU.add))
            link(nc.vector.tensor_scalar(cnt_i[:, 1, :], cnt_i[:, 0, :], P.bit_length() - 1, None, ALU.logical_shift_right))
            link(nc.vector.tensor_scalar(tiles, cnt_i[:, 1, :], 1.0, None, ALU.max))
            link(nc.vector.tensor_tensor_scan(upto, ones_np, tiles, 0.0, ALU.mult, ALU.add))
            link(nc.vector.tensor_tensor(first, upto, tiles, ALU.subtract))
            link(nc.vector.tensor_scalar(at_or_after, first, part_no[:, 0:1], None, ALU.is_le))
            nc.vector.tensor_reduce(p_no, at_or_after, AX.X, ALU.add)
            link(nc.vector.tensor_tensor(tmp, at_or_after, first, ALU.mult))
            link(nc.vector.tensor_reduce(p_first, tmp, AX.X, ALU.max))
            link(nc.vector.tensor_scalar(p_no, p_no, -1.0, None, ALU.add))
            link(nc.vector.tensor_scalar(at_or_after, pair_no[:], p_no, None, ALU.is_equal))
            nc.vector.tensor_tensor(tiles, at_or_after, lo_tab[:], ALU.mult)
            nc.vector.tensor_tensor(used, part_no[:], upto[:, NP - 1:NP], ALU.is_lt)
            nc.vector.tensor_tensor(within, part_no[:], p_first, ALU.subtract)
            link(nc.vector.tensor_tensor(tmp, at_or_after, hi_tab[:], ALU.mult))
            nc.vector.tensor_reduce(plan_f[:, 0:1], tiles, AX.X, ALU.add)
            nc.vector.tensor_reduce(plan_f[:, 1:2], tmp, AX.X, ALU.add)
            link(nc.vector.tensor_scalar(within, within, float(P), float(-SPARE), ALU.mult, ALU.add))
            link(nc.vector.scalar_tensor_tensor(within, p_no, float(REGION), within, ALU.mult, ALU.add))
            link(nc.vector.tensor_tensor(within, within, used, ALU.mult))
            link(nc.vector.tensor_scalar(plan_f[:, 2:3], within, float(SPARE), None, ALU.add))
            assert k[0] == PLAN
            dve.wait_ge(plan_psum, 1)
            W = RB + 1
            nc.vector.tensor_copy(plan_e[:, 0, :], bank[6][0:1, 0:2 * W + 2])
            nc.vector.tensor_copy(plan_row[:], bank[6][0:1, 2 * P:3 * P]).then_inc(plan_step, 1)
            dve.wait_ge(plan_step, PLAN + 1)
            for q in range(2):
                src = bank[6][0:1, q * P:q * P + NS]
                nc.vector.tensor_copy(plan_e[:, 1:NG + 1, q * W], src.rearrange("p (g k) -> p g k", k=RB)[:, :, RB - 1])
                ins = nc.vector.tensor_copy(plan_e[:, :, q * W + 1:(q + 1) * W],
                                            bank[6][0:1, q * P:q * P + NS + RB].rearrange("p (g k) -> p g k", k=RB))
            nc.vector.tensor_copy(plan_e[:, :, 2 * W:2 * W + 2], bank[6][0:1, 0:2 * (NG + 1)].rearrange("p (g k) -> p g k", k=2))\
              .then_inc(plan_ready, 1)

            dve.wait_ge(w1_in, 16)
            nc.vector.tensor_scalar(g256[:], g_c[:], WSCALE, None, ALU.mult).then_inc(w1_hi_done, 1)
            dve.wait_ge(w1_hi_done, 1)
            nc.vector.tensor_scalar(aw_hi[:], aw_n[:], g256[:, 0:1], None, ALU.mult)
            nc.vector.tensor_scalar(w1_hi[:], w1_n[:], g256[:, 0:1], None, ALU.mult).then_inc(w1_hi_done, 1)
            dve.wait_ge(w1_hi_done, 2)
            nc.vector.scalar_tensor_tensor(aw_lo[:], aw_n[:], g256[:, 0:1], aw_hi[:], ALU.mult, ALU.subtract)
            nc.vector.scalar_tensor_tensor(w1_lo[:], w1_n[:], g256[:, 0:1], w1_hi[:], ALU.mult, ALU.subtract).then_inc(w1_ready, 1)
            dve.wait_ge(bias_psum, 1)
            dve.wait_ge(bias_copied, 1)
            nc.vector.tensor_tensor(b1_s[:], bank[1][:, 0:E * FB], b1_t[:], ALU.add).then_inc(bias_step, 1)
            rows_split(ab_hl[:], ab_h[:], ab_l[:], ab_s[:], 1)
            rows_split(b2_hl[:], b2_h[:], b2_l[:], b2_s[:], 5)
            for ex in range(E):
                at = slice(ex * FB, (ex + 1) * FB)
                dve.wait_ge(w2r_copied, ex + 1)
                nc.vector.tensor_copy(w2_hi[:, at, :], w2_f[ex % 2][:]).then_inc(w2_hi_done, 1)
                dve.wait_ge(w2_hi_done, ex + 1)
                nc.vector.tensor_tensor(w2_lo[:, at, :], w2_f[ex % 2][:], w2_hi[:, at, :], ALU.subtract).then_inc(w2_ready, 1)

            def tile(j, half, par, quarter, slot):
                jj = known(j, 0)
                here = jj is None or jj < NS
                prev = jj is None or 1 <= jj <= NS

                def split(j, par, k):
                    dve.wait_ge(h_ready[k], j + 1)
                    after(dve, down_psum[k], j - 1)
                    nc.vector.tensor_copy(h_hi[k][par][:], h_f[k][:]).then_inc(hhi_done[k], 1)
                    dve.wait_ge(hhi_done[k], j + 1)
                    nc.vector.tensor_tensor(h_lo[k][par][:], h_f[k][:], h_hi[k][par][:], ALU.subtract)\
                      .then_inc(hlo_ready[k], 1)

                def low_x(j, par):
                    dve.wait_ge(xhi_ready, j + 1)
                    nc.vector.tensor_tensor(x_lo[par][:], bank[0][:, 0:P], x_hi[par][:], ALU.subtract).then_inc(xlo_ready, 1)

                if jj == 0:
                    low_x(0, 0)
                row, both = srow[(slot - 1) % RB], cat[1 - par]
                if prev:
                    dve.wait_ge(down_psum[0], j)
                    nc.vector.tensor_scalar(y_lo, bank[3][:, 0:P], row[:, W_LO:W_LO + 1], None, ALU.mult).then_inc(ylo_done, 1)
                if jj is None or jj >= 2:
                    dve.wait_ge(tg_ready, j - 1)
                    nc.vector.tensor_scalar(gate[:], tg[:], 0.5, 0.5, ALU.mult, ALU.add).then_inc(gate_done, 1)
                if jj is None or jj < NS - 1:
                    after(dve, up_psum[1], j)
                    low_x(j + 1, 1 - par)
                if jj is None or jj >= 2:
                    dve.wait_ge(gate_done, j - 1)
                    dve.wait_ge(diff_ready, j - 1)
                    after(dve, fin_ready, j - 2)
                    nc.vector.scalar_tensor_tensor(part, diff, gate[:, 0:1], cat[par][:, 0:P],
                                                   ALU.mult, ALU.add).then_inc(part_done, 1)
                if here:
                    split(j, par, 0)
                if prev:
                    dve.wait_ge(down_psum[1], j)
                    nc.vector.scalar_tensor_tensor(both[:, P:2 * P], bank[4][:, 0:P], row[:, W_HI:W_HI + 1], y_lo,
                                                   ALU.mult, ALU.add).then_inc(nonabel_ready, 1)
                    dve.wait_ge(nonabel_ready, j)
                    dve.wait_ge(abel_ready, j)
                    nc.vector.tensor_tensor_reduce(prod, both[:], mix_b_all[:, 0:2 * P], 1.0, 0.0,
                                                   ALU.mult, ALU.add, dot[1 - par][:]).then_inc(dot_ready, 1)
                if here:
                    split(j, par, 1)

            walk(dve, tile, NS, RB)


NAMES = ["L0_attn_x", "L0_attn_Wz", "L0_attn_bz", "L0_attn_Wh", "L0_attn_bh", "L0_ffn_ln_g", "L0_ffn_ln_b",
         "L0_ffn_abel_w", "L0_ffn_abel_b", "L0_ffn_gate_w_moe", "L0_ffn_gate_b_moe", "L0_ffn_w1", "L0_ffn_b1",
         "L0_ffn_w2", "L0_ffn_b2", "L0_ffn_gens", "L0_ffn_mix_w", "L0_ffn_mix_b"]


def kernel(**inputs):
    import numpy as np
    import concourse.bacc as bacc
    from concourse.bass_utils import run_bass_kernel_spmd

    nc = bacc.Bacc("TRN2", target_bir_lowering=False, num_devices=1)
    arrays, args = {}, []
    for name in NAMES:
        a = np.ascontiguousarray(inputs[name])
        arrays[f"in_{name}"] = a
        args.append(nc.dram_tensor(f"in_{name}", a.shape, mybir.dt.from_np(a.dtype), kind="ExternalInput").ap())
    shape = inputs["L0_attn_x"].shape
    args.append(nc.dram_tensor("result", shape, F32, kind="ExternalOutput").ap())
    gru_moe_block(nc, *args)
    r = run_bass_kernel_spmd(nc, [arrays], core_ids=[0])
    return r.results[0]["result"]
```

```python
from contextlib import ExitStack

import concourse.bass as bass
from concourse import mybir

F32 = mybir.dt.float32
F16 = mybir.dt.float16
BF16 = mybir.dt.bfloat16
I32 = mybir.dt.int32
U32 = mybir.dt.uint32
ALU = mybir.AluOpType
ACT = mybir.ActivationFunctionType
AX = mybir.AxisListType

P = 128
EPS = 1e-5
A_GUARD = 1e-8
WSCALE = 256.0
MAGIC = float(0x5F3759DF)


def gru_moe_block(nc, x, wz, bz, wh, bh, ln_g, ln_b, abel_w, abel_b, gate_w, gate_b,
                  w1, b1, w2, b2, gens, mix_w, mix_b, out):
    B, T, D = x.shape
    E, _, DF = w1.shape
    NROT = gens.shape[0]
    assert D == P and T % P == 0 and DF % P == 0
    TOK = B * T
    NT = TOK // P
    CT = 4
    NCH = NT // CT
    CW = CT * P
    BPC = CW // T
    FB = DF // P
    NP = E * (E - 1) // 2
    HT = 2
    TS = HT * P
    REGION = TOK + TS
    SPARE = NP * REGION
    NS = TOK // TS + NP - 1
    W_LO, W_HI, SCALE_R, MEAN_R, TOKEN, DENSE = P, P + 1, P + 2, P + 3, P + 4, P + 5
    ROW = DENSE + P
    NX = 4
    RB = 4
    NG = -(-NS // RB)
    XT = NT // NX
    SQUARINGS = NCH - 2 * RB
    assert NS + RB <= P and TOK % TS == 0 and NCH % RB == 0
    assert SQUARINGS == E and SQUARINGS % 2 == 0 and E % RB == 0
    PAIRS = [(a, b) for a in range(E) for b in range(a + 1, E)]

    x_tiles = x.rearrange("b t d -> (b t) d").rearrange("(n p) d -> p n d", p=P)
    out_rows = out.rearrange("b t d -> (b t) d")
    slots = nc.dram_tensor("slots", [SPARE + TS, ROW], F32).ap()

    ctx = ExitStack()
    with ctx:
        def sb(name, shape, dt=F32):
            return ctx.enter_context(nc.sbuf_tensor(name, shape, dt))

        def sem(name):
            return ctx.enter_context(nc.semaphore(name))

        bank = [ctx.enter_context(nc.psum_tensor(f"bank{i}", [P, 512], F32)) for i in range(8)]

        ident = sb("ident", [P, P])
        ident2 = sb("ident2", [P, P])
        tri = sb("tri", [P, P], BF16)
        ones_b = sb("ones_b", [P, P], BF16)
        ones_f = sb("ones_f", [1, P])
        ones_h = sb("ones_h", [2, P], F16)
        pair_no = sb("pair_no", [P, NP])
        pad_base = sb("pad_base", [P, NP])
        first_row = sb("first_row", [P, NP], F16)
        ones_p = sb("ones_p", [P, P], F16)
        code_tab = sb("code_tab", [P, NP])
        lo_tab = sb("lo_tab", [P, NP])
        hi_tab = sb("hi_tab", [P, NP])
        part_no = sb("part_no", [P, 1])
        half_c = sb("half_c", [P, 1])
        guard_c = sb("guard_c", [P, 1])
        tok_no = sb("tok_no", [P, NT])
        row_sel = sb("row_sel", [2, 2])
        zero_row = sb("zero_row", [P, HT, ROW])
        x_all = sb("x_all", [P, NT, P])
        wz_n = sb("wz_n", [P, P])
        wh_n = sb("wh_n", [P, P])
        bz_c = sb("bz_c", [P, 1])
        bh_c = sb("bh_c", [P, 1])
        g_c = sb("g_c", [P, 1])
        beta_c = sb("beta_c", [P, 2])
        aw_n = sb("aw_n", [P, P])
        ab_r = sb("ab_r", [1, P])
        gw_n = sb("gw_n", [P, E])
        gb_r = sb("gb_r", [1, E])
        w1_n = sb("w1_n", [P, E, DF])
        b1_n = sb("b1_n", [E * FB, P])
        w2_n = sb("w2_n", [P, E * FB, P])
        b2_n = sb("b2_n", [E, P])
        mix_r = sb("mix_r", [1, 2 * P + 1])
        wzh_t = sb("wzh_t", [P, 2, P])
        nbz = sb("nbz", [P, 1])
        g256 = sb("g256", [P, 1])
        gw = sb("gw", [P, E])
        gb_all = sb("gb_all", [P, E])
        beta_all = sb("beta_all", [P, P])
        aw_s = sb("aw_s", [P, P])
        ab_hl = sb("ab_hl", [2, P], F16)
        ab_s = sb("ab_s", [2, P])
        ab_h = sb("ab_h", [2, P], F16)
        ab_l = sb("ab_l", [2, P])
        w1_hi = sb("w1_hi", [P, E, DF], F16)
        w1_lo = sb("w1_lo", [P, E, DF], F16)
        b1_t = sb("b1_t", [P, E * FB])
        b1_s = sb("b1_s", [P, E * FB])
        w2_hi = sb("w2_hi", [P, E * FB, P], F16)
        w2_lo = sb("w2_lo", [P, E * FB, P], F16)
        b2_t = sb("b2_t", [P, E, 2])
        b2_h = sb("b2_h", [2, E * P], F16)
        b2_hl = sb("b2_hl", [2, E * P], F16)
        mix_b_all = sb("mix_b_all", [P, 2 * P + 1])
        mixb_h = sb("mixb_h", [P, 1])
        RG = NROT * P
        poly = sb("poly", [P, 8, RG])
        a_1, a_1t, a_2, a_2t, a_3, a_4t, q_s, p_s = (poly[:, k, :] for k in range(8))
        w1_s = [poly[:].rearrange("p k n -> p (k n)")[:, k * DF:(k + 1) * DF] for k in range(2)]
        em = [sb(f"em{i}", [P, RG]) for i in range(2)]
        emt = [sb(f"emt{i}", [P, RG]) for i in range(2)]
        f_s = sb("f_s", [P, 2, P])
        rot = sb("rot", [P, P])
        st0 = sb("st0", [P, NT, 6])
        mv0 = sb("mv0", [P, NT, 2])
        nw0 = sb("nw0", [P, 4, NT])
        shift0 = sb("shift0", [P, NT])
        xn = [sb(f"xn{i}", [P, CT, P]) for i in range(2)]
        x_t = sb("x_t", [P, CW])
        tneg = sb("tneg", [P, CW])
        hcand = sb("hcand", [P, CW])
        omz = sb("omz", [P, CW])
        acoef = [sb(f"acoef{i}", [P, CW]) for i in range(2)]
        bneg = sb("bneg", [P, CW])
        hseq = [sb(f"hseq{i}", [P, CW]) for i in range(2)]
        st1 = sb("st1", [P, CT, 6])
        mv1 = sb("mv1", [P, CT, 2])
        nw1 = sb("nw1", [P, 4, 2 * CT])
        sy = sb("sy", [P, CT])
        h_row = sb("h_row", [P, CW])
        x1 = sb("x1", [P, CT, P])
        rows = [sb(f"rows{i}", [P, CT, ROW]) for i in range(RB)]
        y2_t = sb("y2_t", [P, CW])
        lg = sb("lg", [P, CT, E])
        mx = sb("mx", [P, CT, 8])
        mi = sb("mi", [P, CT, 8], U32)
        gap = sb("gap", [P, CT])
        elo = sb("elo", [P, CT])
        ehi = sb("ehi", [P, CT])
        sgn = sb("sgn", [P, CT])
        gaps = sb("gaps", [P, CT])
        th = sb("th", [P, CT])
        code = sb("code", [P, CT])
        hot = sb("hot", [P, CT, NP], BF16)
        hsum = sb("hsum", [P, NP])
        carry = sb("carry", [P, NP], BF16)
        rsel = sb("rsel", [P, CT, NP])
        rank = sb("rank", [P, CT])
        pos = [sb(f"pos{i}", [P, CT], I32) for i in range(RB)]
        pad_at = sb("pad_at", [1, NP], I32)
        cnt_i = sb("cnt_i", [P, 2, NP], I32)
        pl = sb("pl", [P, 6, NP])
        pc = sb("pc", [P, 8])
        plan_f = sb("plan_f", [P, 3])
        plan_e = sb("plan_e", [1, NG + 1, 2 * (RB + 1) + 2], I32)
        plan_row = sb("plan_row", [1, P], I32)
        srow = [rows[i][:].rearrange("p t r -> p (t r)")[:, 0:HT * (ROW + P)].rearrange("p (s r) -> p s r", s=HT)
                for i in range(RB)]
        x_hi = [sb(f"x_hi{i}", [P, TS], F16) for i in range(2)]
        x_lo = [sb(f"x_lo{i}", [P, TS], F16) for i in range(2)]
        h_hi = [[sb(f"h_hi{k}{i}", [P, FB, TS], F16) for i in range(2)] for k in range(2)]
        h_lo = [[sb(f"h_lo{k}{i}", [P, FB, TS], F16) for i in range(2)] for k in range(2)]
        dot = [sb(f"dot{i}", [P, HT]) for i in range(2)]
        tg = sb("tg", [P, HT])
        gate = sb("gate", [P, HT])
        tok_i = [sb(f"tok_i{i}", [P, HT], I32) for i in range(2)]
        placed = [0]

        def in_x(blocks):
            k = placed[0]
            placed[0] += blocks
            assert placed[0] <= NT
            return x_all[:, k:k + blocks, :]

        h_f = [in_x(FB * HT).rearrange("p (f s) d -> p f (s d)", f=FB) for k in range(2)]
        y_lo, diff, part = in_x(HT), in_x(HT), in_x(HT)
        base = [in_x(HT) for i in range(2)]
        scratch = placed[0]
        prod = in_x(2 * HT).rearrange("p (s a) d -> p s (a d)", s=HT)
        fin = [in_x(HT) for i in range(2)]
        assert placed[0] - scratch == E
        b2_s = x_all[0:2, scratch:scratch + E, :].rearrange("p e d -> p (e d)")
        b2_l = in_x(E)[0:2].rearrange("p e d -> p (e d)")
        w2_t = [in_x(FB) for i in range(2)]
        w2_f = [poly[:].rearrange("p k n -> p (k n)")[:, k * DF:(k + 1) * DF].rearrange("p (f d) -> p f d", f=FB)
                for k in range(8 * RG // DF)]
        w2_f += [in_x(FB) for k in range(E - len(w2_f))]

        attn_in = sem("attn_in")
        small_in = sem("small_in")
        gens_in = sem("gens_in")
        w1_in = sem("w1_in")
        w2_in = sem("w2_in")
        x_in = [sem(f"x_in{i}") for i in range(NX)]
        spare_in = sem("spare_in")
        consts = sem("consts")
        prep_pe = sem("prep_pe")
        prep_act = sem("prep_act")
        prep_dve = sem("prep_dve")
        sq_psum = sem("sq_psum")
        sq_copied = sem("sq_copied")
        f_psum = sem("f_psum")
        f_copied = sem("f_copied")
        rot_psum = sem("rot_psum")
        rot_ready = sem("rot_ready")
        w1_s_done = sem("w1_s_done")
        w1_hi_done = sem("w1_hi_done")
        w1_ready = sem("w1_ready")
        w2t_psum = sem("w2t_psum")
        w2t_copied = sem("w2t_copied")
        w2r_psum = sem("w2r_psum")
        w2r_copied = sem("w2r_copied")
        w2_hi_done = sem("w2_hi_done")
        w2_ready = sem("w2_ready")
        bt_psum = sem("bt_psum")
        bias_psum = sem("bias_psum")
        bias_copied = sem("bias_copied")
        bias_step = sem("bias_step")
        xn_ready = sem("xn_ready")
        xt_psum = sem("xt_psum")
        xt_ready = sem("xt_ready")
        u_psum = sem("u_psum")
        v_psum = sem("v_psum")
        tneg_ready = sem("tneg_ready")
        hcand_ready = sem("hcand_ready")
        omz_done = sem("omz_done")
        acoef_ready = sem("acoef_ready")
        bneg_done = sem("bneg_done")
        scan_done = sem("scan_done")
        h_psum = sem("h_psum")
        h_copied = sem("h_copied")
        x1_ready = sem("x1_ready")
        st1_done = sem("st1_done")
        mv1_done = sem("mv1_done")
        newton = sem("newton")
        y2_ready = sem("y2_ready")
        y2t_psum = sem("y2t_psum")
        y2t_ready = sem("y2t_ready")
        lg_psum = sem("lg_psum")
        lg_copied = sem("lg_copied")
        sy_done = sem("sy_done")
        route = sem("route")
        gap_ready = sem("gap_ready")
        th_ready = sem("th_ready")
        hot_ready = sem("hot_ready")
        carry_ready = sem("carry_ready")
        dense_psum = sem("dense_psum")
        dense_ready = sem("dense_ready")
        rank_psum = sem("rank_psum")
        rank_done = sem("rank_done")
        rank_sum = sem("rank_sum")
        stat0 = sem("stat0")
        pos_ready = sem("pos_ready")
        scattered = [sem(f"scattered{i}") for i in range(RB)]
        pads_in = [sem(f"pads_in{i}") for i in range(2)]
        counts_psum = sem("counts_psum")
        pads_ready = sem("pads_ready")
        plan_step = sem("plan_step")
        plan_psum = sem("plan_psum")
        plan_ready = sem("plan_ready")
        row_in = [sem(f"row_in{i}") for i in range(RB)]
        x_psum = sem("x_psum")
        xhi_ready = sem("xhi_ready")
        xlo_ready = sem("xlo_ready")
        up_psum = [sem(f"up_psum{k}") for k in range(2)]
        h_ready = [sem(f"h_ready{k}") for k in range(2)]
        hhi_done = [sem(f"hhi_done{k}") for k in range(2)]
        hlo_ready = [sem(f"hlo_ready{k}") for k in range(2)]
        down_psum = [sem(f"down_psum{k}") for k in range(2)]
        ylo_done = sem("ylo_done")
        nonabel_ready = sem("nonabel_ready")
        dot_ready = sem("dot_ready")
        tg_ready = sem("tg_ready")
        diff_ready = sem("diff_ready")
        base_ready = sem("base_ready")
        part_done = sem("part_done")
        gate_done = sem("gate_done")
        fin_ready = sem("fin_ready")
        tok_ready = sem("tok_ready")
        stored = [sem(f"stored{i}") for i in range(2)]

        block = ctx.enter_context(nc.Block())

        def after(eng, s, n):
            if not isinstance(n, int) or n > 0:
                eng.wait_ge(s, n)

        def wait_apart(eng, *waits):
            waits = [(s, n if isinstance(n, int) else eng.to_reg(n)) for s, n in waits]
            eng.wait_ge(consts, CONSTS)
            for s, n in waits:
                after(eng, s, n)

        def walk(eng, step, n, width=2):
            for j in range(width):
                step(j, j // 2, j % 2, 0, j)
            last = (n - 1) // width * width
            with eng.Fori(1, last // width) as i:
                for k in range(width):
                    step(width * i + k, width // 2 * i + k // 2, k % 2, i, k)
            for j in range(last, n + 2):
                step(j, j // 2, j % 2, j // width, j % width)

        def load_experts(eng, table, group):
            table.clear()
            _, v = nc.values_load_multi_w_load_instructions(
                plan_e[:, bass.ds(group, 1), :].rearrange("p a n -> p (a n)"), engines=[eng], min_val=0, max_val=E - 1,
                skip_runtime_bounds_check_because="the plan's experts come from lo_tab and hi_tab")
            for k in range(-1, RB):
                table[k] = (v[k + 1], v[k + 2 + RB])

        def known(j, n):
            return j if isinstance(j, int) else None

        NEWTON = 11

        def rsqrt(dve, tab, s, base_count, first_src_done):
            v, y, t, u = (tab[:, k, :] for k in range(4))
            n = [0]

            def link(ins):
                n[0] += 1
                ins.then_inc(s, 1)
                return n[0]

            def wait():
                dve.wait_ge(s, base_count + n[0])

            first_src_done()
            link(nc.vector.tensor_scalar(t.bitcast(I32), v.bitcast(I32), 1, None, ALU.logical_shift_right))
            wait()
            link(nc.vector.tensor_scalar(y.bitcast(I32), t.bitcast(I32), -1.0, MAGIC, ALU.mult, ALU.add))
            for _ in range(3):
                wait()
                link(nc.vector.tensor_tensor(t, y, y, ALU.mult))
                wait()
                link(nc.vector.scalar_tensor_tensor(u, t, -0.5, v, ALU.mult, ALU.mult))
                wait()
                link(nc.vector.scalar_tensor_tensor(y, u, 1.5, y, ALU.add, ALU.mult))
            assert n[0] == NEWTON

        STAT_FIRST = 2 + 1 + NEWTON + 1
        STAT_ALL = STAT_FIRST + 2 * (NX - 1) + 1 + NEWTON + 1
        BIAS = 9
        NEWTON1 = NEWTON + 2
        ROUTE = 8
        CONSTS = 23 + 3 * NP
        ACT_PREP = 9
        PE_PREP = 7
        DVE_PREP = 10
        PLAN = 15

        @block.sync
        def _(sp):
            for dst, src in ((wz_n[:], wz), (wh_n[:], wh), (bz_c[:], bz.rearrange("(p a) -> p a", a=1)),
                             (bh_c[:], bh.rearrange("(p a) -> p a", a=1))):
                sp.dma_start(dst, src).then_inc(attn_in, 16)
            sp.dma_start(a_1.rearrange("p (g d) -> p g d", g=NROT), gens.rearrange("g p d -> p g d")).then_inc(gens_in, 16)
            def load_x(c):
                sp.dma_start(x_all[:, c * XT:(c + 1) * XT, :], x_tiles[:, c * XT:(c + 1) * XT, :]).then_inc(x_in[c], 16)
            load_x(0)
            for dst, src in (
                (g_c[:], ln_g.rearrange("(p a) -> p a", a=1)),
                (beta_c[:, 0:1], ln_b.rearrange("(p a) -> p a", a=1)),
                (beta_c[:, 1:2], ln_b.rearrange("(p a) -> p a", a=1)),
                (aw_n[:], abel_w), (ab_r[:], abel_b.rearrange("(a n) -> a n", a=1)),
                (gw_n[:], gate_w), (gb_r[:], gate_b.rearrange("(a n) -> a n", a=1)),
                (b1_n[:], b1.rearrange("e (f p) -> (e f) p", p=P)), (b2_n[:], b2),
                (mix_r[:, 0:2 * P], mix_w.rearrange("n a -> a n")),
                (mix_r[:, 2 * P:2 * P + 1], mix_b.rearrange("(a n) -> a n", a=1)),
            ):
                sp.dma_start(dst, src).then_inc(small_in, 16)
            for c in range(1, NX):
                load_x(c)
            sp.dma_start(w1_n[:], w1.rearrange("e d f -> d e f")).then_inc(w1_in, 16)
            sp.dma_start(w2_n[:].rearrange("p (e f) d -> p e f d", e=E),
                         w2.rearrange("e (f p) d -> p e f d", p=P)).then_inc(w2_in, 16)
            sp.wait_ge(consts, CONSTS)
            sp.dma_start(slots[SPARE:SPARE + TS, :].rearrange("(s p) r -> p s r", p=P), zero_row[:]).then_inc(spare_in, 16)
            sp.wait_ge(spare_in, 16)
            sp.wait_ge(pads_ready, 1)
            _, pads = nc.values_load_multi_w_load_instructions(
                pad_at[:], engines=[mybir.EngineType.SP], min_val=0, max_val=SPARE - TS,
                skip_runtime_bounds_check_because="a bucket holds at most TOK of its TOK + TS rows")
            def pad(some, done):
                for at in some:
                    sp.dma_start(slots[bass.ds(at, TS), :].rearrange("(s p) r -> p s r", p=P), zero_row[:]).then_inc(done, 16)

            pad(pads[0:RB], pads_in[0])
            pad(pads[RB:RB + 4], pads_in[1])
            sp.wait_ge(pads_in[0], 16 * RB)
            for s in scattered:
                sp.wait_ge(s, 16 * CT * NCH // RB)
            sp.wait_ge(plan_ready, 1)

            def step(j, half, par, quarter, slot):
                jj = known(j, 0)
                if jj is not None and jj >= NS:
                    return
                at = sp.value_load(plan_row[:, bass.ds(j, 1)], min_val=0, max_val=SPARE)
                after(sp, tok_ready, j - RB + 1)
                sp.dma_start(srow[slot][:, :, 0:ROW], slots[bass.ds(at, TS), :].rearrange("(s p) r -> p s r", p=P)).then_inc(row_in[slot], 16)
                if jj == RB - 1:
                    pad(pads[RB + 4:], pads_in[1])
                    sp.wait_ge(pads_in[1], 16 * (NP - RB))

            walk(sp, step, NS, RB)

        @block.gpsimd
        def _(pool):
            n = [0]

            def done(ins):
                n[0] += 1
                ins.then_inc(consts, 1)

            done(pool.memset(ident[:], 0.0))
            done(pool.memset(ident2[:], 0.0))
            done(pool.memset(tri[:], 1.0))
            done(pool.memset(ones_b[:], 1.0))
            done(pool.memset(ones_f[:], 1.0))
            done(pool.memset(ones_p[:], 1.0))
            done(pool.memset(ones_h[:], 1.0))
            done(pool.memset(row_sel[:], 0.0))
            done(pool.memset(zero_row[:], 0.0))
            done(pool.memset(pl[:, 5, :], 1.0))
            done(pool.memset(carry[:], 0.0))
            done(pool.memset(half_c[:], 0.5))
            done(pool.memset(guard_c[:], A_GUARD))
            pool.wait_ge(consts, n[0])
            done(pool.memset(zero_row[:, :, TOKEN:TOKEN + 1], float(TOK)))
            done(pool.affine_select(out=ident[:], in_=ident[:], compare_op=ALU.not_equal, fill=1.0,
                                    base=0, pattern=[[-1, P]], channel_multiplier=1))
            done(pool.affine_select(out=ident2[:], in_=ident2[:], compare_op=ALU.not_equal, fill=2.0,
                                    base=0, pattern=[[-1, P]], channel_multiplier=1))
            done(pool.affine_select(out=tri[:], in_=tri[:], compare_op=ALU.is_gt, fill=0.0,
                                    base=0, pattern=[[1, P]], channel_multiplier=-1))
            done(pool.affine_select(out=row_sel[:], in_=row_sel[:], compare_op=ALU.not_equal, fill=1.0,
                                    base=0, pattern=[[-1, 2]], channel_multiplier=1))
            exact = dict(allow_small_or_imprecise_dtypes=True)
            done(pool.iota(pair_no[:], pattern=[[1, NP]], base=0, channel_multiplier=0, **exact))
            done(pool.iota(pad_base[:], pattern=[[REGION, NP]], base=0, channel_multiplier=0, **exact))
            assert NP * (REGION // P) <= 2048 and REGION % P == 0
            done(pool.iota(first_row[:], pattern=[[REGION // P, NP]], base=0, channel_multiplier=0, **exact))
            done(pool.iota(part_no[:], pattern=[[0, 1]], base=0, channel_multiplier=1, **exact))
            done(pool.iota(tok_no[:], pattern=[[P, NT]], base=0, channel_multiplier=1, **exact))
            for k, (a, b) in enumerate(PAIRS):
                done(pool.memset(code_tab[:, k:k + 1], float(a * E + b)))
                done(pool.memset(lo_tab[:, k:k + 1], float(a)))
                done(pool.memset(hi_tab[:, k:k + 1], float(b)))
            assert n[0] == CONSTS

            def step(i, half, par, quarter, slot):
                ii = known(i, 0)
                if ii is None or ii < NCH:
                    pool.wait_ge(h_copied, i + 1)
                    after(pool, y2_ready, CT * i)
                    pool.tensor_tensor(x1[:].rearrange("p t d -> p (t d)"), h_row[:],
                                       x_all[:, bass.ds(i * CT, CT), :].rearrange("p t d -> p (t d)"),
                                       ALU.add).then_inc(x1_ready, 1)
                if ii is None:
                    pool.wait_ge(w1_hi_done, i - RB + 1)
                    ex = bass.ds(i - RB, 1)
                    pool.tensor_tensor(w1_lo[:, ex, :].rearrange("p a n -> p (a n)"), w1_s[par],
                                       w1_hi[:, ex, :].rearrange("p a n -> p (a n)"), ALU.subtract).then_inc(w1_ready, 1)
                if ii is None or ii >= 2:
                    wait_apart(pool, (pos_ready, i - 1), (dense_ready, i - 1))
                    s = (slot - 2) % RB
                    for t in range(CT):
                        pool.indirect_dma_start(
                            out=slots, out_offset=bass.IndirectOffsetOnAxis(ap=pos[s][:, t:t + 1], axis=0),
                            in_=rows[s][:, t, :], in_offset=None).then_inc(scattered[s], 16)

            walk(pool, step, NCH, RB)
            def tile(j, half, par, quarter, slot):
                jj = known(j, 0)
                if jj is None or jj >= 2:
                    after(pool, stored[par], 16 * HT * (half - 1))
                    pool.wait_ge(part_done, j - 1)
                    pool.wait_ge(base_ready, j - 1)
                    pool.tensor_tensor(fin[par], part, base[par], ALU.add).then_inc(fin_ready, 1)
                    wait_apart(pool, (fin_ready, j - 1))
                    pool.tensor_copy(tok_i[par][:], srow[(slot - 2) % RB][:, :, TOKEN]).then_inc(tok_ready, 1)
                    wait_apart(pool, (tok_ready, j - 1))
                    for h in range(HT):
                        pool.indirect_dma_start(
                            out=out_rows, out_offset=bass.IndirectOffsetOnAxis(ap=tok_i[par][:, h:h + 1], axis=0),
                            in_=fin[par][:, h, :], in_offset=None, bounds_check=TOK - 1, oob_is_err=False,
                        ).then_inc(stored[par], 16)
                if jj is None or 1 <= jj <= NS:
                    pool.wait_ge(dot_ready, j)
                    row = srow[(slot - 1) % RB]
                    after(pool, part_done, j - 1)
                    pool.tensor_tensor(diff, row[:, :, ROW:ROW + P], row[:, :, DENSE:DENSE + P],
                                       ALU.subtract).then_inc(diff_ready, 1)

            walk(pool, tile, NS, RB)
            for k, s in enumerate(stored):
                pool.wait_ge(s, 16 * HT * ((NS + 1 - k) // 2))

        @block.scalar
        def _(act):
            n = [0]

            def done(ins):
                n[0] += 1
                ins.then_inc(prep_act, 1)

            act.wait_ge(attn_in, 64)
            done(act.activation(nbz[:], bz_c[:], ACT.Gelu))
            act.wait_ge(prep_act, 1)
            done(act.mul(nbz[:], bz_c[:], -0.5))
            act.wait_ge(prep_pe, 1)
            done(act.copy(wzh_t[:].rearrange("p a b -> p (a b)"), bank[0][:, 0:2 * P]))
            act.wait_ge(prep_pe, 2)
            done(act.copy(a_1t, bank[1][:, 0:RG]))
            act.wait_ge(prep_pe, 3)
            done(act.copy(a_2, bank[1][:, 0:RG]))
            done(act.copy(a_2t, bank[2][:, 0:RG]))
            act.wait_ge(prep_pe, 4)
            done(act.copy(a_3, bank[3][:, 0:RG]))
            done(act.mul(a_4t, bank[4][:, 0:RG], 1.0 / 24.0))
            def normalize(i, par):
                after(act, xt_psum, i - 1)
                for t in range(CT):
                    c = i * CT + t
                    ins = act.activation(xn[par][:, t, :], x_all[:, bass.ds(c, 1), :].rearrange("p a d -> p (a d)"),
                                         ACT.Identity, bias=shift0[:, bass.ds(c, 1)], scale=nw0[:, 1, bass.ds(c, 1)])
                ins.then_inc(xn_ready, 1)

            def turned(i):
                act.wait_ge(xt_psum, i + 1)
                after(act, v_psum, i)
                act.copy(x_t[:], bank[0][:]).then_inc(xt_ready, 1)

            def projected(i):
                act.wait_ge(u_psum, i + 1)
                act.activation(tneg[:], bank[1][:], ACT.Tanh, bias=nbz[:], scale=-0.5).then_inc(tneg_ready, 1)
                act.wait_ge(v_psum, i + 1)
                after(act, bneg_done, i)
                act.activation(hcand[:], bank[2][:], ACT.Identity, bias=bh_c[:]).then_inc(hcand_ready, 1)
                act.wait_ge(tneg_ready, i + 1)
                act.activation(omz[:], tneg[:], ACT.Identity, bias=half_c[:], scale=0.5).then_inc(omz_done, 1)

            def decay(i, par):
                act.wait_ge(omz_done, i + 1)
                after(act, scan_done, i - 1)
                act.activation(acoef[par][:], omz[:], ACT.Identity, bias=guard_c[:]).then_inc(acoef_ready, 1)

            act.wait_ge(stat0, STAT_FIRST)
            act.wait_ge(consts, CONSTS - 3 * NP)
            normalize(0, 0)
            turned(0)
            projected(0)
            normalize(1, 1)
            decay(0, 0)
            turned(1)
            act.wait_ge(prep_pe, 5)
            act.copy(em[0][:], bank[5][:, 0:RG]).then_inc(sq_copied, 1)
            act.wait_ge(prep_pe, 6)
            act.mul(ab_s[:], bank[7][0:2, P:2 * P], WSCALE)
            done(act.copy(gb_all[:], bank[7][:, 0:E]))
            assert n[0] == ACT_PREP
            act.wait_ge(prep_pe, PE_PREP)
            act.copy(emt[0][:], bank[7][:, 0:RG]).then_inc(sq_copied, 1)

            def w2_rotated(e):
                if e + 1 < E:
                    act.wait_ge(w2t_psum, e + 2)
                    if e >= 1:
                        act.wait_ge(w2r_psum, e)
                    act.copy(w2_t[(e + 1) % 2].rearrange("p f d -> p (f d)"), bank[(3, 0)[(e + 1) % 2]][:])\
                       .then_inc(w2t_copied, 1)
                act.wait_ge(w2r_psum, e + 1)
                act.mul(w2_f[e].rearrange("p a b -> p (a b)"), bank[(5, 2)[e % 2]][:], WSCALE).then_inc(w2r_copied, 1)

            def step(i, half, par, quarter, slot):
                ii = known(i, 0)
                if ii is None or ii < NCH - 1:
                    projected(i + 1)
                if ii == XT // CT - 2:
                    act.wait_ge(stat0, STAT_ALL)
                if ii is None or ii < NCH - 2:
                    normalize(i + 2, par)
                if ii is None or ii < NCH - 1:
                    decay(i + 1, 1 - par)
                if ii == RB - 1:
                    act.wait_ge(w1_in, 16)
                    act.wait_ge(prep_dve, 9)
                if ii is None or ii >= 2:
                    act.wait_ge(gap_ready, i - 1)
                    after(act, pos_ready, i - 2)
                    act.activation(th[:], gaps[:], ACT.Tanh).then_inc(th_ready, 1)
                if ii is None or 1 <= ii <= NCH:
                    act.wait_ge(y2t_psum, i)
                    after(act, dense_psum, i - 1)
                    act.copy(y2_t[:], bank[4][:]).then_inc(y2t_ready, 1)
                if ii is None or ii < NCH:
                    act.wait_ge(h_psum, i + 1)
                    after(act, x1_ready, i)
                    act.copy(h_row[:], bank[3][:]).then_inc(h_copied, 1)
                if ii is None or ii < NCH - 2:
                    turned(i + 2)
                if ii is None:
                    act.wait_ge(sq_psum, i - RB + 1)
                    act.copy(em[1 - par][:], bank[5][:, 0:RG]).then_inc(sq_copied, 1)
                    act.copy(emt[1 - par][:], bank[7][:, 0:RG]).then_inc(sq_copied, 1)
                    ex = bass.ds(i - RB, 1)
                    act.wait_ge(x1_ready, i)
                    act.activation(w1_s[par], w1_n[:, ex, :].rearrange("p a n -> p (a n)"), ACT.Identity,
                                   scale=g256[:, 0:1]).then_inc(w1_s_done, 1)
                    act.wait_ge(w1_s_done, i - RB + 1)
                    act.copy(w1_hi[:, ex, :].rearrange("p a n -> p (a n)"), w1_s[par]).then_inc(w1_hi_done, 1)
                if ii == NCH - RB:
                    act.wait_ge(f_psum, 1)
                    act.copy(b1_t[:], bank[5][:, 384:384 + E * FB])
                    for k in range(2):
                        act.copy(b2_t[:, :, k], bank[5][:, 448:448 + E])
                    act.copy(f_s[:].rearrange("p a b -> p (a b)"), bank[5][:, 0:2 * P]).then_inc(f_copied, 1)
                if ii == NCH - RB + 1:
                    act.wait_ge(rot_psum, 1)
                    act.copy(rot[:], bank[5][:, 2 * P:3 * P]).then_inc(rot_ready, 1)
                if ii == NCH - 1:
                    act.wait_ge(bias_psum, 1)
                    for k in range(2):
                        act.mul(b2_s[:, k * 512:(k + 1) * 512], bank[1 + k][0:2, :], WSCALE)
                    act.copy(mix_b_all[:], bank[5][:, 0:2 * P + 1]).then_inc(bias_copied, 1)
                    act.wait_ge(bias_copied, 1)
                    act.mul(mixb_h[:], mix_b_all[:, 2 * P:2 * P + 1], 0.5)

                if ii is None or 1 <= ii <= NCH:
                    act.wait_ge(dense_psum, i)
                    act.activation(rows[(slot - 1) % RB][:, :, DENSE:DENSE + P], bank[4][:].rearrange("p (t d) -> p t d", t=CT),
                                   ACT.Gelu, scale=1.0 / WSCALE).then_inc(dense_ready, 1)
                if ii == NCH:
                    act.wait_ge(w2t_psum, 1)
                    act.copy(w2_t[0].rearrange("p f d -> p (f d)"), bank[3][:]).then_inc(w2t_copied, 1)

            walk(act, step, NCH, RB)

            for e in range(E):
                w2_rotated(e)
            act.wait_ge(bias_step, 5)
            act.wait_ge(plan_ready, 1)

            experts = {}

            def tile(j, half, par, quarter, slot):
                jj = known(j, 0)
                if slot == 0 and (jj is None or jj < NS):
                    load_experts(mybir.EngineType.Activation, experts, quarter)

                def up(k):
                    e = experts[slot][k]
                    after(act, hlo_ready[k], j)
                    for f in range(FB):
                        if f % 2 == 0:
                            act.wait_ge(up_psum[k], 2 * j + f // 2 + 1)
                        ins = act.activation(h_f[k][:, f, :], bank[1 + 2 * k + f // 2][:, f % 2 * TS:(f % 2 + 1) * TS],
                                             ACT.Gelu, bias=b1_s[:, bass.ds(e * FB + f, 1)], scale=1.0 / WSCALE)
                        if f % 2:
                            ins.then_inc(h_ready[k], 1)

                if jj == 0:
                    act.wait_ge(x_psum, 1)
                    act.copy(x_hi[0][:], bank[0][:, 0:TS]).then_inc(xhi_ready, 1)
                if jj is None or jj < NS:
                    up(0)
                if jj is None or jj >= 2:
                    act.wait_ge(dot_ready, j - 1)
                    act.activation(tg[:], dot[par][:], ACT.Tanh, bias=mixb_h[:], scale=0.5).then_inc(tg_ready, 1)
                if jj is None or jj < NS - 1:
                    act.wait_ge(x_psum, j + 2)
                    after(act, up_psum[1], 2 * j)
                    act.copy(x_hi[1 - par][:], bank[0][:, 0:TS]).then_inc(xhi_ready, 1)
                if jj is None or 1 <= jj <= NS:
                    act.wait_ge(down_psum[0], j)
                    after(act, nonabel_ready, j - 1)
                    for h in range(HT):
                        ins = act.activation(y_lo[:, h, :], bank[5][:, h * P:(h + 1) * P], ACT.Identity,
                                             scale=srow[(slot - 1) % RB][:, h, W_LO:W_LO + 1])
                    ins.then_inc(ylo_done, 1)
                if jj is None or jj < NS:
                    up(1)
                    act.wait_ge(h_ready[1], 2 * (j + 1))
                    after(act, down_psum[1], j - 1)
                    act.copy(h_hi[1][par][:], h_f[1]).then_inc(hhi_done[1], 1)
                    after(act, fin_ready, j - 1)
                    for h in range(HT):
                        ins = act.activation(base[par][:, h, :], srow[slot][:, h, 0:P], ACT.Identity,
                                             bias=srow[slot][:, h, MEAN_R:MEAN_R + 1],
                                             scale=srow[slot][:, h, SCALE_R:SCALE_R + 1])
                    ins.then_inc(base_ready, 1)

            walk(act, tile, NS, RB)

        @block.tensor
        def _(pe):
            n = [0]

            def done(ins):
                n[0] += 1
                ins.then_inc(prep_pe, 1)

            def mm(o, lhs, rhs, start=True, stop=True):
                return pe.matmul(o, lhs, rhs, start=start, stop=stop)

            def g(t, k):
                return t[:, k * P:(k + 1) * P]

            pe.wait_ge(consts, CONSTS - 3 * NP)
            pe.wait_ge(attn_in, 64)
            pe.transpose(bank[0][:, 0:P], wz_n[:], ident[:])
            done(pe.transpose(bank[0][:, P:2 * P], wh_n[:], ident[:]))
            pe.wait_ge(prep_dve, 1)
            for k in range(NROT):
                ins = pe.transpose(g(bank[1], k), g(a_1, k), ident[:])
            done(ins)
            pe.wait_ge(prep_act, 4)
            for k in range(NROT):
                mm(g(bank[1], k), g(a_1t, k), g(a_1, k))
                ins = mm(g(bank[2], k), g(a_1, k), g(a_1t, k))
            done(ins)
            pe.wait_ge(prep_act, 6)
            for k in range(NROT):
                mm(g(bank[3], k), g(a_1t, k), g(a_2, k))
                ins = mm(g(bank[4], k), g(a_2, k), g(a_2t, k))
            done(ins)
            def turn(i, par):
                pe.wait_ge(xn_ready, i + 1)
                after(pe, xt_ready, i)
                for t in range(CT):
                    ins = pe.transpose(g(bank[0], t), xn[par][:, t, :], ident[:])
                ins.then_inc(xt_psum, 1)

            def project(i):
                pe.wait_ge(xt_ready, i + 1)
                after(pe, tneg_ready, i)
                mm(bank[1][:], wzh_t[:, 0, :], x_t[:]).then_inc(u_psum, 1)
                after(pe, hcand_ready, i)
                mm(bank[2][:], wzh_t[:, 1, :], x_t[:]).then_inc(v_psum, 1)

            turn(0, 0)
            project(0)
            pe.wait_ge(prep_act, 8)
            pe.wait_ge(prep_dve, 6)
            for k in range(NROT):
                mm(g(bank[5], k), g(a_4t, k), g(q_s, k), stop=False)
                ins = mm(g(bank[5], k), ident[:], g(p_s, k), start=False)
            done(ins)
            turn(1, 1)
            pe.wait_ge(small_in, 16 * 11)
            pe.wait_ge(prep_dve, 8)
            mm(bank[7][:, 0:E], beta_all[:], gw_n[:], stop=False)
            mm(bank[7][:, 0:E], ones_f[:], gb_r[:], start=False)
            mm(bank[7][0:2, P:2 * P], beta_c[:], aw_n[:], stop=False)
            done(mm(bank[7][0:2, P:2 * P], ones_f[:, 0:2], ab_r[:], start=False))
            pe.wait_ge(sq_copied, 1)
            pe.wait_ge(prep_act, ACT_PREP)
            for k in range(NROT):
                ins = pe.transpose(g(bank[7], k), g(em[0], k), ident[:])
            done(ins)
            assert n[0] == PE_PREP

            def w2_turn(ex):
                for f in range(FB):
                    ins = pe.transpose(g(bank[(3, 0)[ex % 2]], f), w2_n[:, ex * FB + f, :], ident[:])
                ins.then_inc(w2t_psum, 1)

            def w2_product(ex):
                pe.wait_ge(w2t_copied, ex + 1)
                if ex < 2:
                    pe.wait_ge(bias_copied, 1)
                else:
                    pe.wait_ge(w2r_copied, ex - 1)
                for f in range(FB):
                    ins = mm(g(bank[(5, 2)[ex % 2]], f), w2_t[ex % 2][:, f, :], rot[:])
                ins.then_inc(w2r_psum, 1)
                if ex + 2 < E:
                    w2_turn(ex + 2)

            def squaring(par):
                e, et = em[par], emt[par]
                for k in range(NROT):
                    mm(g(bank[5], k), g(et, k), g(e, k), stop=False)
                    mm(g(bank[5], k), ident2[:], g(e, k), start=False)
                    mm(g(bank[7], k), g(e, k), g(et, k), stop=False)
                    ins = mm(g(bank[7], k), ident2[:], g(et, k), start=False)
                ins.then_inc(sq_psum, 1)

            def first_two():
                e, et = em[SQUARINGS % 2], emt[SQUARINGS % 2]
                mm(g(bank[5], 0), g(et, 0), g(e, 1), stop=False)
                mm(g(bank[5], 0), ident[:], g(e, 0), start=False, stop=False)
                mm(g(bank[5], 0), ident[:], g(e, 1), start=False)
                mm(g(bank[5], 1), g(e, 1), g(et, 0), stop=False)
                mm(g(bank[5], 1), ident[:], g(et, 0), start=False, stop=False)
                mm(g(bank[5], 1), ident[:], g(et, 1), start=False).then_inc(f_psum, 1)

            def rotation():
                e = em[SQUARINGS % 2]
                mm(g(bank[5], 2), f_s[:, 1, :], g(e, 2), stop=False)
                mm(g(bank[5], 2), ident[:], f_s[:, 0, :], start=False, stop=False)
                mm(g(bank[5], 2), ident[:], g(e, 2), start=False, stop=False)
                mm(g(bank[5], 2), ident[:], ident[:], start=False).then_inc(rot_psum, 1)

            def step(i, half, par, quarter, slot):
                ii = known(i, 0)
                a = ii is None or ii < NCH
                b = ii is None or 1 <= ii <= NCH
                c = ii is None or ii >= 2
                if ii is None or ii < NCH - 1:
                    project(i + 1)
                if ii is None:
                    pe.wait_ge(sq_copied, 2 * (i - RB + 1))
                    squaring(par)
                if ii == NCH - RB:
                    pe.wait_ge(sq_copied, 2 * (SQUARINGS + 1))
                    pe.transpose(bank[5][:, 384:384 + E * FB], b1_n[:], ident[0:E * FB, 0:E * FB])
                    pe.transpose(bank[5][:, 448:448 + E], b2_n[:], ident[0:E, 0:E])
                    first_two()
                if ii == NCH - RB + 1:
                    pe.wait_ge(f_copied, 1)
                    rotation()
                if ii is not None and NCH - RB <= ii < NCH:
                    pe.wait_ge(w1_in, 16)
                    k = ii - (NCH - RB)
                    for ex in range(k * E // RB, (k + 1) * E // RB):
                        for f in range(FB):
                            ins = mm(bank[7][:, 128 + ex * FB + f:129 + ex * FB + f], w1_n[:, ex, f * P:(f + 1) * P],
                                     beta_c[:, 0:1])
                    if ii == NCH - 1:
                        ins.then_inc(bt_psum, 1)
                        pe.wait_ge(rot_ready, 1)
                        pe.wait_ge(hcand_ready, NCH)
                        for ex in range(E):
                            mm(bank[1 + ex // 4][0:2, (ex % 4) * P:(ex % 4 + 1) * P], b2_t[:, ex, :], rot[:])
                        mm(bank[5][:, 0:2 * P + 1], ones_f[:], mix_r[:]).then_inc(bias_psum, 1)
                if c:
                    pe.wait_ge(hot_ready, i - 1)
                    after(pe, carry_ready, i - 2)
                    after(pe, rank_done, i - 2)
                    r = bank[6][:, P:P + CT * NP]
                    mm(r, tri[:], hot[:].rearrange("p t n -> p (t n)"), stop=False)
                    r3 = r.rearrange("p (t n) -> p t n", t=CT)
                    for t in range(CT - 1):
                        mm(r3[:, t + 1:CT, :], ones_b[:],
                           hot[:, t:t + 1, :].broadcast_to([P, CT - 1 - t, NP]), start=False, stop=False)
                    mm(r3, ones_p[:], first_row[:].rearrange("p (a n) -> p a n", a=1).broadcast_to([P, CT, NP]),
                       start=False, stop=False)
                    mm(r3, ones_b[:], carry[:].rearrange("p (a n) -> p a n", a=1).broadcast_to([P, CT, NP]),
                       start=False).then_inc(rank_psum, 1)
                if b:
                    after(pe, dense_ready, i - 1)
                    for t in range(CT):
                        pe.wait_ge(y2_ready, CT * (i - 1) + t + 1)
                        ins = pe.transpose(g(bank[4], t), rows[(slot - 1) % RB][:, t, 0:P], ident[:])
                    ins.then_inc(y2t_psum, 1)
                if a:
                    pe.wait_ge(scan_done, i + 1)
                    after(pe, h_copied, i)
                    for t in range(CT):
                        ins = pe.transpose(g(bank[3], t), g(hseq[par], t), ident[:])
                    ins.then_inc(h_psum, 1)
                if b:
                    pe.wait_ge(y2t_ready, i)
                    after(pe, lg_copied, i - 1)
                    after(pe, rank_done, i - 1)
                    for t in range(CT):
                        ins = mm(bank[6][:, t * E:(t + 1) * E], g(y2_t, t), gw[:])
                    ins.then_inc(lg_psum, 1)
                if ii is None or ii < NCH - 2:
                    turn(i + 2, par)
                if b:
                    if ii == 1:
                        pe.wait_ge(prep_dve, DVE_PREP)
                        pe.wait_ge(bias_step, 4)
                    for t in range(CT):
                        mm(g(bank[4], t), g(y2_t, t), aw_s[:], start=(t == 0), stop=False)
                    mm(bank[4][:].rearrange("p (t d) -> p t d", t=CT), ones_h[:],
                       ab_hl[:].rearrange("p (a d) -> p a d", a=1).broadcast_to([2, CT, P]), start=False).then_inc(dense_psum, 1)

                if ii == NCH:
                    pe.wait_ge(w2_in, 16)
                    pe.wait_ge(h_copied, NCH)
                    w2_turn(0)
                    w2_turn(1)

            walk(pe, step, NCH, RB)
            pe.wait_ge(carry_ready, NCH)
            pe.wait_ge(rank_done, NCH)
            pe.wait_ge(bias_step, 5)
            mm(bank[7][:, 0:NP], ones_b[:], carry[:]).then_inc(counts_psum, 1)
            for ex in range(E):
                w2_product(ex)
                if ex == 3:
                    pe.wait_ge(plan_step, PLAN)
                    for q in range(3):
                        ins = pe.transpose(bank[6][0:1, q * P:(q + 1) * P], plan_f[:, q:q + 1], ident[:])
                    ins.then_inc(plan_psum, 1)
            pe.wait_ge(plan_ready, 1)
            pe.wait_ge(w2r_copied, E)
            pe.wait_ge(w1_ready, E)

            experts = {}

            def tile(j, half, par, quarter, slot):
                jj = known(j, 0)
                if slot == 0:
                    load_experts(mybir.EngineType.PE, experts, quarter)

                def turn(j, slot, n):
                    pe.wait_ge(row_in[slot], 16 * n)
                    after(pe, xlo_ready, j)
                    for h in range(HT):
                        ins = pe.transpose(bank[0][:, h * P:(h + 1) * P], srow[slot][:, h, 0:P], ident[:])
                    ins.then_inc(x_psum, 1)

                def up(k):
                    e = experts[slot][k]
                    pe.wait_ge(xlo_ready, j + 1)
                    for f in range(FB):
                        if f % 2 == 0:
                            after(pe, h_ready[k], 2 * j - 1 + f // 2)
                        o = bank[1 + 2 * k + f // 2][:, f % 2 * TS:(f % 2 + 1) * TS]
                        hi = w1_hi[:, bass.ds(e, 1), f * P:(f + 1) * P].rearrange("p a n -> p (a n)")
                        lo = w1_lo[:, bass.ds(e, 1), f * P:(f + 1) * P].rearrange("p a n -> p (a n)")
                        mm(o, hi, x_hi[par][:], stop=False)
                        mm(o, hi, x_lo[par][:], start=False, stop=False)
                        ins = mm(o, lo, x_hi[par][:], start=False)
                        if f % 2:
                            ins.then_inc(up_psum[k], 1)

                def down(k):
                    e = experts[slot - 1][k]
                    pe.wait_ge(hlo_ready[k], j)
                    after(pe, ylo_done if k == 0 else nonabel_ready, j - 1)
                    for f in range(FB):
                        at = bass.ds(e * FB + f, 1)
                        hi, lo = (w[:, at, :].rearrange("p a n -> p (a n)") for w in (w2_hi, w2_lo))
                        for h in range(HT):
                            o, part_h = g(bank[5 + k], h), slice(h * P, (h + 1) * P)
                            mm(o, h_hi[k][1 - par][:, f, part_h], hi, start=(f == 0 and h == 0), stop=False)
                            mm(o, h_hi[k][1 - par][:, f, part_h], lo, start=False, stop=False)
                            mm(o, h_lo[k][1 - par][:, f, part_h], hi, start=False, stop=False)
                    for h in range(HT):
                        ins = mm(g(bank[5 + k], h), ones_h[:], b2_hl[:, bass.ds(e * P, P)], start=False, stop=(h == HT - 1))
                    ins.then_inc(down_psum[k], 1)

                here = jj is None or jj < NS
                prev = jj is None or 1 <= jj <= NS
                if jj == 0:
                    turn(0, 0, 1)
                if here:
                    up(0)
                if jj == 1:
                    pe.wait_ge(w2_ready, E)
                    pe.wait_ge(bias_step, BIAS)
                if prev:
                    down(0)
                if jj is None or jj < NS - 1:
                    turn(j + 1, (slot + 1) % RB, quarter + (slot + 1) // RB + 1)
                if here:
                    up(1)
                if prev:
                    down(1)

            walk(pe, tile, NS, RB)

        @block.vector
        def _(dve):
            n = [0]

            def done(ins):
                n[0] += 1
                ins.then_inc(prep_dve, 1)

            def rows_split(dst, hi, lo, src, k):
                nc.vector.tensor_copy(hi, src).then_inc(bias_step, 1)
                dve.wait_ge(bias_step, k + 1)
                nc.vector.scalar_tensor_tensor(lo, src, 1.0, hi, ALU.mult, ALU.subtract).then_inc(bias_step, 1)
                dve.wait_ge(bias_step, k + 2)
                nc.vector.tensor_scalar(lo, lo, row_sel[:, 1:2], None, ALU.mult).then_inc(bias_step, 1)
                dve.wait_ge(bias_step, k + 3)
                nc.vector.scalar_tensor_tensor(dst, hi, row_sel[:, 0:1], lo, ALU.mult, ALU.add).then_inc(bias_step, 1)

            dve.wait_ge(gens_in, 16)
            done(nc.vector.tensor_scalar(a_1, a_1, 2.0 ** -SQUARINGS, None, ALU.mult))

            m = [0]

            def stat(ins):
                m[0] += 1
                ins.then_inc(stat0, 1)

            def stats(c):
                dve.wait_ge(x_in[c], 16)
                for t in range(c * XT, (c + 1) * XT):
                    ins = nc.vector.bn_stats(st0[:, t, :], x_all[:, t, :])
                stat(ins)
                dve.wait_ge(stat0, m[0])
                for t in range(c * XT, (c + 1) * XT):
                    ins = nc.vector.bn_aggr(mv0[:, t, :], st0[:, t, :])
                stat(ins)

            def scales(first, last):
                at = slice(first, last)
                dve.wait_ge(stat0, m[0])
                stat(nc.vector.tensor_scalar(nw0[:, 0, at], mv0[:, at, 1], EPS, None, ALU.add))
                base_count = m[0]
                rsqrt(dve, nw0[:, :, at], stat0, base_count, lambda: dve.wait_ge(stat0, base_count))
                m[0] += NEWTON
                dve.wait_ge(stat0, m[0])
                stat(nc.vector.scalar_tensor_tensor(shift0[:, at], mv0[:, at, 0], -1.0, nw0[:, 1, at], ALU.mult, ALU.mult))

            stats(0)
            scales(0, XT)
            assert m[0] == STAT_FIRST
            dve.wait_ge(prep_act, 8)
            dve.wait_ge(consts, CONSTS - 3 * NP)
            def g3(t):
                return t.rearrange("p (g d) -> p g d", g=NROT)
            id3 = ident[:].rearrange("p (a d) -> p a d", a=1).broadcast_to([P, NROT, P])
            done(nc.vector.scalar_tensor_tensor(p_s, a_2, 0.5, a_1, ALU.mult, ALU.add))
            done(nc.vector.scalar_tensor_tensor(g3(q_s), g3(a_1), 1.0 / 5, id3, ALU.mult, ALU.add))
            dve.wait_ge(prep_dve, 3)
            done(nc.vector.scalar_tensor_tensor(p_s, a_3, 1.0 / 6, p_s, ALU.mult, ALU.add))
            done(nc.vector.scalar_tensor_tensor(q_s, a_2, 1.0 / 30, q_s, ALU.mult, ALU.add))
            dve.wait_ge(prep_dve, 5)
            done(nc.vector.scalar_tensor_tensor(q_s, a_3, 1.0 / 210, q_s, ALU.mult, ALU.add))
            dve.wait_ge(small_in, 16 * 11)
            done(nc.vector.tensor_scalar(gw[:], gw_n[:], g_c[:, 0:1], None, ALU.mult))
            done(nc.vector.tensor_copy(beta_all[:], beta_c[:, 0:1].broadcast_to([P, P])))
            done(nc.vector.tensor_scalar(g256[:], g_c[:], WSCALE, None, ALU.mult))
            dve.wait_ge(prep_dve, 9)
            done(nc.vector.tensor_scalar(aw_s[:], aw_n[:], g256[:, 0:1], None, ALU.mult))
            stats(1)
            assert n[0] == DVE_PREP

            def scan_input(i):
                after(dve, scan_done, i)
                dve.wait_ge(omz_done, i + 1)
                dve.wait_ge(hcand_ready, i + 1)
                nc.vector.scalar_tensor_tensor(bneg[:], omz[:], 1.0, hcand[:], ALU.subtract, ALU.mult).then_inc(bneg_done, 1)

            scan_input(0)

            def step(i, half, par, quarter, slot):
                ii = known(i, 0)
                a = ii is None or ii < NCH
                b = ii is None or 1 <= ii <= NCH
                c = ii is None or ii >= 2
                rb, rc = rows[(slot - 1) % RB], rows[(slot - 2) % RB]
                n1, r1 = (i - 1) * NEWTON1, (i - 2) * ROUTE
                v, y, t, u = (nw1[:, k, :] for k in range(4))

                if ii == 1:
                    scales(XT, NT)
                    assert m[0] == STAT_ALL
                if c:
                    if ii == 2:
                        dve.wait_ge(prep_act, ACT_PREP)
                    dve.wait_ge(lg_psum, i - 1)
                    nc.vector.tensor_tensor(lg[:], bank[6][:, 0:CT * E].rearrange("p (t e) -> p t e", t=CT),
                                            gb_all[:].rearrange("p (a e) -> p a e", a=1).broadcast_to([P, CT, E]),
                                            ALU.add).then_inc(lg_copied, 1)
                    wait_apart(dve, (lg_copied, i - 1))
                    for k in range(CT):
                        ins = nc.vector.max(mx[:, k, :], lg[:, k, :])
                    ins.then_inc(route, 1)
                    wait_apart(dve, (route, r1 + 1))
                    for k in range(CT):
                        ins = nc.vector.max_index(mi[:, k, :], mx[:, k, :], lg[:, k, :])
                    ins.then_inc(route, 1)
                    nc.vector.tensor_tensor(gap[:], mx[:, :, 0], mx[:, :, 1], ALU.subtract).then_inc(route, 1)
                if b:
                    dve.wait_ge(x1_ready, i)
                    for k in range(CT):
                        ins = nc.vector.bn_stats(st1[:, k, :], x1[:, k, :])
                    ins.then_inc(st1_done, 1)
                    wait_apart(dve, (st1_done, i))
                    for k in range(CT):
                        ins = nc.vector.bn_aggr(mv1[:, k, :], st1[:, k, :])
                    ins.then_inc(mv1_done, 1)
                if c:
                    dve.wait_ge(route, r1 + 3)
                    nc.vector.tensor_tensor(elo[:], mi[:, :, 0], mi[:, :, 1], ALU.min).then_inc(route, 1)
                    nc.vector.tensor_tensor(sgn[:], mi[:, :, 0], mi[:, :, 1], ALU.is_lt).then_inc(route, 1)
                    nc.vector.tensor_tensor(ehi[:], mi[:, :, 0], mi[:, :, 1], ALU.max).then_inc(route, 1)
                if b:
                    dve.wait_ge(mv1_done, i)
                    nc.vector.tensor_scalar(nw1[:, 0, 0:CT], mv1[:, :, 1], EPS, None, ALU.add).then_inc(newton, 1)
                    nc.vector.tensor_scalar(nw1[:, 0, CT:2 * CT], mv1[:, :, 1], 1.0 + EPS, EPS * EPS,
                                            ALU.mult, ALU.add).then_inc(newton, 1)
                if c:
                    dve.wait_ge(route, r1 + 6)
                    nc.vector.scalar_tensor_tensor(gaps[:], sgn[:], -0.5, gap[:], ALU.add, ALU.mult).then_inc(gap_ready, 1)
                    nc.vector.scalar_tensor_tensor(code[:], elo[:], float(E), ehi[:], ALU.mult, ALU.add).then_inc(route, 1)
                if b:
                    dve.wait_ge(newton, n1 + 2)
                    nc.vector.tensor_scalar(t.bitcast(I32), v.bitcast(I32), 1, None, ALU.logical_shift_right)\
                      .then_inc(newton, 1)
                    dve.wait_ge(newton, n1 + 3)
                    nc.vector.tensor_scalar(y.bitcast(I32), t.bitcast(I32), -1.0, MAGIC, ALU.mult, ALU.add)\
                      .then_inc(newton, 1)

                def newton_step(k, between=None):
                    dve.wait_ge(newton, n1 + 4 + 3 * k)
                    nc.vector.tensor_tensor(t, y, y, ALU.mult).then_inc(newton, 1)
                    if between:
                        between()
                    dve.wait_ge(newton, n1 + 5 + 3 * k)
                    nc.vector.scalar_tensor_tensor(u, t, -0.5, v, ALU.mult, ALU.mult).then_inc(newton, 1)

                def newton_end(k):
                    dve.wait_ge(newton, n1 + 6 + 3 * k)
                    nc.vector.scalar_tensor_tensor(y, u, 1.5, y, ALU.add, ALU.mult).then_inc(newton, 1)

                def one_hot():
                    dve.wait_ge(route, r1 + 7)
                    nc.vector.tensor_tensor(
                        hot[:], code_tab[:].rearrange("p (a n) -> p a n", a=1).broadcast_to([P, CT, NP]),
                        code[:].rearrange("p (t a) -> p t a", a=1).broadcast_to([P, CT, NP]), ALU.is_equal).then_inc(hot_ready, 1)

                def hot_sum():
                    dve.wait_ge(hot_ready, i - 1)
                    nc.vector.tensor_reduce(hsum[:], hot[:].rearrange("p t n -> p n t"), AX.X, ALU.add).then_inc(route, 1)

                if b:
                    newton_step(0, one_hot if c else None)
                elif c:
                    one_hot()
                if c:
                    hot_sum()
                if b:
                    newton_end(0)
                    newton_step(1)
                    newton_end(1)
                    newton_step(2)
                    if slot:
                        after(dve, scattered[slot - 1], 16 * CT * quarter)
                    nc.vector.tensor_copy(rb[:, :, MEAN_R], mv1[:, :, 0])
                    nc.vector.tensor_copy(rb[:, :, TOKEN], tok_no[:, bass.ds((i - 1) * CT, CT)])
                    newton_end(2)
                    dve.wait_ge(newton, n1 + NEWTON1)
                    for k in range(CT):
                        nc.vector.tensor_scalar(rb[:, k, 0:P], x1[:, k, :], mv1[:, k, 0:1],
                                                nw1[:, 1, CT + k:CT + k + 1], ALU.subtract, ALU.mult).then_inc(y2_ready, 1)
                    nc.vector.tensor_tensor(sy[:], nw1[:, 0, CT:2 * CT], nw1[:, 1, CT:2 * CT], ALU.mult).then_inc(sy_done, 1)
                if a:
                    dve.wait_ge(bneg_done, i + 1)
                    dve.wait_ge(acoef_ready, i + 1)
                    after(dve, h_psum, i - 1)
                    for k in range(BPC):
                        at = slice(k * T, (k + 1) * T)
                        ins = nc.vector.tensor_tensor_scan(hseq[par][:, at], acoef[par][:, at], bneg[:, at], 0.0,
                                                           ALU.mult, ALU.subtract)
                    ins.then_inc(scan_done, 1)
                if ii == 0:
                    for load in range(2, NX):
                        stats(load)
                    dve.wait_ge(prep_act, ACT_PREP)
                    rows_split(ab_hl[:], ab_h[:], ab_l[:], ab_s[:], 0)
                if b:
                    dve.wait_ge(sy_done, i)
                    nc.vector.scalar_tensor_tensor(rb[:, :, SCALE_R], nw1[:, 1, 0:CT], 1.0, sy[:], ALU.add, ALU.mult)
                if c:
                    dve.wait_ge(rank_psum, i - 1)
                    nc.vector.tensor_tensor(rsel[:].rearrange("p t n -> p (t n)"), hot[:].rearrange("p t n -> p (t n)"),
                                            bank[6][:, P:P + CT * NP], ALU.mult).then_inc(rank_done, 1)
                    dve.wait_ge(route, r1 + 8)
                    nc.vector.tensor_tensor(carry[:], carry[:], hsum[:], ALU.add).then_inc(carry_ready, 1)
                    dve.wait_ge(th_ready, i - 1)
                    nc.vector.tensor_scalar(rc[:, :, W_LO], th[:], 0.5 / WSCALE, 0.5 / WSCALE, ALU.mult, ALU.add)
                    nc.vector.tensor_scalar(rc[:, :, W_HI], th[:], -0.5 / WSCALE, 0.5 / WSCALE, ALU.mult, ALU.add)
                    dve.wait_ge(rank_done, i - 1)
                    nc.vector.tensor_reduce(rank[:], rsel[:], AX.X, ALU.add).then_inc(rank_sum, 1)
                    dve.wait_ge(rank_sum, i - 1)
                    nc.vector.tensor_copy(pos[(slot - 2) % RB][:], rank[:]).then_inc(pos_ready, 1)
                if ii is None or ii < NCH - 1:
                    scan_input(i + 1)
                if slot == RB - 1:
                    after(dve, scattered[slot], 16 * CT * quarter)
                if ii == NCH:
                    dve.wait_ge(bt_psum, 1)
                    dve.wait_ge(f_copied, 1)
                    nc.vector.tensor_tensor(b1_s[:], bank[7][:, 128:128 + E * FB], b1_t[:], ALU.add).then_inc(bias_step, 1)
                    dve.wait_ge(bias_copied, 1)
                    rows_split(b2_hl[:], b2_h[:], b2_l, b2_s, 5)

            walk(dve, step, NCH, RB)

            k = [0]

            def link(ins):
                k[0] += 1
                ins.then_inc(plan_step, 1)
                dve.wait_ge(plan_step, k[0])

            counts = bank[7][:, 0:NP]
            dve.wait_ge(counts_psum, 1)
            nc.vector.tensor_tensor(pad_at[:], pad_base[0:1, :], bank[7][0:1, 0:NP], ALU.add).then_inc(pads_ready, 1)
            tiles, upto, first, at_or_after, tmp, ones_np = (pl[:, q, :] for q in range(6))
            p_no, p_first, used, within = pc[:, 0:1], pc[:, 1:2], pc[:, 2:3], pc[:, 3:4]
            link(nc.vector.tensor_scalar(cnt_i[:, 0, :], counts, float(TS - 1), None, ALU.add))
            link(nc.vector.tensor_scalar(cnt_i[:, 1, :], cnt_i[:, 0, :], TS.bit_length() - 1, None, ALU.logical_shift_right))
            link(nc.vector.tensor_scalar(tiles, cnt_i[:, 1, :], 1.0, None, ALU.max))
            link(nc.vector.tensor_tensor_scan(upto, ones_np, tiles, 0.0, ALU.mult, ALU.add))
            link(nc.vector.tensor_tensor(first, upto, tiles, ALU.subtract))
            link(nc.vector.tensor_scalar(at_or_after, first, part_no[:, 0:1], None, ALU.is_le))
            nc.vector.tensor_reduce(p_no, at_or_after, AX.X, ALU.add)
            link(nc.vector.tensor_tensor(tmp, at_or_after, first, ALU.mult))
            link(nc.vector.tensor_reduce(p_first, tmp, AX.X, ALU.max))
            link(nc.vector.tensor_scalar(p_no, p_no, -1.0, None, ALU.add))
            link(nc.vector.tensor_scalar(at_or_after, pair_no[:], p_no, None, ALU.is_equal))
            nc.vector.tensor_tensor(tiles, at_or_after, lo_tab[:], ALU.mult)
            nc.vector.tensor_tensor(used, part_no[:], upto[:, NP - 1:NP], ALU.is_lt)
            nc.vector.tensor_tensor(within, part_no[:], p_first, ALU.subtract)
            link(nc.vector.tensor_tensor(tmp, at_or_after, hi_tab[:], ALU.mult))
            nc.vector.tensor_reduce(plan_f[:, 0:1], tiles, AX.X, ALU.add)
            nc.vector.tensor_reduce(plan_f[:, 1:2], tmp, AX.X, ALU.add)
            link(nc.vector.tensor_scalar(within, within, float(TS), float(-SPARE), ALU.mult, ALU.add))
            link(nc.vector.scalar_tensor_tensor(within, p_no, float(REGION), within, ALU.mult, ALU.add))
            link(nc.vector.tensor_tensor(within, within, used, ALU.mult))
            link(nc.vector.tensor_scalar(plan_f[:, 2:3], within, float(SPARE), None, ALU.add))
            assert k[0] == PLAN
            dve.wait_ge(plan_psum, 1)
            W = RB + 1
            nc.vector.tensor_copy(plan_e[:, 0, :], bank[6][0:1, 0:2 * W + 2])
            nc.vector.tensor_copy(plan_row[:], bank[6][0:1, 2 * P:3 * P]).then_inc(plan_step, 1)
            dve.wait_ge(plan_step, PLAN + 1)
            for q in range(2):
                src = bank[6][0:1, q * P:q * P + NG * RB]
                nc.vector.tensor_copy(plan_e[:, 1:NG + 1, q * W], src.rearrange("p (g k) -> p g k", k=RB)[:, :, RB - 1])
                ins = nc.vector.tensor_copy(plan_e[:, :, q * W + 1:(q + 1) * W],
                                            bank[6][0:1, q * P:q * P + (NG + 1) * RB].rearrange("p (g k) -> p g k", k=RB))
            nc.vector.tensor_copy(plan_e[:, :, 2 * W:2 * W + 2], bank[6][0:1, 0:2 * (NG + 1)].rearrange("p (g k) -> p g k", k=2))\
              .then_inc(plan_ready, 1)

            def cast_w2(first, last):
                for ex in range(first, last):
                    at = slice(ex * FB, (ex + 1) * FB)
                    dve.wait_ge(w2r_copied, ex + 1)
                    nc.vector.tensor_copy(w2_hi[:, at, :], w2_f[ex]).then_inc(w2_hi_done, 1)
                    dve.wait_ge(w2_hi_done, ex + 1)
                    nc.vector.tensor_tensor(w2_lo[:, at, :], w2_f[ex], w2_hi[:, at, :], ALU.subtract).then_inc(w2_ready, 1)

            EARLY = E // 2
            cast_w2(0, EARLY)

            def tile(j, half, par, quarter, slot):
                jj = known(j, 0)
                here = jj is None or jj < NS
                prev = jj is None or 1 <= jj <= NS

                def split(k):
                    if k == 0:
                        dve.wait_ge(h_ready[0], 2 * (j + 1))
                        after(dve, down_psum[0], j - 1)
                        nc.vector.tensor_copy(h_hi[0][par][:], h_f[0]).then_inc(hhi_done[0], 1)
                    dve.wait_ge(hhi_done[k], j + 1)
                    nc.vector.tensor_tensor(h_lo[k][par][:], h_f[k], h_hi[k][par][:], ALU.subtract)\
                      .then_inc(hlo_ready[k], 1)

                def low_x(j, par):
                    dve.wait_ge(xhi_ready, j + 1)
                    nc.vector.tensor_tensor(x_lo[par][:], bank[0][:, 0:TS], x_hi[par][:], ALU.subtract).then_inc(xlo_ready, 1)

                if jj == 0:
                    low_x(0, 0)
                    cast_w2(EARLY, E)
                row = srow[(slot - 1) % RB]
                if jj is None or jj >= 2:
                    dve.wait_ge(tg_ready, j - 1)
                    nc.vector.tensor_scalar(gate[:], tg[:], 0.5, 0.5, ALU.mult, ALU.add).then_inc(gate_done, 1)
                if jj is None or jj < NS - 1:
                    after(dve, up_psum[1], 2 * j)
                    low_x(j + 1, 1 - par)
                if jj is None or jj >= 2:
                    dve.wait_ge(gate_done, j - 1)
                    dve.wait_ge(diff_ready, j - 1)
                    after(dve, fin_ready, j - 2)
                    for h in range(HT):
                        ins = nc.vector.scalar_tensor_tensor(part[:, h, :], diff[:, h, :], gate[:, h:h + 1],
                                                             srow[(slot - 2) % RB][:, h, DENSE:DENSE + P],
                                                             ALU.mult, ALU.add)
                    ins.then_inc(part_done, 1)
                if here:
                    split(0)
                if prev:
                    dve.wait_ge(down_psum[1], j)
                    dve.wait_ge(ylo_done, j)
                    for h in range(HT):
                        ins = nc.vector.scalar_tensor_tensor(row[:, h, ROW:ROW + P], bank[6][:, h * P:(h + 1) * P],
                                                             row[:, h, W_HI:W_HI + 1], y_lo[:, h, :], ALU.mult, ALU.add)
                    ins.then_inc(nonabel_ready, 1)
                    dve.wait_ge(nonabel_ready, j)
                    for h in range(HT):
                        ins = nc.vector.tensor_tensor_reduce(prod[:, h, :], row[:, h, DENSE:DENSE + 2 * P], mix_b_all[:, 0:2 * P], 1.0, 0.0,
                                                             ALU.mult, ALU.add, dot[1 - par][:, h:h + 1])
                    ins.then_inc(dot_ready, 1)
                if here:
                    split(1)

            walk(dve, tile, NS, RB)


NAMES = ["L0_attn_x", "L0_attn_Wz", "L0_attn_bz", "L0_attn_Wh", "L0_attn_bh", "L0_ffn_ln_g", "L0_ffn_ln_b",
         "L0_ffn_abel_w", "L0_ffn_abel_b", "L0_ffn_gate_w_moe", "L0_ffn_gate_b_moe", "L0_ffn_w1", "L0_ffn_b1",
         "L0_ffn_w2", "L0_ffn_b2", "L0_ffn_gens", "L0_ffn_mix_w", "L0_ffn_mix_b"]


def kernel(**inputs):
    import numpy as np
    import concourse.bacc as bacc
    from concourse.bass_utils import run_bass_kernel_spmd

    nc = bacc.Bacc("TRN2", target_bir_lowering=False, num_devices=1)
    arrays, args = {}, []
    for name in NAMES:
        a = np.ascontiguousarray(inputs[name])
        arrays[f"in_{name}"] = a
        args.append(nc.dram_tensor(f"in_{name}", a.shape, mybir.dt.from_np(a.dtype), kind="ExternalInput").ap())
    shape = inputs["L0_attn_x"].shape
    args.append(nc.dram_tensor("result", shape, F32, kind="ExternalOutput").ap())
    gru_moe_block(nc, *args)
    r = run_bass_kernel_spmd(nc, [arrays], core_ids=[0])
    return r.results[0]["result"]
```
